# Optimizing a Trainium2 kernel written in Bass

```python
import numpy as np
import jax
import jax.numpy as jnp

def _softmax(x, axis=-1):
    return jax.nn.softmax(x, axis=axis)
def _gelu(x):
    return jax.nn.gelu(x, approximate=True)
def _silu(x):
    return jax.nn.silu(x)
def _sigmoid(x):
    return jax.nn.sigmoid(x)
def _layernorm(x, axis=-1, eps=1e-5):
    m = jnp.mean(x, axis=axis, keepdims=True)
    v = jnp.var(x, axis=axis, keepdims=True)
    return (x - m) / jnp.sqrt(v + eps)
def _scatter_add(tgt, idx, src, axis=0):
    return tgt.at[idx].add(src)
def _segment_sum(src, seg, n):
    return jax.ops.segment_sum(src, seg, n)

kernel_name = 'mk_conv_preact_d4_conv_nchw32_3f2219'

def setup_inputs(seed: int = 0):
    np.random.seed(seed)
    _w = jnp.asarray
    def _rec_inputs():
        import jax
        import jax.numpy as jnp
        _gk = jax.random.key(seed)
        x = -0.000125 + 0.9999 * jax.random.normal(jax.random.fold_in(_gk, 1), (16, 32, 256, 256), jnp.float32)
        return x
    x = _rec_inputs()
    def _L0_conv_setup():
        import jax, jax.numpy as jnp
        import numpy as np
        K_MAX = 16
        SCALE = 1.0 / (32 * 32)
        key = jax.random.key(seed)
        k1, k2, k3 = jax.random.split(key, 3)
        B, C_in, C_out, H, W = (16, 32, 32, 256, 256)
        x = jax.random.normal(k1, (B, C_in, H, W), dtype=jnp.float32)
        weights_real = SCALE * jax.random.normal(k2, (C_in, C_out, K_MAX, K_MAX), dtype=jnp.float32)
        weights_imag = SCALE * jax.random.normal(k3, (C_in, C_out, K_MAX, K_MAX), dtype=jnp.float32)
        return {'x': x, 'weights_real': weights_real, 'weights_imag': weights_imag}
    _L0_conv_all = _L0_conv_setup()
    _L0_conv_in = {k: v for k, v in _L0_conv_all.items() if k in ('weights_real', 'weights_imag', )}
    del _L0_conv_all

    def _L1_conv_setup():
        import jax, jax.numpy as jnp
        import numpy as np
        B, IN_CH, OUT_CH, R = (16, 32, 32, 32)
        M1, M2 = (32, 32)
        H, W = (256, 256)
        key = jax.random.key(seed)
        k1, k2, k3, k4 = jax.random.split(key, 4)
        x = jax.random.normal(k1, (B, IN_CH, H, W), jnp.float32)
        coeff_real = jax.random.normal(k2, (R, M1, M2, IN_CH), jnp.float32)
        coeff_imag = jax.random.normal(k3, (R, M1, M2, IN_CH), jnp.float32)
        proj = jax.random.normal(k4, (OUT_CH, R), jnp.float32)
        return {'x': x, 'coeff_real': coeff_real, 'coeff_imag': coeff_imag, 'proj': proj}
    _L1_conv_all = _L1_conv_setup()
    _L1_conv_in = {k: v for k, v in _L1_conv_all.items() if k in ('coeff_real', 'coeff_imag', 'proj', )}
    del _L1_conv_all

    def _L2_conv_setup():
        import jax, jax.numpy as jnp
        import numpy as np
        STRIDE = 1
        PADDING = 1
        key = jax.random.key(seed)
        k1, k2, k3 = jax.random.split(key, 3)
        x = jax.random.normal(k1, (8, 32, 512, 512), dtype=jnp.float32)
        W = jax.random.normal(k2, (32, 32, 3, 3), dtype=jnp.float32)
        b = jax.random.normal(k3, (32,), dtype=jnp.float32)
        return {'x': x, 'W': W, 'b': b}
    _L2_conv_all = _L2_conv_setup()
    _L2_conv_in = {k: v for k, v in _L2_conv_all.items() if k in ('W', 'b', )}
    del _L2_conv_all

    def _L3_conv_setup():
        import jax, jax.numpy as jnp
        import numpy as np
        key = jax.random.key(seed)
        k1, k2 = jax.random.split(key)
        x = jax.random.normal(k1, (8, 32, 252, 252), dtype=jnp.float32)
        weight = jax.random.normal(k2, (32, 32, 5, 5), dtype=jnp.float32)
        return {'x': x, 'weight': weight}
    _L3_conv_all = _L3_conv_setup()
    _L3_conv_in = {k: v for k, v in _L3_conv_all.items() if k in ('weight', )}
    del _L3_conv_all

    return {
        "x": x,
        "L0_conv_weights_real": _L0_conv_in["weights_real"],
        "L0_conv_weights_imag": _L0_conv_in["weights_imag"],
        "L1_conv_coeff_real": _L1_conv_in["coeff_real"],
        "L1_conv_coeff_imag": _L1_conv_in["coeff_imag"],
        "L1_conv_proj": _L1_conv_in["proj"],
        "L2_conv_W": _L2_conv_in["W"],
        "L2_conv_b": _L2_conv_in["b"],
        "L3_conv_weight": _L3_conv_in["weight"],
    }

def reference(x, L0_conv_weights_real, L0_conv_weights_imag, L1_conv_coeff_real, L1_conv_coeff_imag, L1_conv_proj, L2_conv_W, L2_conv_b, L3_conv_weight):
    import jax
    import jax.numpy as jnp
    def _L0_conv_ref(x, weights_real, weights_imag):
        import jax, jax.numpy as jnp
        import numpy as np
        K_MAX = 16
        SCALE = 1.0 / (32 * 32)
        B, C, H, W = x.shape
        C_out = weights_real.shape[1]
        k = min(K_MAX, H, W // 2 + 1)
        x_ft = jnp.fft.rfft2(x, norm='ortho')
        w = (weights_real + 1j * weights_imag)[:, :, :k, :k]
        S = jnp.sum(x_ft[:, :, :k, :k], axis=2)
        blk = jnp.einsum('bir,iorc->borc', S, w)
        out_ft = jnp.zeros((B, C_out, H, W // 2 + 1), dtype=x_ft.dtype)
        out_ft = out_ft.at[:, :, :k, :k].set(blk)
        return jnp.fft.irfft2(out_ft, s=(H, W), norm='ortho')

    def _L1_conv_ref(x, coeff_real, coeff_imag, proj):
        import jax, jax.numpy as jnp
        import numpy as np
        B, IN_CH, OUT_CH, R = (16, 32, 32, 32)
        M1, M2 = (32, 32)
        H, W = (256, 256)
        x_ft = jnp.fft.rfftn(x, axes=(-2, -1))
        coeff = (coeff_real + 1j * coeff_imag).astype(jnp.complex64)
        Wt = jnp.einsum('or,rabi->oabi', proj.astype(jnp.complex64), coeff)
        Hf, Wf = (x_ft.shape[-2], x_ft.shape[-1])
        m1 = min(M1, Hf)
        m2 = min(M2, Wf)
        sub = jnp.einsum('bcij,ocij->boij', x_ft[..., :m1, :m2], Wt[:, :, :m1, :m2])
        out_ft = jnp.zeros((x.shape[0], OUT_CH, Hf, Wf), jnp.complex64)
        out_ft = out_ft.at[..., :m1, :m2].set(sub.astype(jnp.complex64))
        return jnp.fft.irfftn(out_ft, s=(x.shape[-2], x.shape[-1]), axes=(-2, -1))

    def _L2_conv_ref(x, W, b):
        import jax, jax.numpy as jnp
        import numpy as np
        STRIDE = 1
        PADDING = 1
        out = jax.lax.conv_general_dilated(x, W, window_strides=(STRIDE, STRIDE), padding=((PADDING, PADDING), (PADDING, PADDING)), dimension_numbers=('NCHW', 'OIHW', 'NCHW'))
        out = out + b[None, :, None, None]
        return out

    def _L3_conv_ref(x, weight):
        import jax, jax.numpy as jnp
        import numpy as np
        k = weight.shape[-1]
        p = k // 2
        xp = jnp.pad(x, ((0, 0), (0, 0), (p, p), (p, p)), mode='reflect')
        H, W = (xp.shape[-2], xp.shape[-1])
        wp = jnp.zeros((weight.shape[0], weight.shape[1], H, W), dtype=x.dtype)
        wp = wp.at[:, :, :k, :k].set(weight)
        shift = -k // 2
        wp = jnp.roll(wp, shift=(shift, shift), axis=(-2, -1))
        x_fft = jnp.fft.fft2(xp)
        w_fft = jnp.fft.fft2(wp)
        out_fft = jnp.einsum('bihw,oihw->bohw', x_fft, w_fft)
        out = jnp.fft.ifft2(out_fft).real
        return out[:, :, p:-p, p:-p]

    def _gn(v, G=16, eps=1e-5):
        B_, C_, H_, W_ = v.shape
        g = v.reshape(B_, G, C_ // G, H_, W_)
        m = jnp.mean(g, axis=(2, 3, 4), keepdims=True)
        s = jnp.var(g, axis=(2, 3, 4), keepdims=True)
        return ((g - m) / jnp.sqrt(s + eps)).reshape(v.shape)

    def _ln_c(v, eps=1e-6):
        m = jnp.mean(v, axis=1, keepdims=True)
        s = jnp.var(v, axis=1, keepdims=True)
        return (v - m) / jnp.sqrt(s + eps)

    def _ln_t(v, eps=1e-5):
        m = jnp.mean(v, axis=-1, keepdims=True)
        s = jnp.var(v, axis=-1, keepdims=True)
        return (v - m) / jnp.sqrt(s + eps)

    def _to_tokens(v):
        B_, C_, H_, W_ = v.shape
        return v.reshape(B_, C_, H_ * W_).transpose(0, 2, 1)
    def _from_tokens(t, like):
        B_, C_, H_, W_ = like.shape
        return t.transpose(0, 2, 1).reshape(B_, C_, H_, W_)

    x = x + _L0_conv_ref(_gn(x), L0_conv_weights_real, L0_conv_weights_imag)
    x = x + _L1_conv_ref(_gn(x), L1_conv_coeff_real, L1_conv_coeff_imag, L1_conv_proj)
    x = x + _L2_conv_ref(_gn(x), L2_conv_W, L2_conv_b)
    x = x + _L3_conv_ref(_gn(x), L3_conv_weight)
    return x


_drawn_inputs = setup_inputs


def setup_inputs(seed=0):
    import zlib

    import numpy as np

    out = dict(_drawn_inputs(seed))
    spreads = {}
    factors = {'L0_conv_weights_real': 5.36, 'L0_conv_weights_imag': 5.358}
    for name, (base, spread) in spreads.items():
        noise = np.random.default_rng([zlib.crc32(name.encode()), seed]).standard_normal(out[name].shape)
        drawn = base * np.exp(spread * noise) if base else spread * noise
        out[name] = jnp.asarray(drawn.astype(out[name].dtype))
    for name, factor in factors.items():
        out[name] = (out[name] * factor).astype(out[name].dtype)
    return out
```

```python
from contextlib import ExitStack

import numpy as np
import concourse.bass as bass
from concourse import mybir

F32 = mybir.dt.float32
F16 = mybir.dt.float16
ALU = mybir.AluOpType
ACT = mybir.ActivationFunctionType
AX = mybir.AxisListType

P = 128
C, H, W = 32, 256, 256
HW = H * W
GROUP = 2
NG = C // GROUP
M0, M1 = 16, 32
R = P // C
NKH = M1 // R
EPS = 1e-5
N_GROUP = GROUP * HW

CH = 8
NCH = C // CH

BLOCKS = H // R + 1
STEPS = H // R // 2
PER = 8
W2 = W + 2
W3 = W + 4
SHIFT = 2
TAPS3, TAPS5 = 3, 5
CENTRE3, CENTRE5 = 1, 3


def constants(batch):
    f64 = np.float64
    a = 2 * np.pi * np.outer(np.arange(H), np.arange(M1)).astype(f64) / H
    cs, sn = np.cos(a), np.sin(a)
    halves = lambda t: np.ascontiguousarray(t.reshape(2, P, 2 * M1).transpose(1, 0, 2).astype(np.float32))
    dft_real = halves(np.concatenate([cs, -sn], 1))
    dft_imag = halves(np.concatenate([sn, cs], 1))
    wave = np.concatenate([cs, -sn], 1).T
    rows = (wave * 2 / HW).astype(np.float32)
    hi = wave.astype(np.float16)
    lo = (wave - hi.astype(f64)).astype(np.float16)
    cols = np.stack([np.concatenate([hi, hi]), np.concatenate([lo, lo])], 1)
    p = np.arange(P)
    ch, q = p % C, p // C
    same_group = (ch[:, None] // GROUP == ch[None, :] // GROUP).astype(np.float32)
    own_group = (ch[:, None] // GROUP == np.arange(NG)[None, :]).astype(np.float32)
    pick = np.zeros((P, 2, 2 * C), np.float32)
    pick[p, 0, ch] = 1
    pick[p, 1, C + ch] = 1
    column0 = np.full((P, NKH, 2), 0.5, np.float32)
    column0[q == 0, 0, 0] = 1
    column0[q == 0, 0, 1] = 0
    centre = np.zeros((P, 2, P), np.float32)
    for block in range(2):
        for rin in range(R):
            rout = R * block + rin - 1
            if 0 <= rout < R:
                centre[rin * C + np.arange(C), block, rout * C + np.arange(C)] = 1
    return {"dft_real": dft_real, "dft_imag": dft_imag, "rows": rows, "cols": cols, "same_group": same_group,
            "own_group": own_group, "pick": pick, "column0": column0, "centre": centre}


def four_convolutions(nc, B, x, w0r, w0i, coeff_r, coeff_i, proj_t, w3_t, bias3, w5_t,
                      dft_real, dft_imag, rows, cols, same_group, own_group, pick, column0, centre, y):
    spectrum = nc.dram_tensor("spectrum_dram", (B, 2, M1, C, 2, M1), F32, kind="Internal").ap()

    keep = ExitStack()
    with keep:
        def sb(name, shape, dt=F32, at=keep):
            return at.enter_context(nc.sbuf_tensor(name, shape, dt))

        def sem(name, at=keep):
            return at.enter_context(nc.semaphore(name))

        bank = [keep.enter_context(nc.psum_tensor(f"bank{n}", [P, 512], F32)) for n in range(8)]
        std2 = sb("std2", [P, B])
        rstd2 = sb("rstd2", [P, B])
        bias2 = sb("bias2", [P, B])
        group_sum = sb("group_sum", [P, P])
        centre_sb = sb("centre_sb", [P, 2, P])
        w3 = sb("w3", [P, 2, 2, TAPS3, P], F16)
        w5 = sb("w5", [P, 2, 2, TAPS5, P], F16)
        w3_centre = sb("w3_centre", [P, 2, P])
        w5_centre = sb("w5_centre", [P, 2, P])
        w5_sum = sb("w5_sum", [P, P])
        eps = sb("eps", [P, 1])

        early = ExitStack()
        spec = sb("spec", [P, B, NKH, 2, M1], at=early)
        records = sb("records", [P, B, 2 * NG * 2, 3], at=early)
        analysis(nc, B, x, dft_real, dft_imag, spec, records, bank)
        mixing(nc, B, w0r, w0i, coeff_r, coeff_i, proj_t, w3_t, bias3, w5_t, same_group, own_group, pick, column0,
               centre, spectrum, spec, records, bank, std2, rstd2, bias2, group_sum, centre_sb, w3, w5, w3_centre,
               w5_centre, w5_sum, eps)
        early.close()
        spatial(nc, B, x, rows, cols, spectrum, y, bank, std2, rstd2, bias2, group_sum, centre_sb, w3, w5, w3_centre,
                w5_centre, w5_sum, eps)


def analysis(nc, B, x, dft_real, dft_imag, spec, records, bank):
    own = ExitStack()
    with own:
        def sb(name, shape, dt=F32):
            return own.enter_context(nc.sbuf_tensor(name, shape, dt))

        def sem(name):
            return own.enter_context(nc.semaphore(name))

        tile = [sb(f"x_chunk{k}", [P, 2, CH, W]) for k in range(NCH)]
        half_dft = sb("half_dft", [P, 2, 2, M1, C])
        t_real = sb("t_real", [P, 2, 2 * M1])
        t_imag = sb("t_imag", [P, 2, 2 * M1])

        tables_loaded = sem("tables_loaded")
        chunk_loaded = [sem(f"chunk_loaded{k}") for k in range(NCH)]
        rows_done = sem("rows_done")
        stats_done = sem("stats_done")
        rows_copied = sem("rows_copied")
        cols_done = sem("cols_done")
        cols_copied = sem("cols_copied")

        block = own.enter_context(nc.Block())

        @block.sync
        def _(sp):
            sp.dma_start(t_real[:], dft_real).then_inc(tables_loaded, 16)
            sp.dma_start(t_imag[:], dft_imag).then_inc(tables_loaded, 16)
            with sp.Fori(0, B) as b:
                for k in range(NCH):
                    sp.wait_ge(rows_done, b * NCH + (k + 1))
                    sp.wait_ge(stats_done, b * NCH + (k + 1))
                    for h in range(2):
                        src = x[b, CH * k:CH * (k + 1), P * h:P * (h + 1), :].rearrange("c y x -> y c x")
                        sp.dma_start(tile[k][:, h], src).then_inc(chunk_loaded[k], 16)

        @block.tensor
        def _(pe):
            pe.sem_inc(rows_done, NCH)
            pe.sem_inc(cols_done, 1)
            pe.wait_ge(tables_loaded, 32)
            with pe.Fori(0, B) as b:
                for k in range(NCH):
                    pe.wait_ge(chunk_loaded[k], b * 32 + 32)
                    pe.wait_ge(rows_copied, b * NCH + (k + 1))
                    for c in range(CH):
                        for xh in range(2):
                            out = bank[2 * (k % 2) + xh][:, 2 * M1 * c:2 * M1 * (c + 1)]
                            for yh in range(2):
                                last = nc.tensor.matmul(out, tile[k][:, yh, c, P * xh:P * (xh + 1)], t_real[:, yh, :],
                                                        start=(yh == 0), stop=(yh == 1))
                    last.then_inc(rows_done, 1)
                pe.wait_ge(rows_copied, b * NCH + (2 + NCH))
                pe.wait_ge(cols_copied, b + 1)
                for g in range(NKH):
                    out = bank[4][:, 2 * M1 * g:2 * M1 * (g + 1)]
                    for n, (xh, part) in enumerate([(0, 0), (0, 1), (1, 0), (1, 1)]):
                        last = nc.tensor.matmul(out, half_dft[:, xh, part, R * g:R * (g + 1), :],
                                                (t_real, t_imag)[part][:, xh, :], start=(n == 0), stop=(n == 3))
                last.then_inc(cols_done, 1)

        @block.scalar
        def _(act):
            act.sem_inc(rows_copied, 2)
            act.sem_inc(cols_copied, 1)
            with act.Fori(0, B) as b:
                act.wait_ge(cols_done, b + 1)
                for k in range(NCH):
                    act.wait_ge(rows_done, b * NCH + (NCH + k + 1))
                    for xh in range(2):
                        last = nc.scalar.activation(
                            half_dft[:, xh, :, :, CH * k:CH * (k + 1)].rearrange("p r f c -> p c (r f)"),
                            bank[2 * (k % 2) + xh][:, :].rearrange("p (c f) -> p c f", c=CH), ACT.Copy)
                    last.then_inc(rows_copied, 1)
                act.wait_ge(cols_done, b + 2)
                nc.scalar.activation(spec[:, b, :, :, :].rearrange("p g r f -> p (g r f)"), bank[4][:, :],
                                     ACT.Copy).then_inc(cols_copied, 1)

        @block.vector
        def _(dve):
            dve.sem_inc(stats_done, NCH)
            with dve.Fori(0, B) as b:
                for k in range(NCH):
                    dve.wait_ge(chunk_loaded[k], b * 32 + 32)
                    for g in range(CH // GROUP):
                        for h in range(2):
                            n = 2 * (h * NG + k * CH // GROUP + g)
                            last = nc.vector.bn_stats(
                                records[:, b, n:n + 2, :].rearrange("p n t -> p (n t)"),
                                tile[k][:, h, GROUP * g:GROUP * (g + 1), :].rearrange("p c x -> p (c x)"))
                    last.then_inc(stats_done, 1)


def mixing(nc, B, w0r, w0i, coeff_r, coeff_i, proj_t, w3_t, bias3, w5_t, same_group, own_group, pick, column0,
           centre, spectrum, spec, records, bank, std2, rstd2, bias2, group_sum, centre_sb, w3, w5, w3_centre,
           w5_centre, w5_sum, eps):
    own = ExitStack()
    with own:
        def sb(name, shape, dt=F32):
            return own.enter_context(nc.sbuf_tensor(name, shape, dt))

        def sem(name):
            return own.enter_context(nc.semaphore(name))

        HF = M1 // 2
        HALVES = 2 * NKH
        delta = sb("delta", [P, B, NKH, 2, M1])
        coeff_in = sb("coeff_in", [2 * C, C, R, M1])
        coeff = sb("coeff", [2 * C, M1, R, C])
        diagonals = sb("diagonals", [P, 2, 2, HF, P])
        diagonal = [diagonals[:, n] for n in range(2)]
        w0 = diagonals[0:2 * C].rearrange("p n s f m -> p (n s f m)").rearrange("p (o f c) -> p o f c", o=C, f=M0)
        scaled = [sb(f"scaled{n}", [P, 2, B, 2, M1]) for n in range(2)]
        mixed = [sb(f"mixed{n}", [P, B, 2, HF]) for n in range(2)]
        low = scaled[0]
        low_s = sb("low_s", [2 * C, M0, 2, B])
        proj = sb("proj", [2 * C, C])
        pick_sb = sb("pick_sb", [P, 2, 2 * C])
        own_group_sb = sb("own_group_sb", [P, NG])
        column0_sb = sb("column0_sb", [P, 2 * NKH])
        ones = sb("ones", [P, P])
        moment2 = sb("moment2", [P, B, 4 * NG])
        masked = sb("masked", [P, 2 * B, NG])
        moments = sb("moments", [P, 2 * B])
        energy = sb("energy", [P, 3, B])
        ends = sb("ends", [P, 2, B])
        mean, var, std, rstd, total, tmp, dc0, dc1, dc1c = (sb(n, [P, B]) for n in (
            "mean", "var", "std", "rstd", "total", "tmp", "dc0", "dc1", "dc1c"))
        junk = sb("junk", [P, NKH * 2 * M1])
        t3 = sb("t3", [P, 2, TAPS3, P])
        t5 = sb("t5", [P, 2, TAPS5, P])
        bias_sb = sb("bias_sb", [P, 1])
        DC = slice(0, C)

        tables_loaded = sem("mix_tables_loaded")
        toeplitz_cleared = sem("toeplitz_cleared")
        toeplitz_loaded = sem("toeplitz_loaded")
        toeplitz_split = sem("toeplitz_split")
        cleared = sem("cleared")
        coeff_loaded = sem("coeff_loaded")
        coeff_turned = sem("coeff_turned")
        dve_step = sem("mix_dve_step")
        squares_ready = sem("squares_ready")
        moments_summed = sem("moments_summed")
        variance_ready = sem("variance_ready")
        root_ready = sem("root_ready")
        centred = sem("centred")
        energy_ready = sem("energy_ready")
        low_ready = sem("low_ready")
        low_summed = sem("low_summed")
        low_copied = sem("low_copied")
        layer0_done = sem("layer0_done")
        ends_ready = sem("ends_ready")
        ends_summed = sem("ends_summed")
        scaled_ready = sem("scaled_ready")
        combined = sem("combined")
        diagonal_real = sem("diagonal_real")
        diagonal_imag = sem("diagonal_imag")
        product_done = sem("product_done")
        mixed_ready = sem("mixed_ready")
        mixed_added = sem("mixed_added")
        delta_ready = sem("delta_ready")
        turned_real = sem("turned_real")
        turned_imag = sem("turned_imag")
        written = sem("spectrum_written")

        def taps(n):
            for blk in range(2):
                for rin in range(R):
                    for rout in range(R):
                        d = R * blk + rin - rout
                        if 0 <= d < n:
                            yield rin, blk, rout, d if n == TAPS3 else n - 1 - d

        N_TAPS = sum(1 for t in (TAPS3, TAPS5) for _ in taps(t))
        N_TABLES = 9 + R

        block = own.enter_context(nc.Block())

        @block.sync
        def _(sp):
            for dst, src in ((group_sum[:], same_group), (pick_sb[:], pick), (own_group_sb[:], own_group),
                             (column0_sb[:], column0.rearrange("p g r -> p (g r)")), (centre_sb[:], centre)):
                sp.dma_start(dst, src).then_inc(tables_loaded, 16)
            for part in range(2):
                sp.dma_start(proj[C * part:C * (part + 1), :], proj_t).then_inc(tables_loaded, 16)
                sp.dma_start(w0[C * part:C * (part + 1)], (w0r, w0i)[part]).then_inc(tables_loaded, 16)
            for r in range(R):
                sp.dma_start(bias_sb[C * r:C * (r + 1), :], bias3).then_inc(tables_loaded, 16)
            sp.wait_ge(toeplitz_cleared, 2)
            for dst, src, n in ((t3, w3_t, TAPS3), (t5, w5_t, TAPS5)):
                for rin, blk, rout, tap in taps(n):
                    sp.dma_start(dst[C * rin:C * (rin + 1), blk, :, C * rout:C * (rout + 1)],
                                 src[:, tap, :, :]).then_inc(toeplitz_loaded, 16)
            for g in range(NKH):
                if g >= 1:
                    sp.wait_ge(coeff_turned, g)
                for part in range(2):
                    sp.dma_start(coeff_in[C * part:C * (part + 1)],
                                 (coeff_r, coeff_i)[part][:, :, R * g:R * (g + 1), :]).then_inc(coeff_loaded, 16)
            sp.wait_ge(delta_ready, 1)
            for part, src in enumerate((delta, spec)):
                if part:
                    sp.wait_ge(turned_real, 1)
                    sp.wait_ge(turned_imag, 1)
                for b in range(B):
                    sp.dma_start(spectrum[b, part].rearrange("(g q) c r f -> (q c) g (r f)", q=R),
                                 src[:, b].rearrange("p g r f -> p g (r f)")).then_inc(written, 16)
            sp.wait_ge(written, 16 * 2 * B)

        @block.tensor
        def _(pe):
            pe.wait_ge(tables_loaded, 16 * N_TABLES)
            pe.wait_ge(cleared, 1)
            pe.wait_ge(squares_ready, 1)
            means = records[:, :, :, 1].rearrange("p b (h g e) -> p h e b g", h=2, g=NG)
            squares = moment2[:].rearrange("p b (h g e) -> p h e b g", h=2, g=NG)
            for kind, src in enumerate((means, squares)):
                for n, (h, e) in enumerate([(0, 0), (0, 1), (1, 0), (1, 1)]):
                    last = nc.tensor.matmul(bank[0][:, B * NG * kind:B * NG * (kind + 1)], ones[:], src[:, h, e],
                                            start=(n == 0), stop=(n == 3))
            last.then_inc(moments_summed, 1)
            pe.wait_ge(low_ready, 1)
            for part in range(2):
                last = nc.tensor.matmul(bank[1][0:2 * C, 0:M0 * 2 * B], pick_sb[:, part, :],
                                        low[:, part, :, :, 0:M0].rearrange("p b r f -> p f r b"),
                                        start=(part == 0), stop=(part == 1))
            last.then_inc(low_summed, 1)
            pe.wait_ge(low_copied, 1)
            for f in range(M0):
                q = f % R
                for c in range(M0):
                    last = nc.tensor.matmul(bank[4 + f // R][C * q:C * (q + 1), 2 * B * c:2 * B * (c + 1)],
                                            w0[:, :, f, c], low_s[:, f, :, :].rearrange("p r b -> p (r b)"),
                                            start=True, stop=True)
            last.then_inc(layer0_done, 1)
            pe.wait_ge(ends_ready, 1)
            nc.tensor.matmul(bank[0][:, 0:2 * B], group_sum[:], ends[:].rearrange("p k b -> p (k b)"),
                             start=True, stop=True).then_inc(ends_summed, 1)

            def combine(n):
                g, half = n // 2, n % 2
                pe.wait_ge(coeff_turned, g + 1)
                if n >= 2:
                    pe.wait_ge(diagonal_real, n - 1)
                    pe.wait_ge(diagonal_imag, n - 1)
                for f in range(HF):
                    for part in range(2):
                        rank = slice(C * part, C * (part + 1))
                        last = nc.tensor.matmul(bank[4 + 2 * (n % 2) + part][:, C * f:C * (f + 1)],
                                                coeff[rank, HF * half + f].rearrange("p q c -> p (q c)"), proj[rank, :],
                                                start=True, stop=True)
                last.then_inc(combined, 1)

            pe.wait_ge(scaled_ready, 1)
            combine(0)
            for n in range(HALVES):
                if n + 1 < HALVES:
                    combine(n + 1)
                pe.wait_ge(diagonal_real, n + 1)
                pe.wait_ge(diagonal_imag, n + 1)
                pe.wait_ge(scaled_ready, n // 2 + 1)
                if n >= 2:
                    pe.wait_ge(mixed_ready, n - 1)
                for f in range(HF):
                    for part in range(2):
                        rhs = scaled[n // 2 % 2][:, part, :, :, HF * (n % 2) + f].rearrange("p b r -> p r b")
                        last = nc.tensor.matmul(bank[2 + n % 2][:, 2 * B * f:2 * B * (f + 1)],
                                                diagonal[n % 2][:, part, f, :], rhs, start=(part == 0),
                                                stop=(part == 1))
                last.then_inc(product_done, 1)
            pe.wait_ge(ends_ready, 2)
            nc.tensor.matmul(bank[0][:, 0:2 * B], group_sum[:], ends[:].rearrange("p k b -> p (k b)"),
                             start=True, stop=True).then_inc(ends_summed, 1)

        @block.gpsimd
        def _(pool):
            nc.gpsimd.memset(t3[:], 0.0).then_inc(toeplitz_cleared, 1)
            nc.gpsimd.memset(t5[:], 0.0).then_inc(toeplitz_cleared, 1)
            nc.gpsimd.memset(ones[:], 1.0 / (4 * P)).then_inc(cleared, 1)

            def turn(g):
                pool.wait_ge(coeff_loaded, 32 * (g + 1))
                if g >= 1:
                    pool.wait_ge(combined, 2 * g)
                nc.gpsimd.tensor_copy(coeff[:].rearrange("p f q c -> p c q f"), coeff_in[:]).then_inc(coeff_turned, 1)

            turn(0)
            pool.wait_ge(layer0_done, 1)
            for n in range(2):
                nc.gpsimd.memset(diagonal[n], 0.0).then_inc(cleared, 1)
            pool.wait_ge(toeplitz_loaded, 16 * N_TAPS)
            pool.wait_ge(tables_loaded, 16 * N_TABLES)
            for t, w, c, n in ((t3, w3, w3_centre, CENTRE3), (t5, w5, w5_centre, CENTRE5)):
                nc.gpsimd.tensor_copy(w[:, 0], t[:]).then_inc(toeplitz_split, 1)
                nc.gpsimd.tensor_copy(c[:], t[:, :, n, :]).then_inc(toeplitz_split, 1)
            pool.wait_ge(toeplitz_split, 4)
            for t, w in ((t3, w3), (t5, w5)):
                nc.gpsimd.tensor_tensor(w[:, 1], t[:], w[:, 0], ALU.subtract).then_inc(toeplitz_split, 1)
            for n in range(HALVES):
                if n % 2 == 0 and n // 2 + 1 < NKH:
                    turn(n // 2 + 1)
                pool.wait_ge(mixed_ready, n + 1)
                for dst in (spec, delta):
                    part = dst[:, :, n // 2, :, HF * (n % 2):HF * (n % 2 + 1)]
                    nc.gpsimd.tensor_tensor(part, part, mixed[n % 2][:], ALU.add).then_inc(mixed_added, 1)

        @block.scalar
        def _(act):
            def energies(k):
                act.wait_ge(centred, k + 1)
                for b in range(B):
                    if B * k + b:
                        act.wait_ge(energy_ready, B * k + b)
                    nc.scalar.activation(junk[:], spec[:, b].rearrange("p g r f -> p (g r f)"), ACT.Square,
                                         accum_out=energy[:, k, b:b + 1]).then_inc(energy_ready, 1)

            def root(k, out):
                act.wait_ge(variance_ready, k + 1)
                nc.scalar.activation(out[:], var[:], ACT.Sqrt, bias=eps[:]).then_inc(root_ready, 1)

            root(0, std)
            energies(0)
            act.wait_ge(low_summed, 1)
            nc.scalar.activation(low_s[:].rearrange("p f r b -> p (f r b)"), bank[1][0:2 * C, 0:M0 * 2 * B],
                                 ACT.Copy).then_inc(low_copied, 1)
            energies(1)
            root(1, std)
            act.wait_ge(cleared, 3)
            for n in range(HALVES):
                act.wait_ge(combined, n + 1)
                if n >= 2:
                    act.wait_ge(product_done, n - 1)
                for q in range(R):
                    rows_q = slice(C * q, C * (q + 1))
                    last = nc.scalar.activation(diagonal[n % 2][rows_q, 0, :, rows_q],
                                                bank[4 + 2 * (n % 2)][rows_q, :].rearrange("p (f o) -> p f o", o=C),
                                                ACT.Copy)
                last.then_inc(diagonal_real, 1)
            energies(2)
            root(2, std2)
            act.wait_ge(delta_ready, 1)
            nc.scalar.activation(spec[:, :, :, 1, :].rearrange("p b g f -> p (b g) f"),
                                 delta[:, :, :, 0, :].rearrange("p b g f -> p (b g) f"), ACT.Copy,
                                 scale=-1.0).then_inc(turned_imag, 1)

        @block.vector
        def _(dve):
            chain = [0]

            def link(ins):
                chain[0] += 1
                ins.then_inc(dve_step, 1)
                dve.wait_ge(dve_step, chain[0])

            def put(out, a, b, op):
                link(nc.vector.tensor_tensor(out, a, b, op))

            def scale(out, a, k, op=ALU.mult):
                link(nc.vector.tensor_scalar(out, a, k, None, op))

            def axpy(out, a, k, b):
                link(nc.vector.scalar_tensor_tensor(out, a, k, b, ALU.mult, ALU.add))

            def over_images(t, n):
                return t[:, :, None].to_broadcast([P, B, n])

            spec_dc = spec[DC, :, 0, 0, 0]
            link(nc.vector.memset(delta[:], 0.0))
            link(nc.vector.memset(eps[:], EPS))
            link(nc.vector.memset(ends[:], 0.0))
            rec_mean, rec_var = records[:, :, :, 1], records[:, :, :, 2]
            put(moment2[:], rec_mean, rec_mean, ALU.mult)
            axpy(moment2[:], rec_var, 1.0 / W, moment2[:])
            dve.sem_inc(squares_ready, 1)
            dve.wait_ge(moments_summed, 1)
            dve.wait_ge(tables_loaded, 16 * N_TABLES)
            put(masked[:], bank[0][:, 0:2 * B * NG].rearrange("p (k g) -> p k g", g=NG),
                own_group_sb[:, None, :].to_broadcast([P, 2 * B, NG]), ALU.mult)
            link(nc.vector.tensor_reduce(moments[:], masked[:], AX.X, ALU.add))
            m0, q0 = moments[:, 0:B], moments[:, B:2 * B]
            put(tmp[:], m0, m0, ALU.mult)
            put(var[:], q0, tmp[:], ALU.subtract)
            dve.sem_inc(variance_ready, 1)
            axpy(spec_dc, m0[DC], -float(HW), spec_dc)
            dve.sem_inc(centred, 1)
            link(nc.vector.tensor_copy(dc0[DC], spec_dc))
            link(nc.vector.tensor_copy(total[:], m0))
            dve.wait_ge(root_ready, 1)
            link(nc.vector.reciprocal(rstd[:], std[:]))
            g_low = [spec[:, :, g, :, 0:M0] for g in range(M0 // R)]
            low0, low1 = low[:, 0, :, :, 0:M0], low[:, 1, :, :, 0:M0]
            put(low0, g_low[0], g_low[1], ALU.add)
            for g in g_low[2:]:
                put(low0, low0, g, ALU.add)
            for r in range(2):
                put(low0[:, :, r, :], low0[:, :, r, :], over_images(rstd, M0), ALU.mult)
            scale(low1[:, :, 0, :], low0[:, :, 1, :], -1.0)
            link(nc.vector.tensor_copy(low1[:, :, 1, :], low0[:, :, 0, :]))
            dve.sem_inc(low_ready, 1)
            dve.wait_ge(layer0_done, 1)
            dve.wait_ge(energy_ready, B)
            for g in range(M0 // R):
                link(nc.vector.tensor_copy(delta[:, :, g, :, 0:M0].rearrange("p b r f -> p f r b"),
                                           bank[4 + g][:, 0:M0 * 2 * B].rearrange("p (f r b) -> p f r b", f=M0, r=2)))
            n_low = 2 * M0 // R
            column = delta[:].rearrange("p b g r f -> p b (g r) f")[:, :, 0:n_low, 0]
            put(column, column, column0_sb[:, None, 0:n_low].to_broadcast([P, B, n_low]), ALU.mult)
            for g in range(M0 // R):
                put(g_low[g], g_low[g], delta[:, :, g, :, 0:M0], ALU.add)
            dve.sem_inc(centred, 1)
            link(nc.vector.tensor_copy(dc1[DC], spec_dc))

            def change(k, dc_old2, dc_old, dc_new):
                dve.wait_ge(energy_ready, B * (k + 1))
                put(tmp[:], energy[:, k], energy[:, k - 1], ALU.subtract)
                scale(ends[:, 0], tmp[:], 2.0)
                for dc, factor in ((dc_old2, 2.0), (dc_old, -1.0), (dc_new, -1.0)):
                    put(tmp[DC], dc, dc, ALU.mult)
                    axpy(ends[DC, 0], tmp[DC], factor, ends[DC, 0])
                link(nc.vector.tensor_copy(ends[DC, 1], dc_new))
                dve.sem_inc(ends_ready, 1)
                dve.wait_ge(ends_summed, k)
                scale(mean[:], bank[0][:, B:2 * B], 1.0 / N_GROUP)
                axpy(var[:], bank[0][:, 0:B], 1.0 / HW / N_GROUP, var[:])
                put(tmp[:], mean[:], mean[:], ALU.mult)
                put(var[:], var[:], tmp[:], ALU.subtract)
                dve.sem_inc(variance_ready, 1)
                put(total[:], total[:], mean[:], ALU.add)

            change(1, dc0[DC], dc0[DC], dc1[DC])
            axpy(spec_dc, mean[DC], -float(HW), spec_dc)
            link(nc.vector.tensor_copy(dc1c[DC], spec_dc))
            dve.wait_ge(root_ready, 2)
            link(nc.vector.reciprocal(rstd[:], std[:]))

            def normalise(g):
                if g >= 2:
                    dve.wait_ge(product_done, 2 * (g - 1))
                s = scaled[g % 2]
                put(s[:, 0].rearrange("p b r f -> p b (r f)"), spec[:, :, g].rearrange("p b r f -> p b (r f)"),
                    over_images(rstd, 2 * M1), ALU.mult)
                scale(s[:, 1, :, 0, :], s[:, 0, :, 1, :], -1.0)
                link(nc.vector.tensor_copy(s[:, 1, :, 1, :], s[:, 0, :, 0, :]))
                dve.sem_inc(scaled_ready, 1)

            def lay_out(n):
                dve.wait_ge(combined, n + 1)
                if n >= 2:
                    dve.wait_ge(product_done, n - 1)
                for q in range(R):
                    rows_q = slice(C * q, C * (q + 1))
                    last = nc.vector.tensor_copy(diagonal[n % 2][rows_q, 1, :, rows_q],
                                                 bank[5 + 2 * (n % 2)][rows_q, :].rearrange("p (f o) -> p f o", o=C))
                last.then_inc(diagonal_imag, 1)

            normalise(0)
            dve.wait_ge(cleared, 3)
            lay_out(0)
            for n in range(HALVES):
                if n % 2 == 0 and n // 2 + 1 < NKH:
                    normalise(n // 2 + 1)
                if n + 1 < HALVES:
                    lay_out(n + 1)
                dve.wait_ge(product_done, n + 1)
                if n >= 2:
                    dve.wait_ge(mixed_added, 2 * (n - 1))
                link(nc.vector.tensor_copy(mixed[n % 2][:].rearrange("p b r f -> p f r b"),
                                           bank[2 + n % 2][:, 0:HF * 2 * B].rearrange("p (f r b) -> p f r b", f=HF, r=2)))
                if n % 2 == 0:
                    column = mixed[n % 2][:, :, :, 0]
                    put(column, column, column0_sb[:, None, n:n + 2].to_broadcast([P, B, 2]), ALU.mult)
                dve.sem_inc(mixed_ready, 1)
            dve.wait_ge(mixed_added, 2 * HALVES)
            dve.sem_inc(centred, 1)
            change(2, dc1[DC], dc1c[DC], spec_dc)
            dve.wait_ge(root_ready, 3)
            link(nc.vector.reciprocal(rstd2[:], std2[:]))
            scale(bias2[:], total[:], bias_sb[:], ALU.add)
            axpy(delta[DC, :, 0, 0, 0], total[DC], -float(HW), delta[DC, :, 0, 0, 0])
            scale(delta[DC, :, 0, 0, 0], delta[DC, :, 0, 0, 0], 0.5)
            dve.sem_inc(delta_ready, 1)
            nc.vector.tensor_copy(spec[:, :, :, 0, :].rearrange("p b g f -> p (b g) f"),
                                  delta[:, :, :, 1, :].rearrange("p b g f -> p (b g) f")).then_inc(turned_real, 1)
            dve.wait_ge(toeplitz_loaded, 16 * N_TAPS)
            link(nc.vector.tensor_reduce(w5_sum[:], t5[:].rearrange("p k t m -> p m (k t)"), AX.X, ALU.add))


def spatial(nc, B, x, rows, cols, spectrum, y, bank, std2, rstd2, bias2, group_sum, centre_sb, w3, w5, w3_centre,
            w5_centre, w5_sum, eps):
    own = ExitStack()
    with own:
        def sb(name, shape, dt=F32):
            return own.enter_context(nc.sbuf_tensor(name, shape, dt))

        def sem(name):
            return own.enter_context(nc.semaphore(name))

        RING = 2 * PER
        CHUNK = RING // 2
        CHUNKS = (BLOCKS - 1) // CHUNK
        PAIRS = STEPS // 2

        x0 = sb("x0", [P, RING, W])
        x2 = [sb(f"x2_{n}", [P, 2, W]) for n in range(2)]
        n2 = sb("n2", [P, BLOCKS, 2, W2], F16)
        x3 = sb("x3", [P, BLOCKS + SHIFT, W3])
        n3 = x3[:].bitcast(F16).rearrange("p j (h w) -> p j h w", h=2)
        x4 = [sb(f"x4_{n}", [P, 4, W]) for n in range(2)]
        wave = sb("wave", [P, H + R, C], F16)
        image_spec = sb("image_spec", [2 * M1, C, 2 * M1])
        rows_sb = sb("rows_sb", [2 * M1, H])
        cols_sb = sb("cols_sb", [P, 2, W], F16)
        records3 = sb("records3", [P, BLOCKS, 6])
        moments3 = sb("moments3", [P, 3])
        centre3, centre5 = sb("centre3", [P, 2, P]), sb("centre5", [P, 2, P])
        stats3 = sb("stats3", [P, 2])
        var3, std3, rstd3, shift3, const4 = (sb(n, [P, 1]) for n in ("var3", "std3", "rstd3", "shift3", "const4"))
        std2_b, rstd2_b, bias2_b = (sb(n, [P, 1]) for n in ("std2_b", "rstd2_b", "bias2_b"))

        tables_loaded = sem("tables_loaded")
        edges_cleared = sem("edges_cleared")
        spec_loaded = sem("spec_loaded")
        x0_loaded = [sem(f"x0_loaded{n}") for n in range(2)]
        wave_summed = sem("wave_summed")
        wave_high = sem("wave_high")
        wave_low = sem("wave_low")
        synth_done = sem("synth_done")
        x2_ready = sem("x2_ready")
        n2_high = sem("n2_high")
        n2_low = sem("n2_low")
        image_ready = sem("image_ready")
        conv3_done = sem("conv3_done")
        x3_ready = sem("x3_ready")
        x3_recorded = sem("x3_recorded")
        columns_done = sem("columns_done")
        rows_done = sem("rows_done")
        stat_step = sem("stat_step")
        moments_ready = sem("moments_ready")
        moments_summed = sem("moments_summed")
        var3_ready = sem("var3_ready")
        std3_ready = sem("std3_ready")
        rstd3_ready = sem("rstd3_ready")
        const_summed = sem("const_summed")
        const4_ready = sem("const4_ready")
        w5_ready = sem("w5_ready")
        n3_high = sem("n3_high")
        n3_low = sem("n3_low")
        conv5_done = sem("conv5_done")
        x4_ready = sem("x4_ready")
        pe_waited, dve_waited, pool_waited = sem("pe_waited"), sem("dve_waited"), sem("pool_waited")
        x4_stored = [sem(f"x4_stored{n}") for n in range(2)]

        S1 = STEPS + 1
        x_rows = x.rearrange("b c (j r) w -> b r c j w", r=R)
        y_rows = y.rearrange("b c (j r) w -> b r c j w", r=R)

        def n_blocks(tail):
            return 1 if tail else 2

        block = own.enter_context(nc.Block())

        @block.sync
        def _(sp):
            sp.dma_start(rows_sb[:], rows).then_inc(tables_loaded, 16)
            sp.dma_start(cols_sb[:], cols).then_inc(tables_loaded, 16)
            for n in range(2):
                sp.dma_start(x4[n][:, 0, 0:2 * M1], cols.bitcast(F32)[:, 0, 0:2 * M1]).then_inc(x4_stored[n], 16)
            sp.wait_ge(edges_cleared, 4)
            with sp.Fori(0, B) as b:
                sp.wait_ge(wave_summed, b * 8 + 1)
                sp.dma_start(image_spec[:].rearrange("p c f -> p (c f)"),
                             spectrum[b].rearrange("s k c r f -> (s k) (c r f)")).then_inc(spec_loaded, 16)
                for k in range(CHUNKS + 1):
                    sp.wait_ge(x2_ready, b * S1 + (1 + (max(0, CHUNK // 2 * (k - 1)) if k >= 2 else 0)))
                    at = CHUNK * k % RING
                    for r in range(R):
                        back = 1 if r < 2 else 0
                        j0, j1 = max(CHUNK * k, back), min(CHUNK * (k + 1), H // R + back)
                        if j0 >= j1:
                            continue
                        sp.dma_start(x0[C * r:C * (r + 1), at + j0 - CHUNK * k:at + j1 - CHUNK * k, :],
                                     x_rows[b, (r + 2) % R, :, j0 - back:j1 - back, :]).then_inc(x0_loaded[k % 2], 16)

        half_total = [sum(16 * (R if k < CHUNKS else 2) for k in range(h, CHUNKS + 1, 2)) for h in range(2)]

        @block.tensor
        def _(pe):
            def row_dft(b):
                pe.wait_ge(spec_loaded, b * 16 + 16)
                for t in range(C // 4):
                    if t == 0:
                        pe.wait_ge(x2_ready, b * S1 + 1)
                    if t >= 2:
                        pe.wait_ge(wave_high, b * 8 + (t - 1))
                        pe.wait_ge(wave_low, b * 8 + (t - 1))
                    for n in range(2):
                        c = 4 * t + 2 * n
                        last = nc.tensor.matmul(bank[4 + t % 2][:, H * n:H * (n + 1)],
                                                image_spec[:, c:c + 2, :].rearrange("p c f -> p (c f)"), rows_sb[:],
                                                start=True, stop=True)
                    last.then_inc(wave_summed, 1)

            def synth(b, s, parity, tail=False):
                for n in range(n_blocks(tail)):
                    out = bank[4 + parity][:, W * n:W * (n + 1)]
                    lhs = wave[:, bass.ds(s * (2 * R) + R * n, R), :].rearrange("p r c -> p (r c)")
                    for part in range(2):
                        last = nc.tensor.matmul(out, lhs, cols_sb[:, part, :], start=(part == 0), stop=(part == 1))
                last.then_inc(synth_done, 1)

            def synth_wait(b, s, first):
                if first:
                    pe.wait_ge(wave_high, b * 8 + 8)
                    pe.wait_ge(wave_low, b * 8 + 8)
                else:
                    pe.wait_ge(x2_ready, b * S1 + s)

            def conv(taps, src, w, out, s, nb, blocks, columns, lead):
                todo = [(wh, xh, blk, t) for wh, xh in ((0, 0), (1, 0), (0, 1)) for blk in range(blocks)
                        for t in range(taps)]
                for n, (wh, xh, blk, t) in enumerate(todo):
                    at = columns(t)
                    last = nc.tensor.matmul(out[:, 0:W * nb], w[:, wh, blk, t, :],
                                            src[:, bass.ds(s * 2 + blk, nb), xh, at:at + W],
                                            start=(n == 0), stop=(n == len(todo) - 1))
                return last

            def conv3(b):
                pe.wait_ge(image_ready, b * 3 + 3)
                pe.wait_ge(n2_low, b * S1 + (S1 + 2))
                pe.sem_inc(pe_waited, 1)
                with pe.Fori(0, STEPS // 2) as i:
                    for u in range(2):
                        pe.wait_ge(x3_ready, b * S1 + i * 2 + (2 if u == 0 else 2))
                        conv(TAPS3, n2, w3, bank[u], i * 2 + u, 2, 2, lambda t: t, 0).then_inc(conv3_done, 1)
                pe.wait_ge(x3_ready, b * S1 + (STEPS + 1))
                conv(TAPS3, n2, w3, bank[0], STEPS, 1, 1, lambda t: t, 0).then_inc(conv3_done, 1)

            def moments(b):
                pe.wait_ge(moments_ready, b + 1)
                nc.tensor.matmul(bank[6][:, 0:2], group_sum[:], moments3[:, 0:2], start=True,
                                 stop=True).then_inc(moments_summed, 1)

            def constant(b):
                pe.wait_ge(rstd3_ready, b + 1)
                nc.tensor.matmul(bank[7][:, 0:1], w5_sum[:], shift3[:], start=True, stop=True).then_inc(const_summed, 1)

            def conv5_step(b, s, u):
                pe.wait_ge(n3_low, b * S1 + (s + 3))
                pe.wait_ge(x4_ready, b * STEPS + (s + 1))
                conv(TAPS5, n3, w5, bank[2 + u % 2], s, 2, 2, lambda t: TAPS5 - 1 - t, 0).then_inc(conv5_done, 1)

            def conv5(b, with_next):
                pe.wait_ge(w5_ready, b + 1)
                if with_next:
                    synth_wait(b + 1, 0, True)
                    synth(b + 1, 0, 0)
                last_body = STEPS // PER - 1

                def body(i, tail):
                    for u in range(PER):
                        s = i * PER + u
                        if with_next:
                            t = tail and u == PER - 1
                            synth_wait(b + 1, s + 1, False)
                            synth(b + 1, s + 1, (u + 1) % 2, tail=t)
                        conv5_step(b, s, u)

                with pe.Fori(0, last_body) as i:
                    body(i, False)
                body(last_body, True)

            pe.wait_ge(tables_loaded, 32)
            pe.sem_inc(wave_summed, 1)
            pe.wait_ge(edges_cleared, 4)
            row_dft(0)
            synth_wait(0, 0, True)
            synth(0, 0, 0)
            with pe.Fori(0, STEPS // 2 - 1) as i:
                for u in range(2):
                    synth_wait(0, i * 2 + (u + 1), False)
                    synth(0, i * 2 + (u + 1), (u + 1) % 2)
            synth_wait(0, STEPS - 1, False)
            synth(0, STEPS - 1, 1)
            synth_wait(0, STEPS, False)
            synth(0, STEPS, 0, tail=True)
            with pe.Fori(0, B - 1) as b:
                conv3(b)
                row_dft(b + 1)
                moments(b)
                constant(b)
                conv5(b, True)
            conv3(B - 1)
            moments(B - 1)
            constant(B - 1)
            conv5(B - 1, False)

        @block.gpsimd
        def _(pool):
            def reflect(b, j0, count, done):
                pool.wait_ge(x3_ready, b * S1 + done)
                pool.sem_inc(pool_waited, 1)
                for to, at in ((0, 2), (W + 1, W - 1), (W + 2, W - 2), (W + 3, 3)):
                    last = nc.gpsimd.tensor_copy(x3[:, bass.ds(j0, count), to:to + 1],
                                                 x3[:, bass.ds(j0, count), at:at + 1])
                last.then_inc(columns_done, 1)

            nc.gpsimd.memset(n2[:, :, :, 0:1], 0.0).then_inc(edges_cleared, 1)
            nc.gpsimd.memset(n2[:, :, :, W + 1:W + 2], 0.0).then_inc(edges_cleared, 1)
            nc.gpsimd.memset(wave[:], 0.0).then_inc(edges_cleared, 1)
            nc.gpsimd.memset(x0[:], 0.0).then_inc(edges_cleared, 1)
            with pool.Fori(0, B) as b:
                with pool.Fori(0, CHUNKS) as k:
                    reflect(b, k * CHUNK + SHIFT, CHUNK, k * (CHUNK // 2) + (CHUNK // 2 + 2))
                reflect(b, BLOCKS - 1 + SHIFT, 1, S1 + 2)

        @block.scalar
        def _(act):
            def wave_parts(b):
                for t in range(C // 4):
                    act.wait_ge(wave_summed, b * 8 + (t + 2))
                    for e in range(2):
                        half = slice(2 * M1 * e, 2 * M1 * (e + 1))
                        last = nc.scalar.activation(
                            wave[0:2 * M1, 2:H + 2, 4 * t + e:4 * t + e + 3:2].rearrange("p y c -> p c y"),
                            bank[4 + t % 2][half, :].rearrange("p (c y) -> p c y", c=2), ACT.Copy)
                    last.then_inc(wave_high, 1)

            def normalise2(b, s, parity, tail=False):
                nb = n_blocks(tail)
                act.wait_ge(x2_ready, b * S1 + s + 2)
                nc.scalar.activation(n2[:, bass.ds(s * 2, nb), 0, 1:W + 1], x2[parity][:, 0:nb, :], ACT.Copy,
                                     scale=rstd2_b[:]).then_inc(n2_high, 1)

            def take_x3(b):
                act.wait_ge(image_ready, b * 3 + 2)
                with act.Fori(0, STEPS // 2) as i:
                    for u in range(2):
                        act.wait_ge(conv3_done, b * S1 + i * 2 + (u + 1))
                        nc.scalar.activation(x3[:, bass.ds(i * 4 + (2 * u + SHIFT), 2), 1:W + 1],
                                             bank[u][:].rearrange("p (j w) -> p j w", j=2), ACT.Identity,
                                             bias=bias2_b[:]).then_inc(x3_ready, 1)
                act.wait_ge(conv3_done, b * S1 + S1)
                nc.scalar.activation(x3[:, BLOCKS - 1 + SHIFT, 1:W + 1], bank[0][:, 0:W], ACT.Identity,
                                     bias=bias2_b[:]).then_inc(x3_ready, 1)
                act.wait_ge(columns_done, b * (CHUNKS + 1) + (CHUNKS + 1))
                act.wait_ge(x3_recorded, b * S1 + S1)
                for to_row, to_block, of_row, of_block in ((0, 0, 2, 0), (1, BLOCKS - 1, 3, BLOCKS - 2),
                                                           (2, BLOCKS - 1, 2, BLOCKS - 2), (3, BLOCKS - 1, 3, 0)):
                    last = nc.scalar.activation(x3[C * to_row:C * (to_row + 1), to_block + SHIFT, :],
                                                x3[C * of_row:C * (of_row + 1), of_block + SHIFT, :], ACT.Copy)
                last.then_inc(rows_done, 1)

            def normalise3(b, s, tail=False):
                nb = n_blocks(tail)
                act.wait_ge(n3_low, b * S1 + s + 1)
                nc.scalar.activation(n3[:, bass.ds(s * 2, nb), 0, :], x3[:, bass.ds(s * 2 + SHIFT, nb), :], ACT.Copy,
                                     scale=rstd3[:]).then_inc(n3_high, 1)

            def take_x4(b, s, u):
                act.wait_ge(conv5_done, b * STEPS + s + 1)
                if u % 2 == 0:
                    act.wait_ge(x4_stored[u // 2 % 2], b * (PAIRS // 2 * 64) + (s // 4 * 64 + 16) if isinstance(s, int)
                                else b * (PAIRS // 2 * 64) + (s - u) * 16 + (u // 4 * 64 + 16))
                nc.scalar.activation(x4[u // 2 % 2][:, 2 * (u % 2):2 * (u % 2) + 2, :],
                                     bank[2 + u % 2][:].rearrange("p (j w) -> p j w", j=2), ACT.Identity,
                                     bias=const4[:]).then_inc(x4_ready, 1)

            def store_x4(b, s, u):
                act.wait_ge(x4_ready, b * STEPS + s + 4)
                for r in range(R):
                    act.dma_start(y_rows[b, r, :, bass.ds(s * 2, 4), :],
                                  x4[u // 2 % 2][C * r:C * (r + 1), :, :]).then_inc(x4_stored[u // 2 % 2], 16)

            def conv5(b, with_next):
                act.wait_ge(rstd3_ready, b + 1)
                act.wait_ge(rows_done, b + 1)
                normalise3(b, 0)
                normalise3(b, 1)
                if with_next:
                    normalise2(b + 1, 0, 0)
                with act.Fori(2, PER) as s:
                    normalise3(b, s)
                act.wait_ge(const4_ready, b + 1)

                def body(i, tail):
                    for u in range(PER):
                        s = i * PER + u
                        if not tail:
                            normalise3(b, s + PER)
                        elif u == 0:
                            normalise3(b, STEPS, tail=True)
                        if with_next:
                            normalise2(b + 1, s + 1, (u + 1) % 2, tail=tail and u == PER - 1)
                        take_x4(b, s, u)
                        if u % 2 == 1:
                            store_x4(b, s - 1, u - 1)

                last_body = STEPS // PER - 1
                with act.Fori(0, last_body) as i:
                    body(i, False)
                body(last_body, True)

            act.sem_inc(x3_ready, 2)
            act.sem_inc(x4_ready, 2)
            act.sem_inc(n3_high, 1)
            act.wait_ge(edges_cleared, 4)
            wave_parts(0)
            with act.Fori(0, STEPS // 2) as i:
                for u in range(2):
                    normalise2(0, i * 2 + u, u)
            normalise2(0, STEPS, 0, tail=True)
            with act.Fori(0, B - 1) as b:
                take_x3(b)
                wave_parts(b + 1)
                act.wait_ge(var3_ready, b + 1)
                nc.scalar.activation(std3[:], var3[:], ACT.Sqrt, bias=eps[:]).then_inc(std3_ready, 1)
                conv5(b, True)
            take_x3(B - 1)
            act.wait_ge(var3_ready, B)
            nc.scalar.activation(std3[:], var3[:], ACT.Sqrt, bias=eps[:]).then_inc(std3_ready, 1)
            conv5(B - 1, False)
            for n in range(2):
                act.wait_ge(x4_stored[n], 16 + B * (PAIRS // 2) * 64)

        @block.vector
        def _(dve):
            STAT_LINKS = 5
            IMAGE_LINKS = 5

            def image_rstd(b):
                nc.vector.tensor_copy(rstd2_b[:], rstd2[:, bass.ds(b, 1)]).then_inc(image_ready, 1)
                dve.wait_ge(image_ready, b * 3 + 1)

            def image_weights(b):
                nc.vector.tensor_copy(bias2_b[:], bias2[:, bass.ds(b, 1)]).then_inc(image_ready, 1)
                nc.vector.tensor_copy(std2_b[:], std2[:, bass.ds(b, 1)]).then_inc(weight_step, 1)
                dve.wait_ge(weight_step, b * 3 + 1)
                nc.vector.scalar_tensor_tensor(centre3[:], centre_sb[:], std2_b[:], w3_centre[:], ALU.mult,
                                               ALU.add).then_inc(weight_step, 1)
                dve.wait_ge(weight_step, b * 3 + 2)
                nc.vector.tensor_copy(w3[:, 0, :, CENTRE3, :], centre3[:]).then_inc(weight_step, 1)
                dve.wait_ge(weight_step, b * 3 + 3)
                nc.vector.tensor_tensor(w3[:, 1, :, CENTRE3, :], centre3[:], w3[:, 0, :, CENTRE3, :],
                                        ALU.subtract).then_inc(image_ready, 1)

            def wave_parts(b):
                for t in range(C // 4):
                    dve.wait_ge(wave_high, b * 8 + (t + 1))
                    for e in range(2):
                        half = slice(2 * M1 * e, 2 * M1 * (e + 1))
                        c = slice(4 * t + e, 4 * t + e + 3, 2)
                        last = nc.vector.tensor_tensor(wave[2 * M1:4 * M1, 2:H + 2, c].rearrange("p y c -> p c y"),
                                                       bank[4 + t % 2][half, :].rearrange("p (c y) -> p c y", c=2),
                                                       wave[0:2 * M1, 2:H + 2, c].rearrange("p y c -> p c y"),
                                                       ALU.subtract)
                    last.then_inc(wave_low, 1)

            def normalise2(b, s, at, tail=False, wait=None):
                nb = n_blocks(tail)
                if wait is not None:
                    dve.wait_ge(x0_loaded[wait[0]], b * half_total[wait[0]] + wait[1])
                dve.wait_ge(synth_done, b * S1 + s + 1)
                dve.wait_ge(n2_low, b * S1 + s + 1)
                x2_s = x2[at // 2 % 2][:, 0:nb, :]
                nc.vector.tensor_tensor(x2_s, bank[4 + at // 2 % 2][:, 0:W * nb].rearrange("p (j w) -> p j w", j=nb),
                                        x0[:, at:at + nb, :], ALU.add).then_inc(x2_ready, 1)
                dve.wait_ge(n2_high, b * S1 + s + 1)
                low = nc.vector.scalar_tensor_tensor(n2[:, bass.ds(s * 2, nb), 1, 1:W + 1], x2_s, rstd2_b[:],
                                                     n2[:, bass.ds(s * 2, nb), 0, 1:W + 1], ALU.mult, ALU.subtract)
                if not tail:
                    low.then_inc(n2_low, 1)
                else:
                    low.then_inc(edge_step, 1)
                    dve.wait_ge(edge_step, b + 1)
                    nc.vector.memset(n2[0:2 * C, 0, :, 1:W + 1], 0.0)
                    nc.vector.memset(n2[2 * C:4 * C, BLOCKS - 1, :, 1:W + 1], 0.0).then_inc(n2_low, 1)

            def x0_wait(step):
                if step % (CHUNK // 2):
                    return None
                k = step // (CHUNK // 2)
                total = sum(16 * (R if j < CHUNKS else 2) for j in range(k % 2, k + 1, 2))
                return k % 2, total

            def records(b):
                with dve.Fori(0, STEPS) as s:
                    dve.wait_ge(x3_ready, b * S1 + s + 3)
                    for n in range(2):
                        last = nc.vector.bn_stats(records3[:, bass.ds(s * 2 + n, 1), :].rearrange("p n t -> p (n t)"),
                                                  x3[:, bass.ds(s * 2 + (n + SHIFT), 1), 1:W + 1].rearrange("p n w -> p (n w)"))
                    last.then_inc(x3_recorded, 1)
                dve.wait_ge(x3_ready, b * S1 + (S1 + 2))
                nc.vector.bn_stats(records3[:, BLOCKS - 1, :], x3[:, BLOCKS - 1 + SHIFT, 1:W + 1]).then_inc(x3_recorded, 1)
                dve.wait_ge(x3_recorded, b * S1 + S1)
                dve.sem_inc(dve_waited, 1)
                nc.vector.bn_aggr(moments3[:, 0:2], records3[:, 0:BLOCKS - 1, :].rearrange("p n t -> p (n t)")).then_inc(stat_step, 1)
                dve.wait_ge(stat_step, b * STAT_LINKS + 1)
                dve.sem_inc(dve_waited, 1)
                nc.vector.bn_aggr(moments3[0:C, 0:2], records3[0:C, 1:BLOCKS, :].rearrange("p n t -> p (n t)")).then_inc(stat_step, 1)
                dve.wait_ge(stat_step, b * STAT_LINKS + 2)
                nc.vector.scalar_tensor_tensor(moments3[:, 1:2], moments3[:, 0:1], moments3[:, 0:1], moments3[:, 1:2],
                                               ALU.mult, ALU.add).then_inc(moments_ready, 1)

            def statistics(b):
                dve.wait_ge(moments_summed, b + 1)
                nc.vector.tensor_scalar(stats3[:], bank[6][:, 0:2], 1.0 / (GROUP * R), None, ALU.mult).then_inc(stat_step, 1)
                dve.wait_ge(stat_step, b * STAT_LINKS + 3)
                nc.vector.tensor_tensor(moments3[:, 2:3], stats3[:, 0:1], stats3[:, 0:1], ALU.mult).then_inc(stat_step, 1)
                dve.wait_ge(stat_step, b * STAT_LINKS + 4)
                nc.vector.tensor_tensor(var3[:], stats3[:, 1:2], moments3[:, 2:3], ALU.subtract).then_inc(var3_ready, 1)
                dve.wait_ge(std3_ready, b + 1)
                nc.vector.reciprocal(rstd3[:], std3[:]).then_inc(stat_step, 1)
                dve.wait_ge(stat_step, b * STAT_LINKS + 5)
                nc.vector.tensor_tensor(shift3[:], stats3[:, 0:1], rstd3[:], ALU.mult).then_inc(rstd3_ready, 1)

            def weights5(b):
                nc.vector.scalar_tensor_tensor(centre5[:], centre_sb[:], std3[:], w5_centre[:], ALU.mult,
                                               ALU.add).then_inc(weight5_step, 1)
                dve.wait_ge(weight5_step, b * 2 + 1)
                nc.vector.tensor_copy(w5[:, 0, :, CENTRE5, :], centre5[:]).then_inc(weight5_step, 1)
                dve.wait_ge(weight5_step, b * 2 + 2)
                nc.vector.tensor_tensor(w5[:, 1, :, CENTRE5, :], centre5[:], w5[:, 0, :, CENTRE5, :],
                                        ALU.subtract).then_inc(w5_ready, 1)
                dve.wait_ge(const_summed, b + 1)
                nc.vector.tensor_scalar(const4[:], bank[7][:, 0:1], -1.0, None, ALU.mult).then_inc(const4_ready, 1)

            def normalise3(b, s, tail=False):
                nb = n_blocks(tail)
                dve.wait_ge(n3_high, b * S1 + s + 2)
                nc.vector.scalar_tensor_tensor(n3[:, bass.ds(s * 2, nb), 1, :], x3[:, bass.ds(s * 2 + SHIFT, nb), :], rstd3[:],
                                               n3[:, bass.ds(s * 2, nb), 0, :], ALU.mult, ALU.subtract).then_inc(n3_low, 1)

            def conv5(b, with_next):
                dve.wait_ge(rows_done, b + 1)
                normalise3(b, 0)
                normalise3(b, 1)
                if with_next:
                    image_rstd(b + 1)
                    normalise2(b + 1, 0, 0, wait=x0_wait(0))
                with dve.Fori(2, PER) as s:
                    normalise3(b, s)

                def body(i, tail):
                    for u in range(PER):
                        s = i * PER + u
                        if not tail:
                            normalise3(b, s + PER)
                        elif u == 0:
                            normalise3(b, STEPS, tail=True)
                        if with_next:
                            wait = None
                            if (u + 1) % (CHUNK // 2) == 0:
                                k = (u + 1) // (CHUNK // 2)
                                half, count = k % 2, 16 * R * (1 + k // 2)
                                if tail and u == PER - 1:
                                    wait = (half, half_total[0])
                                else:
                                    wait = (half, i * (16 * R) + count)
                            normalise2(b + 1, s + 1, 2 * (u + 1) % RING, tail=tail and u == PER - 1, wait=wait)

                last_body = STEPS // PER - 1
                with dve.Fori(0, last_body) as i:
                    body(i, False)
                body(last_body, True)

            weight_step = sem("weight_step")
            weight5_step = sem("weight5_step")
            edge_step = sem("edge_step")
            dve.sem_inc(n3_low, 1)
            dve.sem_inc(x2_ready, 1)
            dve.sem_inc(n2_low, 2)
            dve.wait_ge(edges_cleared, 4)
            image_rstd(0)
            wave_parts(0)
            with dve.Fori(0, STEPS // PER) as i:
                for u in range(PER):
                    wait = None
                    if u % (CHUNK // 2) == 0:
                        wait = (u // (CHUNK // 2), i * (16 * R) + 16 * R)
                    normalise2(0, i * PER + u, 2 * u, wait=wait)
            normalise2(0, STEPS, 0, tail=True, wait=(0, half_total[0]))
            image_weights(0)
            with dve.Fori(0, B - 1) as b:
                records(b)
                wave_parts(b + 1)
                statistics(b)
                weights5(b)
                conv5(b, True)
                image_weights(b + 1)
            records(B - 1)
            statistics(B - 1)
            weights5(B - 1)
            conv5(B - 1, False)


_TABLES = ["dft_real", "dft_imag", "rows", "cols", "same_group", "own_group", "pick", "column0", "centre"]


def kernel(x, L0_conv_weights_real, L0_conv_weights_imag, L1_conv_coeff_real, L1_conv_coeff_imag, L1_conv_proj,
           L2_conv_W, L2_conv_b, L3_conv_weight):
    import concourse.bacc as bacc
    from concourse.bass_utils import run_bass_kernel_spmd

    x = np.ascontiguousarray(x)
    batch = x.shape[0]
    arrays = {
        "x": x,
        "w0r": L0_conv_weights_real, "w0i": L0_conv_weights_imag,
        "coeff_r": L1_conv_coeff_real, "coeff_i": L1_conv_coeff_imag,
        "proj_t": np.asarray(L1_conv_proj).T,
        "w3_t": np.asarray(L2_conv_W).transpose(1, 2, 3, 0),
        "bias3": np.asarray(L2_conv_b).reshape(C, 1),
        "w5_t": np.asarray(L3_conv_weight).transpose(1, 2, 3, 0),
    }
    tables = constants(batch)
    arrays.update({name: tables[name] for name in _TABLES})
    nc = bacc.Bacc("TRN2", target_bir_lowering=False, num_devices=1)
    ins, args = {}, []
    for name, a in arrays.items():
        a = np.ascontiguousarray(a)
        ins[f"{name}_in"] = a
        args.append(nc.dram_tensor(f"{name}_in", a.shape, mybir.dt.from_np(a.dtype), kind="ExternalInput").ap())
    y = nc.dram_tensor("y_out", x.shape, F32, kind="ExternalOutput").ap()
    four_convolutions(nc, batch, *args, y)
    r = run_bass_kernel_spmd(nc, [ins], core_ids=[0])
    return r.results[0]["y_out"]
```

```python
from contextlib import ExitStack

import numpy as np
import concourse.bass as bass
from concourse import mybir

F32 = mybir.dt.float32
F16 = mybir.dt.float16
ALU = mybir.AluOpType
ACT = mybir.ActivationFunctionType
AX = mybir.AxisListType

P = 128
C, H, W = 32, 256, 256
HW = H * W
GROUP = 2
NG = C // GROUP
M0, M1 = 16, 32
R = P // C
NKH = M1 // R
EPS = 1e-5
N_GROUP = GROUP * HW

CH = 8
NCH = C // CH

BLOCKS = H // R
STEPS = BLOCKS // 2
PER = 8
ROWS = 2 * 2
N2 = H // 2 + 2
N3 = H // 2 + 2
OUT3 = H // 2 + 1
ROWS3 = 3
STEPS3 = OUT3 // ROWS3
PER3 = 6
SHIFT = 2 * ROWS
IN3, IN5 = 2, 3
TAPS3, TAPS5 = 3, 5
WAVES = C // 4


def constants(batch):
    f64 = np.float64
    a = 2 * np.pi * np.outer(np.arange(H), np.arange(M1)).astype(f64) / H
    cs, sn = np.cos(a), np.sin(a)
    dft = np.stack([np.concatenate([cs, -sn], 1), np.concatenate([sn, cs], 1)])
    split = lambda t: (t.astype(np.float16), (t - t.astype(np.float16).astype(f64)).astype(np.float16))
    dft_parts = np.stack(split(dft), 1).reshape(2, 2, 2, P, 2 * M1).transpose(3, 0, 1, 2, 4)
    wave = np.concatenate([cs, -sn], 1).T
    hi, lo = split(wave)
    waves = np.stack([np.concatenate([hi, hi]), np.concatenate([lo, lo])], 1)
    p = np.arange(P)
    ch, q = p % C, p // C
    same_group = (ch[:, None] // GROUP == ch[None, :] // GROUP).astype(np.float32)
    own_group = (ch[:, None] // GROUP == np.arange(NG)[None, :]).astype(np.float32)
    pick = np.zeros((P, 2, 2 * C), np.float32)
    pick[p, 0, ch] = 1
    pick[p, 1, C + ch] = 1
    column0 = np.full((P, NKH, 2), 0.5, np.float32)
    column0[q == 0, 0, 0] = 1
    column0[q == 0, 0, 1] = 0
    centre = np.zeros((P, IN3 * IN3, P), np.float32)
    own_pixel = [(0, 1, 0), (1, 0, 1)]
    for a, yi, yo in own_pixel:
        for b, xi, xo in own_pixel:
            centre[(2 * xi + yi) * C + np.arange(C), IN3 * a + b, (2 * xo + yo) * C + np.arange(C)] = 1
    return {"dft_parts": dft_parts, "waves": waves, "same_group": same_group,
            "own_group": own_group, "pick": pick, "column0": column0, "centre": centre}


def four_convolutions(nc, B, x, w0r, w0i, coeff_r, coeff_i, proj_t, w3_t, bias3, w5_t,
                      dft_parts, waves, same_group, own_group, pick, column0, centre, y):
    spectrum = nc.dram_tensor("spectrum_dram", (B, 2, 2, P, NKH * 2 * M1), F16, kind="Internal").ap()

    keep = ExitStack()
    with keep:
        def sb(name, shape, dt=F32, at=keep):
            return at.enter_context(nc.sbuf_tensor(name, shape, dt))

        def sem(name, at=keep):
            return at.enter_context(nc.semaphore(name))

        bank = [keep.enter_context(nc.psum_tensor(f"bank{n}", [P, 512], F32)) for n in range(8)]
        std2 = sb("std2", [P, B])
        rstd2 = sb("rstd2", [P, B])
        bias2 = sb("bias2", [P, B])
        group_sum = sb("group_sum", [P, P])
        centre_sb = sb("centre_sb", [P, IN3 * IN3, P])
        w3 = sb("w3", [P, 2, IN3, IN3, P], F16)
        w5 = sb("w5", [P, 2, IN5, IN5, P], F16)
        w3_centre = sb("w3_centre", [P, IN3, IN3, P])
        w5_centre = sb("w5_centre", [P, IN3, IN3, P])
        w5_sum = sb("w5_sum", [P, P])
        eps = sb("eps", [P, 1])

        early = ExitStack()
        spec = sb("spec", [P, B, NKH, 2, M1], at=early)
        squares = sb("squares", [P, B, NG], at=early)
        records = sb("records", [P, B, NCH, 2 * 2, 3], at=early)
        analysis(nc, B, x, dft_parts, spec, squares, records, bank)
        mixing(nc, B, w0r, w0i, coeff_r, coeff_i, proj_t, w3_t, bias3, w5_t, same_group, own_group, pick, column0,
               centre, spectrum, spec, squares, records, bank, std2, rstd2, bias2, group_sum, centre_sb, w3, w5, w3_centre,
               w5_centre, w5_sum, eps)
        early.close()
        spatial(nc, B, x, waves, spectrum, y, bank, std2, rstd2, bias2, group_sum, centre_sb, w3, w5, w3_centre,
                w5_centre, w5_sum, eps)


def analysis(nc, B, x, dft_parts, spec, squares, records, bank):
    own = ExitStack()
    with own:
        def sb(name, shape, dt=F32):
            return own.enter_context(nc.sbuf_tensor(name, shape, dt))

        def sem(name):
            return own.enter_context(nc.semaphore(name))

        CHG = CH // GROUP
        tile = [sb(f"x_chunk{k}", [P, 2, CH, W]) for k in range(NCH)]
        parts = [sb(f"x_parts{k}", [P, 2, 2, CH, W], F16) for k in range(NCH)]
        half_dft = sb("half_dft", [P, 2, 2, 2, M1, C], F16)
        t_parts = sb("t_parts", [P, 2, 2, 2, 2 * M1], F16)
        x_squared = [sb(f"x_squared{n}", [P, 2, GROUP * W], mybir.dt.bfloat16) for n in range(CHG - 1)]

        tables_loaded = sem("tables_loaded")
        chunk_loaded = [sem(f"chunk_loaded{k}") for k in range(NCH)]
        rows_done = sem("rows_done")
        high_ready = sem("high_ready")
        last_high_ready = sem("last_high_ready")
        low_ready = sem("low_ready")
        records_ready = sem("records_ready")
        squares_ready = sem("squares_ready")
        rows_high = sem("rows_high")
        rows_low = sem("rows_low")
        cols_done = sem("cols_done")
        cols_copied = sem("cols_copied")
        pool_waited = sem("analysis_pool_waited")

        def last_group(v):
            return v[:, :, CH - GROUP:CH, :].rearrange("p h c x -> p h (c x)")

        def others(v):
            return v[:, :, 0:CH - GROUP, :].rearrange("p h c x -> p h (c x)")

        def rows_out(k, part, xh):
            return half_dft[:, part, xh, :, :, CH * k:CH * (k + 1)].rearrange("p r f c -> p c (r f)")

        def rows_in(k, xh):
            return bank[2 * (k % 2) + xh][:, :].rearrange("p (c f) -> p c f", c=CH)

        block = own.enter_context(nc.Block())

        @block.sync
        def _(sp):
            sp.dma_start(t_parts[:], dft_parts).then_inc(tables_loaded, 16)
            with sp.Fori(0, B) as b:
                for k in range(NCH):
                    sp.wait_ge(squares_ready, b * NCH + (k + 1))
                    sp.wait_ge(records_ready, b * NCH + (k + 1))
                    for h in range(2):
                        src = x[b, CH * k:CH * (k + 1), P * h:P * (h + 1), :].rearrange("c y x -> y c x")
                        sp.dma_start(tile[k][:, h], src).then_inc(chunk_loaded[k], 16)

        @block.tensor
        def _(pe):
            pe.sem_inc(rows_done, NCH)
            pe.sem_inc(cols_done, 1)
            pe.wait_ge(tables_loaded, 16)

            def image(b, first):
                for k in range(NCH):
                    pe.wait_ge(low_ready, b * NCH + (k + 1))
                    pe.wait_ge(rows_low, b * NCH + (k + 1))
                    for c in range(CH):
                        for xh in range(2):
                            out = bank[2 * (k % 2) + xh][:, 2 * M1 * c:2 * M1 * (c + 1)]
                            todo = [(yh, xp, tp) for yh in range(2) for xp, tp in ((0, 0), (0, 1), (1, 0))]
                            for n, (yh, xp, tp) in enumerate(todo):
                                last = nc.tensor.matmul(out, parts[k][:, xp, yh, c, P * xh:P * (xh + 1)],
                                                        t_parts[:, 0, tp, yh, :], start=(n == 0),
                                                        stop=(n == len(todo) - 1))
                    last.then_inc(rows_done, 1)
                    if k == 0 and not first:
                        columns(b - 1)

            def columns(b):
                pe.wait_ge(rows_low, b * NCH + (2 + NCH))
                pe.wait_ge(cols_copied, b + 1)
                for g in range(NKH):
                    out = bank[4][:, 2 * M1 * g:2 * M1 * (g + 1)]
                    todo = [(xh, r, hp, tp) for xh in range(2) for r in range(2) for hp, tp in ((0, 0), (0, 1), (1, 0))]
                    for n, (xh, r, hp, tp) in enumerate(todo):
                        last = nc.tensor.matmul(out, half_dft[:, hp, xh, r, R * g:R * (g + 1), :],
                                                t_parts[:, r, tp, xh, :], start=(n == 0), stop=(n == len(todo) - 1))
                last.then_inc(cols_done, 1)

            image(0, True)
            with pe.Fori(1, B) as b:
                image(b, False)
            columns(B - 1)

        @block.gpsimd
        def _(pool):
            with pool.Fori(0, B) as b:
                for k in range(NCH):
                    pool.wait_ge(chunk_loaded[k], b * 32 + 32)
                    pool.wait_ge(rows_done, b * NCH + (k + 1))
                    pool.sem_inc(pool_waited, 1)
                    nc.gpsimd.tensor_copy(last_group(parts[k][:, 0]), last_group(tile[k])).then_inc(last_high_ready, 1)

        @block.scalar
        def _(act):
            act.sem_inc(cols_copied, 1)
            act.sem_inc(squares_ready, NCH)

            def take_rows(b, k):
                act.wait_ge(rows_done, b * NCH + (NCH + k + 1))
                for xh in range(2):
                    last = nc.scalar.activation(rows_out(k, 0, xh), rows_in(k, xh), ACT.Copy)
                last.then_inc(rows_high, 1)

            def take_spectrum(b):
                act.wait_ge(cols_done, b + 2)
                nc.scalar.activation(spec[:, b, :, :, :].rearrange("p g r f -> p (g r f)"), bank[4][:, :],
                                     ACT.Copy).then_inc(cols_copied, 1)

            def high(b, k):
                act.wait_ge(chunk_loaded[k], b * 32 + 32)
                act.wait_ge(rows_done, b * NCH + (k + 1))
                nc.scalar.activation(others(parts[k][:, 0]), others(tile[k]), ACT.Copy).then_inc(high_ready, 1)

            def image(b, first):
                for k in range(NCH):
                    if k != 2:
                        high(b, k)
                    if k == 1:
                        high(b, 2)
                    act.wait_ge(squares_ready, b * NCH + (NCH + k))
                    for g in range(CHG - 1):
                        last = nc.scalar.activation(
                            x_squared[g][:], tile[k][:, :, GROUP * g:GROUP * (g + 1), :].rearrange("p h c x -> p h (c x)"),
                            ACT.Square, accum_out=squares[:, b, CHG * k + g:CHG * k + g + 1])
                    last.then_inc(squares_ready, 1)
                    if k == 1 and not first:
                        take_spectrum(b - 1)
                    if k:
                        take_rows(b, k - 1)
                    elif not first:
                        take_rows(b - 1, NCH - 1)

            image(0, True)
            with act.Fori(1, B) as b:
                image(b, False)
            take_rows(B - 1, NCH - 1)
            take_spectrum(B - 1)

        @block.vector
        def _(dve):
            dve.sem_inc(records_ready, NCH)
            dve.sem_inc(rows_low, 2)

            def take_rows(b, k):
                dve.wait_ge(rows_high, b * NCH + (k + 1))
                for xh in range(2):
                    last = nc.vector.tensor_tensor(rows_out(k, 1, xh), rows_in(k, xh), rows_out(k, 0, xh), ALU.subtract)
                last.then_inc(rows_low, 1)

            def image(b, first):
                for k in range(NCH):
                    dve.wait_ge(high_ready, b * NCH + (k + 1))
                    dve.wait_ge(last_high_ready, b * NCH + (k + 1))
                    nc.vector.tensor_tensor(*(v.rearrange("p h c x -> p (h c x)") for v in (
                        parts[k][:, 1], tile[k][:], parts[k][:, 0])), ALU.subtract).then_inc(low_ready, 1)
                    for h in range(2):
                        last = nc.vector.bn_stats(records[:, b, k, 2 * h:2 * h + 2, :].rearrange("p n t -> p (n t)"),
                                                  tile[k][:, h, CH - GROUP:CH, :].rearrange("p c x -> p (c x)"))
                    last.then_inc(records_ready, 1)
                    if k:
                        take_rows(b, k - 1)
                    elif not first:
                        take_rows(b - 1, NCH - 1)

            image(0, True)
            with dve.Fori(1, B) as b:
                image(b, False)
            take_rows(B - 1, NCH - 1)


def mixing(nc, B, w0r, w0i, coeff_r, coeff_i, proj_t, w3_t, bias3, w5_t, same_group, own_group, pick, column0,
           centre, spectrum, spec, squares, records, bank, std2, rstd2, bias2, group_sum, centre_sb, w3, w5, w3_centre,
           w5_centre, w5_sum, eps):
    own = ExitStack()
    with own:
        def sb(name, shape, dt=F32):
            return own.enter_context(nc.sbuf_tensor(name, shape, dt))

        def sem(name):
            return own.enter_context(nc.semaphore(name))

        HF = M1 // 2
        HALVES = 2 * NKH
        delta = sb("delta", [P, B, NKH, 2, M1])
        coeff_in = sb("coeff_in", [2 * C, C, R, M1])
        coeff = sb("coeff", [2 * C, M1, R, C])
        diagonals = sb("diagonals", [P, 2, 2, HF, P])
        diagonal = [diagonals[:, n] for n in range(2)]
        w0 = diagonals[0:2 * C].rearrange("p n s f m -> p (n s f m)").rearrange("p (o f c) -> p o f c", o=C, f=M0)
        scaled = [sb(f"scaled{n}", [P, 2, B, 2, M1]) for n in range(2)]
        mixed = [sb(f"mixed{n}", [P, B, 2, HF]) for n in range(2)]
        low = scaled[0]
        low_s = sb("low_s", [2 * C, M0, 2, B])
        proj = sb("proj", [2 * C, C])
        pick_sb = sb("pick_sb", [P, 2, 2 * C])
        own_group_sb = sb("own_group_sb", [P, NG])
        column0_sb = sb("column0_sb", [P, 2 * NKH])
        ones = sb("ones", [P, P])
        moment2 = sb("moment2", [P, B, NCH, 4])
        masked = sb("masked", [P, B, NG])
        mean_square = sb("mean_square", [P, B])
        energy = sb("energy", [P, 3, B])
        ends = sb("ends", [P, 2, B])
        mean, var, std, rstd, total, tmp, dc0, dc1, dc1c = (sb(n, [P, B]) for n in (
            "mean", "var", "std", "rstd", "total", "tmp", "dc0", "dc1", "dc1c"))
        junk = sb("junk", [P, NKH * 2 * M1])
        t3 = w3_centre
        delta_parts = spec[:].bitcast(F16).rearrange("p b g r f -> p (b g r f)").rearrange(
            "p (s b r f) -> p s b r f", s=2, b=B * NKH, r=2)
        turned_parts = diagonals[:].bitcast(F16).rearrange("p n s f m -> p (n s f m)")[:, 0:B * 4 * NKH * M1].rearrange(
            "p (s b r f) -> p s b r f", s=2, b=B * NKH, r=2)
        delta_v = delta[:].rearrange("p b g r f -> p (b g) r f")
        SPLITS = -(-B // 4)
        images = lambda k: range(4 * k, min(B, 4 * k + 4))
        t5 = sb("t5", [P, IN5, IN5, P])
        bias_sb = sb("bias_sb", [P, 1])
        DC = slice(0, C)

        tables_loaded = sem("mix_tables_loaded")
        toeplitz_cleared = sem("toeplitz_cleared")
        toeplitz_loaded = sem("toeplitz_loaded")
        toeplitz_split = sem("toeplitz_split")
        cleared = sem("cleared")
        coeff_loaded = sem("coeff_loaded")
        coeff_turned = sem("coeff_turned")
        dve_step = sem("mix_dve_step")
        squares_ready = sem("squares_ready")
        moments_summed = sem("moments_summed")
        variance_ready = sem("variance_ready")
        root_ready = sem("root_ready")
        centred = sem("centred")
        energy_ready = sem("energy_ready")
        low_ready = sem("low_ready")
        low_summed = sem("low_summed")
        low_copied = sem("low_copied")
        layer0_done = sem("layer0_done")
        ends_ready = sem("ends_ready")
        ends_summed = sem("ends_summed")
        scaled_ready = sem("scaled_ready")
        combined = sem("combined")
        diagonal_real = sem("diagonal_real")
        diagonal_imag = sem("diagonal_imag")
        product_done = sem("product_done")
        mixed_ready = sem("mixed_ready")
        mixed_added = sem("mixed_added")
        delta_ready = sem("delta_ready")
        split_high = sem("split_high")
        split_low = sem("split_low")
        turned_low = sem("turned_low")
        written = sem("spectrum_written")

        def taps(n):
            for a in range(IN3 if n == TAPS3 else IN5):
                for i in range(2):
                    for o in range(2):
                        d = 2 * a + i - o
                        if 0 <= d < n:
                            yield a, i, o, d if n == TAPS3 else n - 1 - d

        N_TAPS = sum(len(list(taps(t))) ** 2 for t in (TAPS3, TAPS5))
        N_TABLES = 9 + R

        block = own.enter_context(nc.Block())

        @block.sync
        def _(sp):
            for dst, src in ((group_sum[:], same_group), (pick_sb[:], pick), (own_group_sb[:], own_group),
                             (column0_sb[:], column0.rearrange("p g r -> p (g r)")), (centre_sb[:], centre)):
                sp.dma_start(dst, src).then_inc(tables_loaded, 16)
            for part in range(2):
                sp.dma_start(proj[C * part:C * (part + 1), :], proj_t).then_inc(tables_loaded, 16)
                sp.dma_start(w0[C * part:C * (part + 1)], (w0r, w0i)[part]).then_inc(tables_loaded, 16)
            for r in range(R):
                sp.dma_start(bias_sb[C * r:C * (r + 1), :], bias3).then_inc(tables_loaded, 16)
            sp.wait_ge(toeplitz_cleared, 2)
            for dst, src, n in ((t3, w3_t, TAPS3), (t5, w5_t, TAPS5)):
                for a, yi, yo, ty in taps(n):
                    for b, xi, xo, tx in taps(n):
                        i, o = C * (2 * xi + yi), C * (2 * xo + yo)
                        sp.dma_start(dst[i:i + C, a, b, o:o + C], src[:, ty, tx, :]).then_inc(toeplitz_loaded, 16)
            for g in range(NKH):
                if g >= 1:
                    sp.wait_ge(coeff_turned, g)
                for part in range(2):
                    sp.dma_start(coeff_in[C * part:C * (part + 1)],
                                 (coeff_r, coeff_i)[part][:, :, R * g:R * (g + 1), :]).then_inc(coeff_loaded, 16)
            for k in range(SPLITS):
                sp.wait_ge(split_low, k + 1)
                sp.wait_ge(turned_low, k + 1)
                for b in images(k):
                    for part, src in enumerate((delta_parts, turned_parts)):
                        sp.dma_start(spectrum[b, :, part].rearrange("s p n -> p s n"),
                                     src[:, :, NKH * b:NKH * (b + 1)].rearrange("p s g r f -> p s (g r f)")).then_inc(written, 16)
            sp.wait_ge(written, 16 * 2 * B)

        @block.tensor
        def _(pe):
            pe.wait_ge(tables_loaded, 16 * N_TABLES)
            pe.wait_ge(cleared, 1)
            pe.wait_ge(squares_ready, 1)
            nc.tensor.matmul(bank[0][:, 0:B * NG], ones[:], squares[:].rearrange("p b g -> p (b g)"), start=True, stop=True)
            nc.tensor.matmul(bank[1][:, 0:B], group_sum[:], ends[:, 1], start=True, stop=True).then_inc(moments_summed, 1)
            pe.wait_ge(low_ready, 1)
            for part in range(2):
                last = nc.tensor.matmul(bank[1][0:2 * C, 0:M0 * 2 * B], pick_sb[:, part, :],
                                        low[:, part, :, :, 0:M0].rearrange("p b r f -> p f r b"),
                                        start=(part == 0), stop=(part == 1))
            last.then_inc(low_summed, 1)
            pe.wait_ge(low_copied, 1)
            for f in range(M0):
                q = f % R
                for c in range(M0):
                    last = nc.tensor.matmul(bank[4 + f // R][C * q:C * (q + 1), 2 * B * c:2 * B * (c + 1)],
                                            w0[:, :, f, c], low_s[:, f, :, :].rearrange("p r b -> p (r b)"),
                                            start=True, stop=True)
            last.then_inc(layer0_done, 1)
            pe.wait_ge(ends_ready, 1)
            nc.tensor.matmul(bank[0][:, 0:2 * B], group_sum[:], ends[:].rearrange("p k b -> p (k b)"),
                             start=True, stop=True).then_inc(ends_summed, 1)

            def combine(n):
                g, half = n // 2, n % 2
                pe.wait_ge(coeff_turned, g + 1)
                if n >= 2:
                    pe.wait_ge(diagonal_real, n - 1)
                    pe.wait_ge(diagonal_imag, n - 1)
                for f in range(HF):
                    for part in range(2):
                        rank = slice(C * part, C * (part + 1))
                        last = nc.tensor.matmul(bank[4 + 2 * (n % 2) + part][:, C * f:C * (f + 1)],
                                                coeff[rank, HF * half + f].rearrange("p q c -> p (q c)"), proj[rank, :],
                                                start=True, stop=True)
                last.then_inc(combined, 1)

            pe.wait_ge(scaled_ready, 1)
            combine(0)
            for n in range(HALVES):
                if n + 1 < HALVES:
                    combine(n + 1)
                pe.wait_ge(diagonal_real, n + 1)
                pe.wait_ge(diagonal_imag, n + 1)
                pe.wait_ge(scaled_ready, n // 2 + 1)
                if n >= 2:
                    pe.wait_ge(mixed_ready, n - 1)
                for f in range(HF):
                    for part in range(2):
                        rhs = scaled[n // 2 % 2][:, part, :, :, HF * (n % 2) + f].rearrange("p b r -> p r b")
                        last = nc.tensor.matmul(bank[2 + n % 2][:, 2 * B * f:2 * B * (f + 1)],
                                                diagonal[n % 2][:, part, f, :], rhs, start=(part == 0),
                                                stop=(part == 1))
                last.then_inc(product_done, 1)
            pe.wait_ge(ends_ready, 2)
            nc.tensor.matmul(bank[0][:, 0:2 * B], group_sum[:], ends[:].rearrange("p k b -> p (k b)"),
                             start=True, stop=True).then_inc(ends_summed, 1)

        @block.gpsimd
        def _(pool):
            nc.gpsimd.memset(t3[:], 0.0).then_inc(toeplitz_cleared, 1)
            nc.gpsimd.memset(t5[:], 0.0).then_inc(toeplitz_cleared, 1)
            nc.gpsimd.memset(ones[:], 1.0 / N_GROUP).then_inc(cleared, 1)

            def turn(g):
                pool.wait_ge(coeff_loaded, 32 * (g + 1))
                if g >= 1:
                    pool.wait_ge(combined, 2 * g)
                nc.gpsimd.tensor_copy(coeff[:].rearrange("p f q c -> p c q f"), coeff_in[:]).then_inc(coeff_turned, 1)

            turn(0)
            pool.wait_ge(layer0_done, 1)
            for n in range(2):
                nc.gpsimd.memset(diagonal[n], 0.0).then_inc(cleared, 1)
            pool.wait_ge(toeplitz_loaded, 16 * N_TAPS)
            pool.wait_ge(tables_loaded, 16 * N_TABLES)
            nc.gpsimd.tensor_copy(w5[:, 0], t5[:]).then_inc(toeplitz_split, 1)
            nc.gpsimd.tensor_copy(w5_centre[:], t5[:, 0:IN3, 0:IN3, :]).then_inc(toeplitz_split, 1)
            pool.wait_ge(toeplitz_split, 2)
            nc.gpsimd.tensor_tensor(w5[:, 1], t5[:], w5[:, 0], ALU.subtract).then_inc(toeplitz_split, 1)
            for n in range(HALVES):
                if n % 2 == 0 and n // 2 + 1 < NKH:
                    turn(n // 2 + 1)
                pool.wait_ge(mixed_ready, n + 1)
                for dst in (spec, delta):
                    part = dst[:, :, n // 2, :, HF * (n % 2):HF * (n % 2 + 1)]
                    nc.gpsimd.tensor_tensor(part, part, mixed[n % 2][:], ALU.add).then_inc(mixed_added, 1)

        @block.scalar
        def _(act):
            def energies(k):
                act.wait_ge(centred, k + 1)
                for b in range(B):
                    if B * k + b:
                        act.wait_ge(energy_ready, B * k + b)
                    nc.scalar.activation(junk[:], spec[:, b].rearrange("p g r f -> p (g r f)"), ACT.Square,
                                         accum_out=energy[:, k, b:b + 1]).then_inc(energy_ready, 1)

            def root(k, out):
                act.wait_ge(variance_ready, k + 1)
                nc.scalar.activation(out[:], var[:], ACT.Sqrt, bias=eps[:]).then_inc(root_ready, 1)

            root(0, std)
            energies(0)
            act.wait_ge(low_summed, 1)
            nc.scalar.activation(low_s[:].rearrange("p f r b -> p (f r b)"), bank[1][0:2 * C, 0:M0 * 2 * B],
                                 ACT.Copy).then_inc(low_copied, 1)
            energies(1)
            root(1, std)
            act.wait_ge(cleared, 3)
            for n in range(HALVES):
                act.wait_ge(combined, n + 1)
                if n >= 2:
                    act.wait_ge(product_done, n - 1)
                for q in range(R):
                    rows_q = slice(C * q, C * (q + 1))
                    last = nc.scalar.activation(diagonal[n % 2][rows_q, 0, :, rows_q],
                                                bank[4 + 2 * (n % 2)][rows_q, :].rearrange("p (f o) -> p f o", o=C),
                                                ACT.Copy)
                last.then_inc(diagonal_real, 1)
            energies(2)
            root(2, std2)
            act.wait_ge(delta_ready, 1)
            for k in range(SPLITS):
                at = slice(NKH * images(k)[0], NKH * (images(k)[-1] + 1))
                flat = lambda v: v.rearrange("p b r f -> p (b r f)")
                nc.scalar.activation(flat(delta_parts[:, 0, at]), flat(delta_v[:, at]), ACT.Copy,
                                     scale=2.0 / HW).then_inc(split_high, 1)
                for r in range(2):
                    nc.scalar.activation(turned_parts[:, 0, at, r, :], delta_v[:, at, 1 - r, :], ACT.Copy,
                                         scale=(-2.0 if r else 2.0) / HW).then_inc(split_high, 1)

        @block.vector
        def _(dve):
            chain = [0]

            def link(ins):
                chain[0] += 1
                ins.then_inc(dve_step, 1)
                dve.wait_ge(dve_step, chain[0])

            def put(out, a, b, op):
                link(nc.vector.tensor_tensor(out, a, b, op))

            def scale(out, a, k, op=ALU.mult):
                link(nc.vector.tensor_scalar(out, a, k, None, op))

            def axpy(out, a, k, b):
                link(nc.vector.scalar_tensor_tensor(out, a, k, b, ALU.mult, ALU.add))

            def over_images(t, n):
                return t[:, :, None].to_broadcast([P, B, n])

            spec_dc = spec[DC, :, 0, 0, 0]
            link(nc.vector.memset(delta[:], 0.0))
            link(nc.vector.memset(eps[:], EPS))
            link(nc.vector.memset(ends[:], 0.0))
            rec_mean, rec_var = (records[:, :, :, :, n].rearrange("p b k e -> p (b k e)") for n in (1, 2))
            flat = moment2[:].rearrange("p b k e -> p (b k e)")
            put(flat, rec_mean, rec_mean, ALU.mult)
            axpy(flat, flat, float(W), rec_var)
            link(nc.vector.tensor_reduce(squares[:].rearrange("p b (k g) -> p b k g", k=NCH)[:, :, :, CH // GROUP - 1],
                                         moment2[:], AX.X, ALU.add))
            link(nc.vector.tensor_copy(ends[DC, 1], spec_dc))
            dve.sem_inc(squares_ready, 1)
            dve.wait_ge(moments_summed, 1)
            dve.wait_ge(tables_loaded, 16 * N_TABLES)
            put(masked[:], bank[0][:, 0:B * NG].rearrange("p (b g) -> p b g", g=NG),
                own_group_sb[:, None, :].to_broadcast([P, B, NG]), ALU.mult)
            link(nc.vector.tensor_reduce(mean_square[:], masked[:], AX.X, ALU.add))
            scale(mean[:], bank[1][:, 0:B], 1.0 / N_GROUP)
            m0, q0 = mean[:], mean_square[:]
            put(tmp[:], m0, m0, ALU.mult)
            put(var[:], q0, tmp[:], ALU.subtract)
            dve.sem_inc(variance_ready, 1)
            axpy(spec_dc, m0[DC], -float(HW), spec_dc)
            dve.sem_inc(centred, 1)
            link(nc.vector.tensor_copy(dc0[DC], spec_dc))
            link(nc.vector.tensor_copy(total[:], m0))
            dve.wait_ge(root_ready, 1)
            link(nc.vector.reciprocal(rstd[:], std[:]))
            g_low = [spec[:, :, g, :, 0:M0] for g in range(M0 // R)]
            low0, low1 = low[:, 0, :, :, 0:M0], low[:, 1, :, :, 0:M0]
            put(low0, g_low[0], g_low[1], ALU.add)
            for g in g_low[2:]:
                put(low0, low0, g, ALU.add)
            for r in range(2):
                put(low0[:, :, r, :], low0[:, :, r, :], over_images(rstd, M0), ALU.mult)
            scale(low1[:, :, 0, :], low0[:, :, 1, :], -1.0)
            link(nc.vector.tensor_copy(low1[:, :, 1, :], low0[:, :, 0, :]))
            dve.sem_inc(low_ready, 1)
            dve.wait_ge(layer0_done, 1)
            dve.wait_ge(energy_ready, B)
            for g in range(M0 // R):
                link(nc.vector.tensor_copy(delta[:, :, g, :, 0:M0].rearrange("p b r f -> p f r b"),
                                           bank[4 + g][:, 0:M0 * 2 * B].rearrange("p (f r b) -> p f r b", f=M0, r=2)))
            n_low = 2 * M0 // R
            column = delta[:].rearrange("p b g r f -> p b (g r) f")[:, :, 0:n_low, 0]
            put(column, column, column0_sb[:, None, 0:n_low].to_broadcast([P, B, n_low]), ALU.mult)
            for g in range(M0 // R):
                put(g_low[g], g_low[g], delta[:, :, g, :, 0:M0], ALU.add)
            dve.sem_inc(centred, 1)
            link(nc.vector.tensor_copy(dc1[DC], spec_dc))

            def change(k, dc_old2, dc_old, dc_new):
                dve.wait_ge(energy_ready, B * (k + 1))
                put(tmp[:], energy[:, k], energy[:, k - 1], ALU.subtract)
                scale(ends[:, 0], tmp[:], 2.0)
                for dc, factor in ((dc_old2, 2.0), (dc_old, -1.0), (dc_new, -1.0)):
                    put(tmp[DC], dc, dc, ALU.mult)
                    axpy(ends[DC, 0], tmp[DC], factor, ends[DC, 0])
                link(nc.vector.tensor_copy(ends[DC, 1], dc_new))
                dve.sem_inc(ends_ready, 1)
                dve.wait_ge(ends_summed, k)
                scale(mean[:], bank[0][:, B:2 * B], 1.0 / N_GROUP)
                axpy(var[:], bank[0][:, 0:B], 1.0 / HW / N_GROUP, var[:])
                put(tmp[:], mean[:], mean[:], ALU.mult)
                put(var[:], var[:], tmp[:], ALU.subtract)
                dve.sem_inc(variance_ready, 1)
                put(total[:], total[:], mean[:], ALU.add)

            change(1, dc0[DC], dc0[DC], dc1[DC])
            axpy(spec_dc, mean[DC], -float(HW), spec_dc)
            link(nc.vector.tensor_copy(dc1c[DC], spec_dc))
            dve.wait_ge(root_ready, 2)
            link(nc.vector.reciprocal(rstd[:], std[:]))

            def normalise(g):
                if g >= 2:
                    dve.wait_ge(product_done, 2 * (g - 1))
                s = scaled[g % 2]
                put(s[:, 0].rearrange("p b r f -> p b (r f)"), spec[:, :, g].rearrange("p b r f -> p b (r f)"),
                    over_images(rstd, 2 * M1), ALU.mult)
                scale(s[:, 1, :, 0, :], s[:, 0, :, 1, :], -1.0)
                link(nc.vector.tensor_copy(s[:, 1, :, 1, :], s[:, 0, :, 0, :]))
                dve.sem_inc(scaled_ready, 1)

            def lay_out(n):
                dve.wait_ge(combined, n + 1)
                if n >= 2:
                    dve.wait_ge(product_done, n - 1)
                for q in range(R):
                    rows_q = slice(C * q, C * (q + 1))
                    last = nc.vector.tensor_copy(diagonal[n % 2][rows_q, 1, :, rows_q],
                                                 bank[5 + 2 * (n % 2)][rows_q, :].rearrange("p (f o) -> p f o", o=C))
                last.then_inc(diagonal_imag, 1)

            normalise(0)
            dve.wait_ge(cleared, 3)
            lay_out(0)
            for n in range(HALVES):
                if n % 2 == 0 and n // 2 + 1 < NKH:
                    normalise(n // 2 + 1)
                if n + 1 < HALVES:
                    lay_out(n + 1)
                dve.wait_ge(product_done, n + 1)
                if n >= 2:
                    dve.wait_ge(mixed_added, 2 * (n - 1))
                link(nc.vector.tensor_copy(mixed[n % 2][:].rearrange("p b r f -> p f r b"),
                                           bank[2 + n % 2][:, 0:HF * 2 * B].rearrange("p (f r b) -> p f r b", f=HF, r=2)))
                if n % 2 == 0:
                    column = mixed[n % 2][:, :, :, 0]
                    put(column, column, column0_sb[:, None, n:n + 2].to_broadcast([P, B, 2]), ALU.mult)
                dve.sem_inc(mixed_ready, 1)
            dve.wait_ge(mixed_added, 2 * HALVES)
            dve.sem_inc(centred, 1)
            change(2, dc1[DC], dc1c[DC], spec_dc)
            dve.wait_ge(root_ready, 3)
            link(nc.vector.reciprocal(rstd2[:], std2[:]))
            scale(bias2[:], total[:], bias_sb[:], ALU.add)
            axpy(delta[DC, :, 0, 0, 0], total[DC], -float(HW), delta[DC, :, 0, 0, 0])
            scale(delta[DC, :, 0, 0, 0], delta[DC, :, 0, 0, 0], 0.5)
            dve.sem_inc(delta_ready, 1)
            for k in range(SPLITS):
                at = slice(NKH * images(k)[0], NKH * (images(k)[-1] + 1))
                flat = lambda v: v.rearrange("p b r f -> p (b r f)")
                dve.wait_ge(split_high, 3 * k + 1)
                nc.vector.scalar_tensor_tensor(flat(delta_parts[:, 1, at]), flat(delta_v[:, at]), 2.0 / HW,
                                               flat(delta_parts[:, 0, at]), ALU.mult, ALU.subtract).then_inc(split_low, 1)
                dve.wait_ge(split_high, 3 * k + 3)
                nc.vector.scalar_tensor_tensor(turned_parts[:, 1, at, 0, :], delta_v[:, at, 1, :], 2.0 / HW,
                                               turned_parts[:, 0, at, 0, :], ALU.mult, ALU.subtract)
                nc.vector.scalar_tensor_tensor(turned_parts[:, 1, at, 1, :], delta_v[:, at, 0, :], -2.0 / HW,
                                               turned_parts[:, 0, at, 1, :], ALU.mult,
                                               ALU.subtract).then_inc(turned_low, 1)
            dve.wait_ge(toeplitz_loaded, 16 * N_TAPS)
            link(nc.vector.tensor_reduce(w5_sum[:], t5[:].rearrange("p k t m -> p m (k t)"), AX.X, ALU.add))


def spatial(nc, B, x, waves, spectrum, y, bank, std2, rstd2, bias2, group_sum, centre_sb, w3, w5, w3_centre,
            w5_centre, w5_sum, eps):
    own = ExitStack()
    with own:
        def sb(name, shape, dt=F32):
            return own.enter_context(nc.sbuf_tensor(name, shape, dt))

        def sem(name):
            return own.enter_context(nc.semaphore(name))

        RING = 2 * PER
        CHUNK = RING // 2
        CHUNKS = BLOCKS // CHUNK
        PAIRS = STEPS // 2
        HALF = P // 2
        K = H // 2
        EARLY = STEPS3 - 1 - PER3
        LATE = PER3 + 3

        x0 = sb("x0", [P, RING, W])
        x2 = [sb(f"x2_{n}", [P, ROWS, K]) for n in range(2)]
        n2 = sb("n2", [P, N2, 2, N2], F16)
        x3 = sb("x3", [P, N3 + SHIFT, N3])
        n3 = x3[:].bitcast(F16).rearrange("p i (h k) -> p i h k", h=2)
        x4 = [sb(f"x4_{n}", [P, 4, W]) for n in range(2)]
        wave = sb("wave", [P, H, C], F16)
        wave_v = wave[:].rearrange("p y (t n e) -> p t e n y", n=2, e=2)
        spec_parts = sb("spec_parts", [P, C, 2 * M1], F16)
        waves_sb = sb("waves_sb", [P, 2, W], F16)
        records_early = sb("records_early", [P, EARLY, 6])
        records_late = sb("records_late", [P, 3 + LATE * 6])
        aggregate = sb("aggregate", [P, 2])
        moments3 = sb("moments3", [P, 3])
        centre3, centre5 = sb("centre3", [P, IN3, IN3, P]), sb("centre5", [P, IN3, IN3, P])
        stats3 = sb("stats3", [P, 2])
        var3, std3, rstd3, shift3, const4, warm = (sb(n, [P, 1]) for n in (
            "var3", "std3", "rstd3", "shift3", "const4", "warm"))
        std2_b, rstd2_b, bias2_b = (sb(n, [P, 1]) for n in ("std2_b", "rstd2_b", "bias2_b"))

        tables_loaded = sem("tables_loaded")
        edges_cleared = sem("edges_cleared")
        spec_loaded = sem("spec_loaded")
        x0_loaded = [sem(f"x0_loaded{n}") for n in range(2)]
        wave_summed = sem("wave_summed")
        wave_high = sem("wave_high")
        wave_low = sem("wave_low")
        synth_done = sem("synth_done")
        x2_ready = sem("x2_ready")
        n2_high = sem("n2_high")
        n2_low = sem("n2_low")
        image_ready = sem("image_ready")
        weight_step, weight5_step = sem("weight_step"), sem("weight5_step")
        conv3_done = sem("conv3_done")
        x3_ready = sem("x3_ready")
        pixels_step = sem("pixels_step")
        reflected = sem("reflected")
        stat_step = sem("stat_step")
        moments_ready = sem("moments_ready")
        moments_summed = sem("moments_summed")
        var3_ready = sem("var3_ready")
        std3_ready = sem("std3_ready")
        rstd3_ready = sem("rstd3_ready")
        const_summed = sem("const_summed")
        const4_ready = sem("const4_ready")
        w5_ready = sem("w5_ready")
        n3_high = sem("n3_high")
        n3_low = sem("n3_low")
        conv5_done = sem("conv5_done")
        x4_ready = sem("x4_ready")
        pe_waited, dve_waited, pool_waited = sem("pe_waited"), sem("dve_waited"), sem("pool_waited")
        x4_stored = [sem(f"x4_stored{n}") for n in range(2)]

        S1 = STEPS + 1
        SPEC_LOADS = 2 * 2 * R
        REFLECTS = STEPS3 // PER3 + 1
        x_rows = x.rearrange("b c (j r) w -> b r c j w", r=R)
        y_rows = y.rearrange("b c (j r) w -> b r c j w", r=R)

        block = own.enter_context(nc.Block())

        @block.sync
        def _(sp):
            sp.dma_start(waves_sb[:], waves).then_inc(tables_loaded, 16)
            for n in range(2):
                sp.dma_start(x4[n][:, 0, 0:2 * M1], waves.bitcast(F32)[:, 0, 0:2 * M1]).then_inc(x4_stored[n], 16)
            with sp.Fori(0, B) as b:
                sp.wait_ge(wave_summed, b * WAVES + 1)
                for n in range(2 * 2):
                    for q in range(R):
                        src = spectrum[b, n // 2, n % 2, C * q:C * (q + 1), :].rearrange("c (g n) -> g c n", g=NKH)
                        sp.dma_start(spec_parts[M1 * n + q:M1 * (n + 1):R], src).then_inc(spec_loaded, 16)
                for k in range(CHUNKS):
                    sp.wait_ge(x2_ready, b * STEPS + (2 + (CHUNK // 2 * (k - 1) if k >= 2 else 0)))
                    at = CHUNK * (k % 2)
                    for r in range(R):
                        sp.dma_start(x0[C * r:C * (r + 1), at:at + CHUNK, :],
                                     x_rows[b, r, :, CHUNK * k:CHUNK * (k + 1), :]).then_inc(x0_loaded[k % 2], 16)

        @block.tensor
        def _(pe):
            def row_dft(b, t):
                pe.wait_ge(wave_low, b * WAVES + t + 1)
                for n in range(2):
                    lhs = spec_parts[:, bass.ds(t * 4 + 2 * n, 2), :].rearrange("p c f -> p (c f)")
                    for part in range(2):
                        last = nc.tensor.matmul(bank[6][:, H * n:H * (n + 1)], lhs, waves_sb[:, part, :],
                                                start=(part == 0), stop=(part == 1))
                last.then_inc(wave_summed, 1)

            def synth(b, s, parity):
                pe.wait_ge(x2_ready, b * STEPS + s + 1)
                for n in range(2):
                    lhs = wave[:, bass.ds(s * (2 * R) + R * n, R), :].rearrange("p y c -> p (y c)")
                    for part in range(2):
                        last = nc.tensor.matmul(bank[4 + parity][:, W * n:W * (n + 1)], lhs, waves_sb[:, part, :],
                                                start=(part == 0), stop=(part == 1))
                last.then_inc(synth_done, 1)

            def conv(patches, src, w, out, row, rows, width):
                todo = [(wh, xh, a, b) for wh, xh in ((0, 0), (1, 0), (0, 1)) for a in range(patches)
                        for b in range(patches)]
                for n, (wh, xh, a, b) in enumerate(todo):
                    last = nc.tensor.matmul(out[:, 0:rows * width], w[:, wh, a, b, :],
                                            src[:, bass.ds(row + a, rows), xh, b:b + width],
                                            start=(n == 0), stop=(n == len(todo) - 1))
                return last

            def conv3_step(b, s, u):
                pe.wait_ge(x3_ready, b * STEPS3 + s + (2 if u == 0 else 1))
                conv(IN3, n2, w3, bank[u % 2], s * ROWS3, ROWS3, OUT3).then_inc(conv3_done, 1)

            def conv3(b, with_next):
                pe.wait_ge(image_ready, b * 3 + 3)
                pe.wait_ge(n2_low, b * STEPS + (STEPS + 2))
                pe.sem_inc(pe_waited, 1)
                with pe.Fori(0, STEPS3 // PER3) as i:
                    for u in range(PER3):
                        conv3_step(b, i * PER3 + u, u)
                        if with_next and u == 2:
                            pe.wait_ge(spec_loaded, b * (16 * SPEC_LOADS) + 32 * SPEC_LOADS)
                            row_dft(b + 1, i)
                if with_next:
                    row_dft(b + 1, WAVES - 1)
                conv3_step(b, STEPS3 - 1, 0)

            def moments(b):
                pe.wait_ge(moments_ready, b + 1)
                nc.tensor.matmul(bank[7][:, 0:2], group_sum[:], moments3[:, 0:2], start=True,
                                 stop=True).then_inc(moments_summed, 1)

            def constant(b):
                pe.wait_ge(rstd3_ready, b + 1)
                nc.tensor.matmul(bank[7][:, 0:1], w5_sum[:], shift3[:], start=True, stop=True).then_inc(const_summed, 1)

            def conv5(b, with_next):
                if with_next:
                    pe.wait_ge(wave_low, (b + 1) * WAVES + (WAVES + 1))
                    synth(b + 1, 0, 0)
                moments(b)
                constant(b)
                pe.wait_ge(w5_ready, b + 1)
                pe.sem_inc(pe_waited, 1)

                def body(i, last_one):
                    for u in range(PER):
                        s = i * PER + u
                        if with_next and not (last_one and u == PER - 1):
                            synth(b + 1, s + 1, (u + 1) % 2)
                        pe.wait_ge(n3_low, b * S1 + s + 4)
                        pe.wait_ge(x4_ready, b * STEPS + s + 1)
                        conv(IN5, n3, w5, bank[2 + u % 2], s * ROWS, ROWS, K).then_inc(conv5_done, 1)

                with pe.Fori(0, STEPS // PER - 1) as i:
                    body(i, False)
                body(STEPS // PER - 1, True)

            pe.sem_inc(wave_summed, 1)
            pe.wait_ge(tables_loaded, 16)
            pe.wait_ge(edges_cleared, 4)
            pe.wait_ge(spec_loaded, 16 * SPEC_LOADS)
            for t in range(WAVES):
                row_dft(0, t)
            pe.wait_ge(wave_low, WAVES + 1)
            with pe.Fori(0, STEPS // PER) as i:
                for u in range(PER):
                    synth(0, i * PER + u, u % 2)
            with pe.Fori(0, B - 1) as b:
                conv3(b, True)
                conv5(b, True)
            conv3(B - 1, False)
            conv5(B - 1, False)

        @block.gpsimd
        def _(pool):
            def columns(b, slot, rows, done):
                pool.wait_ge(x3_ready, b * STEPS3 + done)
                pool.sem_inc(pool_waited, 1)
                for xi, to, at in ((0, 0, 1), (0, N3 - 1, N3 - 3), (1, N3 - 2, N3 - 3), (1, N3 - 1, 1)):
                    half = slice(HALF * xi, HALF * (xi + 1))
                    last = nc.gpsimd.tensor_copy(x3[half, bass.ds(slot, rows), to:to + 1],
                                                 x3[half, bass.ds(slot, rows), at:at + 1])
                return last

            def pixel_rows(todo, count):
                copies = [(yi, xi, to, at) for yi, to, at in todo for xi in range(2)]
                for n, (yi, xi, to, at) in enumerate(copies):
                    pool.wait_ge(pixels_step, count + n)
                    pool.sem_inc(pool_waited, 1)
                    q = slice(C * (2 * xi + yi), C * (2 * xi + yi + 1))
                    nc.gpsimd.tensor_copy(x3[q, to + SHIFT, :], x3[q, at + SHIFT, :]).then_inc(pixels_step, 1)
                pool.wait_ge(pixels_step, count + len(copies))
                pool.sem_inc(reflected, 1)

            nc.gpsimd.memset(n2[:, 1:N2 - 1, :, 0:1], 0.0).then_inc(edges_cleared, 1)
            nc.gpsimd.memset(n2[:, 1:N2 - 1, :, N2 - 1:N2], 0.0).then_inc(edges_cleared, 1)
            nc.gpsimd.memset(n2[:, 0, :, :], 0.0).then_inc(edges_cleared, 1)
            nc.gpsimd.memset(n2[:, N2 - 1, :, :], 0.0).then_inc(edges_cleared, 1)
            LINKS = 2 * 5
            with pool.Fori(0, B) as b:
                PR = PER3 * ROWS3
                columns(b, SHIFT, PR, PER3 + 2).then_inc(pixels_step, 1)
                pixel_rows(((0, 0, 1), (1, N3 - 1, 1)), b * LINKS + 1)
                with pool.Fori(1, STEPS3 // PER3) as i:
                    columns(b, i * PR + SHIFT, PR, i * PER3 + (PER3 + 2)).then_inc(reflected, 1)
                columns(b, PR * (STEPS3 // PER3) + SHIFT, ROWS3, STEPS3 + 2).then_inc(pixels_step, 1)
                pixel_rows(((1, N3 - 2, N3 - 3), (0, N3 - 1, N3 - 3)), b * LINKS + LINKS // 2 + 1)

        @block.scalar
        def _(act):
            def wave_part(b, t):
                act.wait_ge(wave_summed, b * WAVES + t + 2)
                for e in range(2):
                    last = nc.scalar.activation(wave_v[0:HALF, t, e], bank[6][HALF * e:HALF * (e + 1), :].rearrange(
                        "p (n y) -> p n y", n=2), ACT.Copy)
                last.then_inc(wave_high, 1)

            def normalise2(b, s, parity):
                act.wait_ge(x2_ready, b * STEPS + s + 3)
                nc.scalar.activation(n2[:, bass.ds(s * ROWS + 1, ROWS), 0, 1:K + 1], x2[parity][:], ACT.Copy,
                                     scale=rstd2_b[:]).then_inc(n2_high, 1)

            def take_x3(b, with_next):
                act.wait_ge(image_ready, b * 3 + 2)

                def step(s, u):
                    act.wait_ge(conv3_done, b * STEPS3 + s + 1)
                    nc.scalar.activation(x3[:, bass.ds(s * ROWS3 + SHIFT, ROWS3), 0:OUT3],
                                         bank[u % 2][:, 0:ROWS3 * OUT3].rearrange("p (i k) -> p i k", i=ROWS3),
                                         ACT.Identity, bias=bias2_b[:]).then_inc(x3_ready, 1)

                with act.Fori(0, STEPS3 // PER3) as i:
                    for u in range(PER3):
                        step(i * PER3 + u, u)
                        if with_next and u == 3:
                            wave_part(b + 1, i)
                nc.scalar.activation(warm[:], eps[:], ACT.Sqrt)
                if with_next:
                    wave_part(b + 1, WAVES - 1)
                step(STEPS3 - 1, 0)

            def normalise3(b, s, rows=ROWS):
                act.wait_ge(n3_low, b * S1 + s + 1)
                nc.scalar.activation(n3[:, bass.ds(s * ROWS, rows), 0, :], x3[:, bass.ds(s * ROWS + SHIFT, rows), :],
                                     ACT.Copy, scale=rstd3[:]).then_inc(n3_high, 1)

            def take_x4(b, i, u):
                s = i * PER + u
                place = x4[u // 2 % 2]
                act.wait_ge(conv5_done, b * STEPS + s + 1)
                if u % 2 == 0:
                    act.wait_ge(x4_stored[u // 2 % 2], b * (PAIRS // 2 * 64) + (i * (PER // 4 * 64) + (u // 4 * 64 + 16)))
                src = bank[2 + u % 2][:].rearrange("p (j h k) -> p h j k", j=2, h=2)
                for xi in range(2):
                    for h in range(2):
                        last = nc.scalar.activation(
                            place[HALF * h:HALF * (h + 1), 2 * (u % 2):2 * (u % 2) + 2, xi:W:2],
                            src[HALF * xi:HALF * (xi + 1), h], ACT.Identity, bias=const4[HALF * xi:HALF * (xi + 1)])
                last.then_inc(x4_ready, 1)

            def store_x4(b, s, u):
                act.wait_ge(x4_ready, b * STEPS + s + 4)
                for r in range(R):
                    act.dma_start(y_rows[b, r, :, bass.ds(s * 2, 4), :],
                                  x4[u // 2 % 2][C * r:C * (r + 1), :, :]).then_inc(x4_stored[u // 2 % 2], 16)

            def conv5(b, with_next):
                act.wait_ge(var3_ready, b + 1)
                nc.scalar.activation(std3[:], var3[:], ACT.Sqrt, bias=eps[:]).then_inc(std3_ready, 1)
                act.wait_ge(rstd3_ready, b + 1)
                act.wait_ge(reflected, b * REFLECTS + REFLECTS)
                normalise3(b, 0)
                normalise3(b, 1)
                if with_next:
                    normalise2(b + 1, 0, 0)
                act.wait_ge(const4_ready, b + 1)

                def body(i, last_one):
                    for u in range(PER):
                        s = i * PER + u
                        if not last_one or u < PER - 2:
                            normalise3(b, s + 2)
                        elif u == PER - 2:
                            normalise3(b, STEPS, N3 - ROWS * STEPS)
                        if with_next and not (last_one and u == PER - 1):
                            normalise2(b + 1, s + 1, (u + 1) % 2)
                        take_x4(b, i, u)
                        if u % 2 == 1:
                            store_x4(b, s - 1, u - 1)

                with act.Fori(0, STEPS // PER - 1) as i:
                    body(i, False)
                body(STEPS // PER - 1, True)

            act.sem_inc(x3_ready, 2)
            act.sem_inc(x4_ready, 2)
            for t in range(WAVES):
                wave_part(0, t)
            with act.Fori(0, STEPS // 2) as i:
                for u in range(2):
                    normalise2(0, i * 2 + u, u)
            with act.Fori(0, B - 1) as b:
                take_x3(b, True)
                conv5(b, True)
            take_x3(B - 1, False)
            conv5(B - 1, False)
            for n in range(2):
                act.wait_ge(x4_stored[n], 16 + B * (PAIRS // 2) * 64)

        @block.vector
        def _(dve):
            STAT_LINKS = 7

            def image_rstd(b):
                nc.vector.tensor_copy(rstd2_b[:], rstd2[:, bass.ds(b, 1)]).then_inc(image_ready, 1)
                dve.wait_ge(image_ready, b * 3 + 1)

            def image_weights(b):
                nc.vector.tensor_copy(bias2_b[:], bias2[:, bass.ds(b, 1)]).then_inc(image_ready, 1)
                nc.vector.tensor_copy(std2_b[:], std2[:, bass.ds(b, 1)]).then_inc(weight_step, 1)
                dve.wait_ge(weight_step, b * 3 + 1)
                nc.vector.scalar_tensor_tensor(centre3[:].rearrange("p a b m -> p (a b) m"), centre_sb[:], std2_b[:],
                                               w3_centre[:].rearrange("p a b m -> p (a b) m"), ALU.mult,
                                               ALU.add).then_inc(weight_step, 1)
                dve.wait_ge(weight_step, b * 3 + 2)
                nc.vector.tensor_copy(w3[:, 0], centre3[:]).then_inc(weight_step, 1)
                dve.wait_ge(weight_step, b * 3 + 3)
                nc.vector.tensor_tensor(w3[:, 1], centre3[:], w3[:, 0], ALU.subtract).then_inc(image_ready, 1)

            def wave_part(b, t):
                dve.wait_ge(wave_high, b * WAVES + t + 1)
                for e in range(2):
                    last = nc.vector.tensor_tensor(wave_v[HALF:P, t, e], bank[6][HALF * e:HALF * (e + 1), :].rearrange(
                        "p (n y) -> p n y", n=2), wave_v[0:HALF, t, e], ALU.subtract)
                last.then_inc(wave_low, 1)

            def normalise2(b, s, u, chunk=None):
                if chunk is not None:
                    dve.wait_ge(x0_loaded[chunk % 2], b * (CHUNKS // 2 * 16 * R) + (chunk // 2 * (16 * R) + 16 * R))
                dve.wait_ge(synth_done, b * STEPS + s + 1)
                dve.wait_ge(n2_low, b * STEPS + s + 1)
                x2_s = x2[u % 2]
                for xi in range(2):
                    for h in range(2):
                        half = slice(HALF * h, HALF * (h + 1))
                        last = nc.vector.tensor_tensor(
                            x2_s[HALF * xi:HALF * (xi + 1), h:ROWS:2, :],
                            bank[4 + u % 2][half, :].rearrange("p (j w) -> p j w", j=2)[:, :, xi:W:2],
                            x0[half, 2 * u:2 * u + 2, xi:W:2], ALU.add)
                last.then_inc(x2_ready, 1)
                dve.wait_ge(n2_high, b * STEPS + s + 1)
                high_low = n2[:, bass.ds(s * ROWS + 1, ROWS)]
                nc.vector.scalar_tensor_tensor(high_low[:, :, 1, 1:K + 1], x2_s[:], rstd2_b[:],
                                               high_low[:, :, 0, 1:K + 1], ALU.mult, ALU.subtract).then_inc(n2_low, 1)

            def record(out, rows, columns):
                return nc.vector.bn_stats(out, x3[rows, columns[0], columns[1]])

            def late(n):
                return slice(3 + 6 * n, 3 + 6 * (n + 1))

            def statistics(b, with_next):
                inner = slice(1, K)

                def take(g, out):
                    dve.wait_ge(x3_ready, b * STEPS3 + g + 4)
                    return nc.vector.bn_stats(out, x3[:, bass.ds(g * ROWS3 + (1 + SHIFT), ROWS3), inner])

                def edge_row(yi, place, n):
                    for xi in range(2):
                        q = slice(C * (2 * xi + yi), C * (2 * xi + yi + 1))
                        last = nc.vector.bn_stats(records_late[q, late(n)], x3[q, place + SHIFT, 1 - xi:K + 1 - xi])
                    return last

                with dve.Fori(0, EARLY // PER3) as i:
                    for u in range(PER3):
                        g = i * PER3 + u
                        take(g, records_early[:, bass.ds(g, 1), :].rearrange("p n t -> p (n t)"))
                        if with_next and u == 3:
                            wave_part(b + 1, i)
                edge_row(1, 0, PER3).then_inc(stat_step, 1)
                dve.wait_ge(stat_step, b * STAT_LINKS + 1)
                dve.sem_inc(dve_waited, 1)
                nc.vector.bn_aggr(aggregate[:], records_early[:].rearrange("p n t -> p (n t)")).then_inc(stat_step, 1)
                dve.wait_ge(stat_step, b * STAT_LINKS + 2)
                nc.vector.tensor_copy(records_late[:, 1:2], aggregate[:, 0:1])
                nc.vector.tensor_scalar(records_late[:, 2:3], aggregate[:, 1:2], float(EARLY * ROWS3 * (K - 1)), None,
                                        ALU.mult)
                for u in range(PER3):
                    take(EARLY + u, records_late[:, late(u)])
                    if with_next and u in (3, 4):
                        wave_part(b + 1, WAVES - 2 + (u - 3))
                nc.vector.bn_stats(records_late[:, late(PER3 + 1)], x3[:, K - 1 + SHIFT, inner])
                edge_row(0, K, PER3)
                for xi in range(2):
                    half = slice(HALF * xi, HALF * (xi + 1))
                    last = nc.vector.bn_stats(records_late[half, late(PER3 + 2)],
                                              x3[half, 1 + SHIFT:K + SHIFT, (0 if xi else K):(1 if xi else K + 1)]
                                              .rearrange("p i k -> p (i k)"))
                last.then_inc(stat_step, 1)
                dve.wait_ge(stat_step, b * STAT_LINKS + 3)
                dve.sem_inc(dve_waited, 1)
                nc.vector.bn_aggr(moments3[:, 0:2], records_late[:]).then_inc(stat_step, 1)
                dve.wait_ge(stat_step, b * STAT_LINKS + 4)
                nc.vector.scalar_tensor_tensor(moments3[:, 1:2], moments3[:, 0:1], moments3[:, 0:1], moments3[:, 1:2],
                                               ALU.mult, ALU.add).then_inc(moments_ready, 1)
                dve.wait_ge(moments_summed, b + 1)
                nc.vector.tensor_scalar(stats3[:], bank[7][:, 0:2], 1.0 / (GROUP * R), None, ALU.mult).then_inc(stat_step, 1)
                dve.wait_ge(stat_step, b * STAT_LINKS + 5)
                nc.vector.tensor_tensor(moments3[:, 2:3], stats3[:, 0:1], stats3[:, 0:1], ALU.mult).then_inc(stat_step, 1)
                dve.wait_ge(stat_step, b * STAT_LINKS + 6)
                nc.vector.tensor_tensor(var3[:], stats3[:, 1:2], moments3[:, 2:3], ALU.subtract).then_inc(var3_ready, 1)
                dve.wait_ge(std3_ready, b + 1)
                nc.vector.reciprocal(rstd3[:], std3[:]).then_inc(stat_step, 1)
                dve.wait_ge(stat_step, b * STAT_LINKS + 7)
                nc.vector.tensor_tensor(shift3[:], stats3[:, 0:1], rstd3[:], ALU.mult).then_inc(rstd3_ready, 1)

            def weights5(b):
                nc.vector.scalar_tensor_tensor(centre5[:].rearrange("p a b m -> p (a b) m"), centre_sb[:], std3[:],
                                               w5_centre[:].rearrange("p a b m -> p (a b) m"), ALU.mult,
                                               ALU.add).then_inc(weight5_step, 1)
                dve.wait_ge(weight5_step, b * 2 + 1)
                nc.vector.tensor_copy(w5[:, 0, 0:IN3, 0:IN3, :], centre5[:]).then_inc(weight5_step, 1)
                dve.wait_ge(weight5_step, b * 2 + 2)
                nc.vector.tensor_tensor(w5[:, 1, 0:IN3, 0:IN3, :], centre5[:], w5[:, 0, 0:IN3, 0:IN3, :],
                                        ALU.subtract).then_inc(w5_ready, 1)

            def normalise3(b, s, rows=ROWS):
                dve.wait_ge(n3_high, b * S1 + s + 1)
                nc.vector.scalar_tensor_tensor(n3[:, bass.ds(s * ROWS, rows), 1, :],
                                               x3[:, bass.ds(s * ROWS + SHIFT, rows), :], rstd3[:],
                                               n3[:, bass.ds(s * ROWS, rows), 0, :], ALU.mult,
                                               ALU.subtract).then_inc(n3_low, 1)

            def conv5(b, with_next):
                weights5(b)
                normalise3(b, 0)
                normalise3(b, 1)
                dve.wait_ge(const_summed, b + 1)
                nc.vector.tensor_scalar(const4[:], bank[7][:, 0:1], -1.0, None, ALU.mult).then_inc(const4_ready, 1)
                if with_next:
                    image_rstd(b + 1)
                    normalise2(b + 1, 0, 0, chunk=0)

                def body(i, last_one):
                    for u in range(PER):
                        s = i * PER + u
                        if not last_one or u < PER - 2:
                            normalise3(b, s + 2)
                        elif u == PER - 2:
                            normalise3(b, STEPS, N3 - ROWS * STEPS)
                        if with_next and not (last_one and u == PER - 1):
                            normalise2_at(b + 1, i, s + 1, (u + 1) % PER, u)

                def normalise2_at(b, i, s, place, u):
                    if (u + 1) % (CHUNK // 2) == 0:
                        n = (u + 1) // (CHUNK // 2)
                        dve.wait_ge(x0_loaded[n % 2], b * (CHUNKS // 2 * 16 * R) + (i * (16 * R) + (n // 2 + 1) * 16 * R))
                    normalise2(b, s, place)

                with dve.Fori(0, STEPS // PER - 1) as i:
                    body(i, False)
                body(STEPS // PER - 1, True)

            dve.sem_inc(n3_low, 2)
            dve.sem_inc(x2_ready, 2)
            dve.sem_inc(n2_low, 2)
            dve.sem_inc(wave_low, 1)
            nc.vector.memset(records_late[:, 0:1], float(EARLY * ROWS3 * (K - 1)))
            dve.wait_ge(edges_cleared, 4)
            image_rstd(0)
            for t in range(WAVES):
                wave_part(0, t)
            with dve.Fori(0, STEPS // PER) as i:
                for u in range(PER):
                    if u % (CHUNK // 2) == 0:
                        dve.wait_ge(x0_loaded[u // (CHUNK // 2)], i * (16 * R) + 16 * R)
                    normalise2(0, i * PER + u, u)
            image_weights(0)
            with dve.Fori(0, B - 1) as b:
                statistics(b, True)
                conv5(b, True)
                image_weights(b + 1)
            statistics(B - 1, False)
            conv5(B - 1, False)


_TABLES = ["dft_parts", "waves", "same_group", "own_group", "pick", "column0", "centre"]


def kernel(x, L0_conv_weights_real, L0_conv_weights_imag, L1_conv_coeff_real, L1_conv_coeff_imag, L1_conv_proj,
           L2_conv_W, L2_conv_b, L3_conv_weight):
    import concourse.bacc as bacc
    from concourse.bass_utils import run_bass_kernel_spmd

    x = np.ascontiguousarray(x)
    batch = x.shape[0]
    arrays = {
        "x": x,
        "w0r": L0_conv_weights_real, "w0i": L0_conv_weights_imag,
        "coeff_r": L1_conv_coeff_real, "coeff_i": L1_conv_coeff_imag,
        "proj_t": np.asarray(L1_conv_proj).T,
        "w3_t": np.asarray(L2_conv_W).transpose(1, 2, 3, 0),
        "bias3": np.asarray(L2_conv_b).reshape(C, 1),
        "w5_t": np.asarray(L3_conv_weight).transpose(1, 2, 3, 0),
    }
    tables = constants(batch)
    arrays.update({name: tables[name] for name in _TABLES})
    nc = bacc.Bacc("TRN2", target_bir_lowering=False, num_devices=1)
    ins, args = {}, []
    for name, a in arrays.items():
        a = np.ascontiguousarray(a)
        ins[f"{name}_in"] = a
        args.append(nc.dram_tensor(f"{name}_in", a.shape, mybir.dt.from_np(a.dtype), kind="ExternalInput").ap())
    y = nc.dram_tensor("y_out", x.shape, F32, kind="ExternalOutput").ap()
    four_convolutions(nc, batch, *args, y)
    r = run_bass_kernel_spmd(nc, [ins], core_ids=[0])
    return r.results[0]["y_out"]
```

```python
from contextlib import ExitStack

import numpy as np
import concourse.bass as bass
from concourse import mybir

F32 = mybir.dt.float32
F16 = mybir.dt.float16
ALU = mybir.AluOpType
ACT = mybir.ActivationFunctionType
AX = mybir.AxisListType

P = 128
C, H, W = 32, 256, 256
HW = H * W
GROUP = 2
NG = C // GROUP
M0, M1 = 16, 32
R = P // C
NKH = M1 // R
EPS = 1e-5
N_GROUP = GROUP * HW

CH = 8
NCH = C // CH

BLOCKS = H // R
STEPS = BLOCKS // 2
PER = 8
ROWS = 2 * 2
N2 = H // 2 + 2
N3 = H // 2 + 2
OUT3 = H // 2 + 1
ROWS3 = 3
STEPS3 = OUT3 // ROWS3
PER3 = 6
SHIFT = 2 * ROWS
IN3, IN5 = 2, 3
TAPS3, TAPS5 = 3, 5
SPEC_LOADS = 2 * 2 * R
WAVES = C // 4


def constants(batch):
    f64 = np.float64
    a = 2 * np.pi * np.outer(np.arange(H), np.arange(M1)).astype(f64) / H
    cs, sn = np.cos(a), np.sin(a)
    dft = np.stack([np.concatenate([cs, -sn], 1), np.concatenate([sn, cs], 1)])
    split = lambda t: (t.astype(np.float16), (t - t.astype(np.float16).astype(f64)).astype(np.float16))
    dft_parts = np.stack(split(dft), 1).reshape(2, 2, 2, P, 2 * M1).transpose(3, 0, 1, 2, 4)
    wave = np.concatenate([cs, -sn], 1).T
    hi, lo = split(wave)
    waves = np.stack([np.concatenate([hi, hi]), np.concatenate([lo, lo])], 1)
    p = np.arange(P)
    ch, q = p % C, p // C
    same_group = (ch[:, None] // GROUP == ch[None, :] // GROUP).astype(np.float32)
    own_group = (ch[:, None] // GROUP == np.arange(NG)[None, :]).astype(np.float32)
    pick = np.zeros((P, 2, 2 * C), np.float32)
    pick[p, 0, ch] = 1
    pick[p, 1, C + ch] = 1
    column0 = np.full((P, NKH, 2), 0.5, np.float32)
    column0[q == 0, 0, 0] = 1
    column0[q == 0, 0, 1] = 0
    centre = np.zeros((P, IN3 * IN3, P), np.float32)
    own_pixel = [(0, 1, 0), (1, 0, 1)]
    for a, yi, yo in own_pixel:
        for b, xi, xo in own_pixel:
            centre[(2 * xi + yi) * C + np.arange(C), IN3 * a + b, (2 * xo + yo) * C + np.arange(C)] = 1
    return {"dft_parts": dft_parts, "waves": waves, "same_group": same_group,
            "own_group": own_group, "pick": pick, "column0": column0, "centre": centre}


def splits(batch):
    return [range(b, min(batch, b + 4)) for b in range(0, batch, 4)]


def store_spectra(sp, images, spectrum, delta_parts, turned_parts, written):
    for b in images:
        for part, src in enumerate((delta_parts, turned_parts)):
            sp.dma_start(spectrum[b, :, part].rearrange("s p n -> p s n"),
                         src[:, :, NKH * b:NKH * (b + 1)].rearrange("p s g r f -> p s (g r f)")).then_inc(written, 16)


def load_spectrum(sp, image, spec_parts, spec_loaded):
    for n in range(2 * 2):
        for q in range(R):
            src = image[n // 2, n % 2, C * q:C * (q + 1), :].rearrange("c (g n) -> g c n", g=NKH)
            sp.dma_start(spec_parts[M1 * n + q:M1 * (n + 1):R], src).then_inc(spec_loaded, 16)


def four_convolutions(nc, B, x, w0r, w0i, coeff_r, coeff_i, proj_t, w3_t, bias3, w5_t,
                      dft_parts, waves, same_group, own_group, pick, column0, centre, y):
    spectrum = nc.dram_tensor("spectrum_dram", (B, 2, 2, P, NKH * 2 * M1), F16, kind="Internal").ap()

    keep = ExitStack()
    with keep:
        def sb(name, shape, dt=F32, at=keep):
            return at.enter_context(nc.sbuf_tensor(name, shape, dt))

        def sem(name, at=keep):
            return at.enter_context(nc.semaphore(name))

        bank = [keep.enter_context(nc.psum_tensor(f"bank{n}", [P, 512], F32)) for n in range(8)]
        std2 = sb("std2", [P, B])
        rstd2 = sb("rstd2", [P, B])
        bias2 = sb("bias2", [P, B])
        group_sum = sb("group_sum", [P, P])
        centre_sb = sb("centre_sb", [P, IN3 * IN3, P])
        w3 = sb("w3", [P, 2, IN3, IN3, P], F16)
        w5 = sb("w5", [P, 2, IN5, IN5, P], F16)
        w3_centre = sb("w3_centre", [P, IN3, IN3, P])
        w5_centre = sb("w5_centre", [P, IN3, IN3, P])
        w5_sum = sb("w5_sum", [P, P])
        eps = sb("eps", [P, 1])
        waves_sb = sb("waves_sb", [P, 2, W], F16)
        spec_parts = sb("spec_parts", [P, C, 2 * M1], F16)
        spec_loaded = sem("spec_loaded")
        waves_loaded = sem("waves_loaded")
        written = [sem(f"spectra_written{k}") for k in range(len(splits(B)))]

        early = ExitStack()
        spec = sb("spec", [P, B, NKH, 2, M1], at=early)
        squares = sb("squares", [P, B, NG], at=early)
        records = sb("records", [P, B, NCH + NCH // 2, 2 * 2, 3], at=early)
        analysis(nc, B, x, dft_parts, spec, squares, records, bank)
        spectrum_parts = mixing(nc, B, w0r, w0i, coeff_r, coeff_i, proj_t, w3_t, bias3, w5_t, same_group, own_group,
                                pick, column0, centre, spectrum, spec, squares, records, bank, std2, rstd2, bias2,
                                group_sum, centre_sb, w3, w5, w3_centre, w5_centre, w5_sum, eps, waves, waves_sb,
                                waves_loaded, spec_parts, spec_loaded, written)
        early.close()
        spatial(nc, B, x, waves, spectrum, y, bank, std2, rstd2, bias2, group_sum, centre_sb, w3, w5, w3_centre,
                w5_centre, w5_sum, eps, waves_sb, waves_loaded, spec_parts, spec_loaded, written, *spectrum_parts)


def analysis(nc, B, x, dft_parts, spec, squares, records, bank):
    own = ExitStack()
    with own:
        def sb(name, shape, dt=F32):
            return own.enter_context(nc.sbuf_tensor(name, shape, dt))

        def sem(name):
            return own.enter_context(nc.semaphore(name))

        CHG = CH // GROUP
        tile = [sb(f"x_chunk{k}", [P, 2, CH, W]) for k in range(NCH)]
        parts = [sb(f"x_parts{k}", [P, 2, 2, CH, W], F16) for k in range(NCH)]
        half_dft = sb("half_dft", [P, 2, 2, 2, M1, C], F16)
        t_parts = sb("t_parts", [P, 2, 2, 2, 2 * M1], F16)
        x_squared = [sb(f"x_squared{n}", [P, 2, GROUP * W], mybir.dt.bfloat16) for n in range(CHG - 1)]

        tables_loaded = sem("tables_loaded")
        chunk_loaded = [sem(f"chunk_loaded{k}") for k in range(NCH)]
        rows_done = sem("rows_done")
        high_ready = sem("high_ready")
        pool_high_ready = sem("pool_high_ready")
        pool_low_ready = sem("pool_low_ready")
        low_ready = sem("low_ready")
        records_ready = sem("records_ready")
        squares_ready = sem("squares_ready")
        rows_high = sem("rows_high")
        rows_low = sem("rows_low")
        cols_done = sem("cols_done")
        cols_copied = sem("cols_copied")
        pool_waited = sem("analysis_pool_waited")

        POOL_CH = GROUP

        def channels(v, first, end):
            return v[:, :, first:end, :].rearrange("p h c x -> p h (c x)")

        def recorded(k):
            return [(CHG - 1, k)] + ([(CHG - 2, NCH + k // 2)] if k % 2 else [])

        def rows_out(k, part, xh):
            return half_dft[:, part, xh, :, :, CH * k:CH * (k + 1)].rearrange("p r f c -> p c (r f)")

        def rows_in(k, xh):
            return bank[2 * (k % 2) + xh][:, :].rearrange("p (c f) -> p c f", c=CH)

        block = own.enter_context(nc.Block())

        @block.sync
        def _(sp):
            sp.dma_start(t_parts[:], dft_parts).then_inc(tables_loaded, 16)
            with sp.Fori(0, B) as b:
                for k in range(NCH):
                    sp.wait_ge(squares_ready, b * NCH + (k + 1))
                    sp.wait_ge(records_ready, b * NCH + (k + 1))
                    sp.wait_ge(pool_low_ready, b * NCH + (k + 1))
                    for h in range(2):
                        src = x[b, CH * k:CH * (k + 1), P * h:P * (h + 1), :].rearrange("c y x -> y c x")
                        sp.dma_start(tile[k][:, h], src).then_inc(chunk_loaded[k], 16)

        @block.tensor
        def _(pe):
            pe.sem_inc(rows_done, NCH)
            pe.sem_inc(cols_done, 1)
            pe.wait_ge(tables_loaded, 16)

            def image(b, first):
                for k in range(NCH):
                    pe.wait_ge(low_ready, b * NCH + (k + 1))
                    pe.wait_ge(pool_low_ready, b * NCH + (NCH + k + 1))
                    pe.wait_ge(rows_low, b * NCH + (k + 1))
                    for c in range(CH):
                        for xh in range(2):
                            out = bank[2 * (k % 2) + xh][:, 2 * M1 * c:2 * M1 * (c + 1)]
                            todo = [(yh, xp, tp) for yh in range(2) for xp, tp in ((0, 0), (0, 1), (1, 0))]
                            for n, (yh, xp, tp) in enumerate(todo):
                                last = nc.tensor.matmul(out, parts[k][:, xp, yh, c, P * xh:P * (xh + 1)],
                                                        t_parts[:, 0, tp, yh, :], start=(n == 0),
                                                        stop=(n == len(todo) - 1))
                    last.then_inc(rows_done, 1)
                    if k == 0 and not first:
                        columns(b - 1)

            def columns(b):
                pe.wait_ge(rows_low, b * NCH + (2 + NCH))
                pe.wait_ge(cols_copied, b + 1)
                for g in range(NKH):
                    out = bank[4][:, 2 * M1 * g:2 * M1 * (g + 1)]
                    todo = [(xh, r, hp, tp) for xh in range(2) for r in range(2) for hp, tp in ((0, 0), (0, 1), (1, 0))]
                    for n, (xh, r, hp, tp) in enumerate(todo):
                        last = nc.tensor.matmul(out, half_dft[:, hp, xh, r, R * g:R * (g + 1), :],
                                                t_parts[:, r, tp, xh, :], start=(n == 0), stop=(n == len(todo) - 1))
                last.then_inc(cols_done, 1)

            image(0, True)
            with pe.Fori(1, B) as b:
                image(b, False)
            columns(B - 1)

        @block.gpsimd
        def _(pool):
            pool.sem_inc(pool_low_ready, NCH)
            with pool.Fori(0, B) as b:
                for k in range(NCH):
                    pool.wait_ge(chunk_loaded[k], b * 32 + 32)
                    pool.wait_ge(rows_done, b * NCH + (k + 1))
                    pool.sem_inc(pool_waited, 1)
                    nc.gpsimd.tensor_copy(channels(parts[k][:, 0], CH - POOL_CH, CH),
                                          channels(tile[k], CH - POOL_CH, CH)).then_inc(pool_high_ready, 1)
                    pool.wait_ge(pool_high_ready, b * NCH + (k + 1))
                    nc.gpsimd.tensor_tensor(*(channels(v, CH - POOL_CH, CH) for v in (
                        parts[k][:, 1], tile[k], parts[k][:, 0])), ALU.subtract).then_inc(pool_low_ready, 1)

        @block.scalar
        def _(act):
            act.sem_inc(cols_copied, 1)
            act.sem_inc(squares_ready, NCH)

            def take_rows(b, k):
                act.wait_ge(rows_done, b * NCH + (NCH + k + 1))
                for xh in range(2):
                    last = nc.scalar.activation(rows_out(k, 0, xh), rows_in(k, xh), ACT.Copy)
                last.then_inc(rows_high, 1)

            def take_spectrum(b):
                act.wait_ge(cols_done, b + 2)
                nc.scalar.activation(spec[:, b, :, :, :].rearrange("p g r f -> p (g r f)"), bank[4][:, :],
                                     ACT.Copy).then_inc(cols_copied, 1)

            def high(b, k):
                act.wait_ge(chunk_loaded[k], b * 32 + 32)
                act.wait_ge(rows_done, b * NCH + (k + 1))
                nc.scalar.activation(channels(parts[k][:, 0], 0, CH - POOL_CH), channels(tile[k], 0, CH - POOL_CH),
                                     ACT.Copy).then_inc(high_ready, 1)

            def image(b, first):
                for k in range(NCH):
                    if k != 2:
                        high(b, k)
                    if k == 1:
                        high(b, 2)
                    act.wait_ge(squares_ready, b * NCH + (NCH + k))
                    for g in range(CHG - len(recorded(k))):
                        last = nc.scalar.activation(
                            x_squared[g][:], channels(tile[k], GROUP * g, GROUP * (g + 1)),
                            ACT.Square, accum_out=squares[:, b, CHG * k + g:CHG * k + g + 1])
                    last.then_inc(squares_ready, 1)
                    if k == 1 and not first:
                        take_spectrum(b - 1)
                    if k:
                        take_rows(b, k - 1)
                    elif not first:
                        take_rows(b - 1, NCH - 1)

            image(0, True)
            with act.Fori(1, B) as b:
                image(b, False)
            take_rows(B - 1, NCH - 1)
            take_spectrum(B - 1)

        @block.vector
        def _(dve):
            dve.sem_inc(records_ready, NCH)
            dve.sem_inc(rows_low, 2)

            def take_rows(b, k):
                dve.wait_ge(rows_high, b * NCH + (k + 1))
                for xh in range(2):
                    last = nc.vector.tensor_tensor(rows_out(k, 1, xh), rows_in(k, xh), rows_out(k, 0, xh), ALU.subtract)
                last.then_inc(rows_low, 1)

            def image(b, first):
                for k in range(NCH):
                    dve.wait_ge(high_ready, b * NCH + (k + 1))
                    dve.wait_ge(pool_high_ready, b * NCH + (k + 1))
                    nc.vector.tensor_tensor(*(channels(v, 0, CH - POOL_CH) for v in (
                        parts[k][:, 1], tile[k], parts[k][:, 0])), ALU.subtract).then_inc(low_ready, 1)
                    for g, n in recorded(k):
                        for h in range(2):
                            last = nc.vector.bn_stats(
                                records[:, b, n, 2 * h:2 * h + 2, :].rearrange("p n t -> p (n t)"),
                                tile[k][:, h, GROUP * g:GROUP * (g + 1), :].rearrange("p c x -> p (c x)"))
                    last.then_inc(records_ready, 1)
                    if k:
                        take_rows(b, k - 1)
                    elif not first:
                        take_rows(b - 1, NCH - 1)

            image(0, True)
            with dve.Fori(1, B) as b:
                image(b, False)
            take_rows(B - 1, NCH - 1)


def mixing(nc, B, w0r, w0i, coeff_r, coeff_i, proj_t, w3_t, bias3, w5_t, same_group, own_group, pick, column0, centre,
           spectrum, spec, squares, records, bank, std2, rstd2, bias2, group_sum, centre_sb, w3, w5, w3_centre,
           w5_centre, w5_sum, eps, waves, waves_sb, waves_loaded, spec_parts, spec_loaded, written):
    own = ExitStack()
    with own:
        def sb(name, shape, dt=F32):
            return own.enter_context(nc.sbuf_tensor(name, shape, dt))

        def sem(name):
            return own.enter_context(nc.semaphore(name))

        HF = M1 // 2
        SHRINK = 1.0 / 256
        diagonal = [sb(f"diagonal{n}", [P, 2, 2, M1, P], F16) for n in range(2)]
        delta = sb("delta", [P, B, NKH, 2, M1])
        coeff = [sb(f"coeff{n}", [P, 2, C, M1]) for n in range(2)]
        normal = sb("normal", [P, 2, B, M1])
        normal_parts = [sb(f"normal_parts{n}", [P, 2, 3, B, M1], F16) for n in range(2)]
        ranks = spec_parts[:].rearrange("p c f -> p (c f)").bitcast(F32)[:, 0:2 * HF * 2 * B].rearrange(
            "p (h n) -> p h n", h=2)
        mixed = [sb(f"mixed{n}", [P, B, 2, M1]) for n in range(2)]
        w0 = diagonal[1][0:2 * C].rearrange("p n h f m -> p (n h f m)").bitcast(F32).rearrange(
            "p (o f c) -> p o f c", o=C, f=M0)
        low = [mixed[n][:].rearrange("p b r f -> p (b r f)")[:, 0:B * 2 * M0].rearrange(
            "p (b r f) -> p b r f", b=B, r=2) for n in range(2)]
        low_s = sb("low_s", [2 * C, M0, 2, B])
        proj = sb("proj", [P, P])
        pick_sb = sb("pick_sb", [P, 2, 2 * C])
        own_group_sb = sb("own_group_sb", [P, NG])
        column0_sb = sb("column0_sb", [P, 2 * NKH])
        ones = sb("ones", [P, P])
        moment2 = sb("moment2", [P, B, NCH + NCH // 2, 4])
        masked = sb("masked", [P, B, NG])
        mean_square = sb("mean_square", [P, B])
        energy = sb("energy", [P, 3, B])
        ends = sb("ends", [P, 2, B])
        mean, var, std, rstd, total, tmp, dc0, dc1, dc1c = (sb(n, [P, B]) for n in (
            "mean", "var", "std", "rstd", "total", "tmp", "dc0", "dc1", "dc1c"))
        junk = sb("junk", [P, NKH * 2 * M1], mybir.dt.bfloat16)
        t3 = w3_centre
        delta_parts = spec[:].bitcast(F16).rearrange("p b g r f -> p (b g r f)").rearrange(
            "p (s b r f) -> p s b r f", s=2, b=B * NKH, r=2)
        turned_parts = diagonal[0][:].rearrange("p n s f m -> p (n s f m)")[:, 0:B * 4 * NKH * M1].rearrange(
            "p (s b r f) -> p s b r f", s=2, b=B * NKH, r=2)
        delta_v = delta[:].rearrange("p b g r f -> p (b g) r f")
        t5 = sb("t5", [P, IN5, IN5, P])
        bias_sb = sb("bias_sb", [P, 1])
        DC = slice(0, C)

        tables_loaded = sem("mix_tables_loaded")
        toeplitz_cleared = sem("toeplitz_cleared")
        toeplitz_loaded = sem("toeplitz_loaded")
        toeplitz_split = sem("toeplitz_split")
        cleared = sem("cleared")
        proj_cleared = sem("proj_cleared")
        proj_loaded = sem("proj_loaded")
        coeff_loaded = [sem(f"coeff_loaded{n}") for n in range(2)]
        coeff_high = sem("coeff_high")
        coeff_low = sem("coeff_low")
        normal_ready = sem("normal_ready")
        normal_high = sem("normal_high")
        normal_low = sem("normal_low")
        product_done = sem("product_done")
        ranks_copied = sem("ranks_copied")
        proj_done = sem("proj_done")
        mixed_copied = sem("mixed_copied")
        mixed_ready = sem("mixed_ready")
        mixed_added = sem("mixed_added")
        dve_step = sem("mix_dve_step")
        squares_ready = sem("squares_ready")
        moments_summed = sem("moments_summed")
        variance_ready = sem("variance_ready")
        root_ready = sem("root_ready")
        centred = sem("centred")
        energy_ready = sem("energy_ready")
        low_ready = sem("low_ready")
        low_summed = sem("low_summed")
        low_copied = sem("low_copied")
        layer0_done = sem("layer0_done")
        ends_ready = sem("ends_ready")
        ends_summed = sem("ends_summed")
        layer0_read = sem("layer0_read")
        pe_waited = sem("mix_pe_waited")
        delta_ready = sem("delta_ready")
        split_high = sem("split_high")
        split_low = sem("split_low")
        turned_low = sem("turned_low")

        def taps(n):
            for a in range(IN3 if n == TAPS3 else IN5):
                for i in range(2):
                    for o in range(2):
                        d = 2 * a + i - o
                        if 0 <= d < n:
                            yield a, i, o, d if n == TAPS3 else n - 1 - d

        N_TAPS = sum(len(list(taps(t))) ** 2 for t in (TAPS3, TAPS5))
        N_TABLES = 7 + R

        block = own.enter_context(nc.Block())

        @block.sync
        def _(sp):
            def load_coefficients(g):
                for part in range(2):
                    for q in range(R):
                        src = (coeff_r, coeff_i)[part][:, :, R * g + q, :].rearrange("r c f -> c r f")
                        sp.dma_start(coeff[g % 2][C * q:C * (q + 1), part], src).then_inc(coeff_loaded[g % 2], 16)

            for dst, src in ((group_sum[:], same_group), (pick_sb[:], pick), (own_group_sb[:], own_group),
                             (column0_sb[:], column0.rearrange("p g r -> p (g r)")), (centre_sb[:], centre)):
                sp.dma_start(dst, src).then_inc(tables_loaded, 16)
            sp.wait_ge(proj_cleared, 1)
            for q in range(R):
                sp.dma_start(proj[C * q:C * (q + 1), C * q:C * (q + 1)], proj_t).then_inc(proj_loaded, 16)
            for part in range(2):
                sp.dma_start(w0[C * part:C * (part + 1)], (w0r, w0i)[part]).then_inc(tables_loaded, 16)
            for r in range(R):
                sp.dma_start(bias_sb[C * r:C * (r + 1), :], bias3).then_inc(tables_loaded, 16)
            for g in range(2):
                load_coefficients(g)
            sp.dma_start(waves_sb[:], waves).then_inc(waves_loaded, 16)
            sp.wait_ge(toeplitz_cleared, 2)
            for dst, src, n in ((t3, w3_t, TAPS3), (t5, w5_t, TAPS5)):
                for a, yi, yo, ty in taps(n):
                    for b, xi, xo, tx in taps(n):
                        i, o = C * (2 * xi + yi), C * (2 * xo + yo)
                        sp.dma_start(dst[i:i + C, a, b, o:o + C], src[:, ty, tx, :]).then_inc(toeplitz_loaded, 16)
            for g in range(2, NKH):
                sp.wait_ge(coeff_high, g - 1)
                sp.wait_ge(coeff_low, g - 1)
                load_coefficients(g)
            sp.wait_ge(split_high, 3)
            sp.wait_ge(turned_low, 1)
            store_spectra(sp, splits(B)[0], spectrum, delta_parts, turned_parts, written[0])
            sp.wait_ge(written[0], 32 * len(splits(B)[0]))
            load_spectrum(sp, spectrum[0], spec_parts, spec_loaded)

        @block.tensor
        def _(pe):
            pe.wait_ge(tables_loaded, 16 * N_TABLES)
            pe.wait_ge(cleared, 1)
            pe.wait_ge(squares_ready, 1)
            nc.tensor.matmul(bank[0][:, 0:B * NG], ones[:], squares[:].rearrange("p b g -> p (b g)"), start=True,
                             stop=True)
            nc.tensor.matmul(bank[1][:, 0:B], group_sum[:], ends[:, 1], start=True,
                             stop=True).then_inc(moments_summed, 1)
            pe.wait_ge(low_ready, 1)
            for part in range(2):
                last = nc.tensor.matmul(bank[1][0:2 * C, 0:M0 * 2 * B], pick_sb[:, part, :],
                                        low[part].rearrange("p b r f -> p f r b"),
                                        start=(part == 0), stop=(part == 1))
            last.then_inc(low_summed, 1)
            pe.wait_ge(low_copied, 1)
            for f in range(M0):
                q = f % R
                for c in range(M0):
                    last = nc.tensor.matmul(bank[4 + f // R][C * q:C * (q + 1), 2 * B * c:2 * B * (c + 1)],
                                            w0[:, :, f, c], low_s[:, f, :, :].rearrange("p r b -> p (r b)"),
                                            start=True, stop=True)
            last.then_inc(layer0_done, 1)
            pe.wait_ge(ends_ready, 1)
            nc.tensor.matmul(bank[0][:, 0:2 * B], group_sum[:], ends[:].rearrange("p k b -> p (k b)"),
                             start=True, stop=True).then_inc(ends_summed, 1)

            pe.sem_inc(ranks_copied, 2)
            pe.sem_inc(mixed_copied, 1)
            pe.wait_ge(layer0_read, 1)
            pe.wait_ge(proj_loaded, 16 * R)
            pe.sem_inc(pe_waited, 1)
            with pe.Fori(0, NKH // 2) as i:
                for n in range(2):
                    g = i * 2 + n
                    pe.wait_ge(coeff_low, g + 1)
                    pe.wait_ge(normal_low, g + 1)
                    pe.wait_ge(ranks_copied, g + 1)
                    for f in range(M1):
                        todo = [(part, cp, xp) for part in range(2) for cp, xp in ((0, 0), (0, 1), (1, 0))]
                        for k, (part, cp, xp) in enumerate(todo):
                            last = nc.tensor.matmul(
                                bank[2 + 2 * n + f // HF][:, 2 * B * (f % HF):2 * B * (f % HF + 1)],
                                diagonal[n][:, part, cp, f, :], normal_parts[n][:, xp, 1 - part:3 - part, :, f],
                                start=(k == 0), stop=(k == len(todo) - 1))
                    last.then_inc(product_done, 1)
                    pe.wait_ge(ranks_copied, g + 3)
                    pe.wait_ge(mixed_copied, g + 1)
                    for half in range(2):
                        last = nc.tensor.matmul(bank[6 + half][:, 0:HF * 2 * B], proj[:], ranks[:, half, :],
                                                start=True, stop=True)
                    last.then_inc(proj_done, 1)
            pe.wait_ge(ends_ready, 2)
            nc.tensor.matmul(bank[0][:, 0:2 * B], group_sum[:], ends[:].rearrange("p k b -> p (k b)"),
                             start=True, stop=True).then_inc(ends_summed, 1)

        @block.gpsimd
        def _(pool):
            nc.gpsimd.memset(t3[:], 0.0).then_inc(toeplitz_cleared, 1)
            nc.gpsimd.memset(t5[:], 0.0).then_inc(toeplitz_cleared, 1)
            nc.gpsimd.memset(proj[:], 0.0).then_inc(proj_cleared, 1)
            nc.gpsimd.memset(ones[:], 1.0 / N_GROUP).then_inc(cleared, 1)

            nc.gpsimd.memset(diagonal[0][:].bitcast(F32), 0.0).then_inc(cleared, 1)
            pool.wait_ge(layer0_done, 1)
            nc.gpsimd.memset(diagonal[1][:].bitcast(F32), 0.0).then_inc(cleared, 1)
            pool.wait_ge(toeplitz_loaded, 16 * N_TAPS)
            pool.wait_ge(tables_loaded, 16 * N_TABLES)
            nc.gpsimd.tensor_copy(w5[:, 0], t5[:]).then_inc(toeplitz_split, 1)
            nc.gpsimd.tensor_copy(w5_centre[:], t5[:, 0:IN3, 0:IN3, :]).then_inc(toeplitz_split, 1)
            pool.wait_ge(toeplitz_split, 2)
            nc.gpsimd.tensor_tensor(w5[:, 1], t5[:], w5[:, 0], ALU.subtract).then_inc(toeplitz_split, 1)
            for g in range(NKH):
                pool.wait_ge(mixed_copied, g + 2)
                column = mixed[g % 2][:, :, :, 0]
                nc.gpsimd.tensor_tensor(column, column, column0_sb[:, None, 2 * g:2 * g + 2].to_broadcast([P, B, 2]),
                                        ALU.mult).then_inc(mixed_ready, 1)
                pool.wait_ge(mixed_ready, g + 1)
                for dst in (spec, delta):
                    part = dst[:, :, g]
                    nc.gpsimd.tensor_tensor(part, part, mixed[g % 2][:], ALU.add).then_inc(mixed_added, 1)

        @block.scalar
        def _(act):
            def energies(k):
                act.wait_ge(centred, k + 1)
                for b in range(B):
                    if B * k + b:
                        act.wait_ge(energy_ready, B * k + b)
                    nc.scalar.activation(junk[:], spec[:, b].rearrange("p g r f -> p (g r f)"), ACT.Square,
                                         accum_out=energy[:, k, b:b + 1]).then_inc(energy_ready, 1)

            def root(k, out):
                act.wait_ge(variance_ready, k + 1)
                nc.scalar.activation(out[:], var[:], ACT.Sqrt, bias=eps[:]).then_inc(root_ready, 1)

            root(0, std)
            energies(0)
            act.wait_ge(low_summed, 1)
            nc.scalar.activation(low_s[:].rearrange("p f r b -> p (f r b)"), bank[1][0:2 * C, 0:M0 * 2 * B],
                                 ACT.Copy).then_inc(low_copied, 1)
            def coefficients_high(g):
                if g >= 2:
                    act.wait_ge(product_done, g - 1)
                act.wait_ge(coeff_loaded[g % 2], 128 * (g // 2 + 1))
                for part in range(2):
                    for q in range(R):
                        rows = slice(C * q, C * (q + 1))
                        last = nc.scalar.activation(diagonal[g % 2][rows, part, 0, :, rows],
                                                    coeff[g % 2][rows, part].rearrange("p r f -> p f r"), ACT.Copy)
                last.then_inc(coeff_high, 1)

            act.wait_ge(cleared, 2)
            coefficients_high(0)
            energies(1)
            root(1, std)
            def normal_high_part(g):
                if g >= 2:
                    act.wait_ge(product_done, g - 1)
                act.wait_ge(normal_ready, g + 1)
                nc.scalar.activation(normal_parts[g % 2][:, 0, 1:3].rearrange("p r b f -> p (r b f)"),
                                     normal[:].rearrange("p r b f -> p (r b f)"), ACT.Copy)
                nc.scalar.activation(normal_parts[g % 2][:, 0, 0], normal[:, 1], ACT.Copy,
                                     scale=-1.0).then_inc(normal_high, 1)

            normal_high_part(0)
            act.wait_ge(cleared, 3)
            coefficients_high(1)
            for g in range(NKH):
                if g + 1 < NKH:
                    normal_high_part(g + 1)
                act.wait_ge(product_done, g + 1)
                for half in range(2):
                    last = nc.scalar.activation(ranks[:, half, :], bank[2 + 2 * (g % 2) + half][:, 0:HF * 2 * B],
                                                ACT.Copy, scale=1.0 / SHRINK)
                last.then_inc(ranks_copied, 1)
                if g + 2 < NKH:
                    coefficients_high(g + 2)
                if g >= 2:
                    act.wait_ge(mixed_added, 2 * (g - 1))
                act.wait_ge(proj_done, g + 1)
                for half in range(2):
                    last = nc.scalar.activation(
                        mixed[g % 2][:, :, :, HF * half:HF * (half + 1)].rearrange("p b r f -> p f r b"),
                        bank[6 + half][:, 0:HF * 2 * B].rearrange("p (f r b) -> p f r b", f=HF, r=2), ACT.Copy)
                last.then_inc(mixed_copied, 1)
            energies(2)
            root(2, std2)
            act.wait_ge(delta_ready, 1)
            for k, images in enumerate(splits(B)):
                at = slice(NKH * images[0], NKH * (images[-1] + 1))
                flat = lambda v: v.rearrange("p b r f -> p (b r f)")
                nc.scalar.activation(flat(delta_parts[:, 0, at]), flat(delta_v[:, at]), ACT.Copy,
                                     scale=2.0 / HW).then_inc(split_high, 1)
                for r in range(2):
                    nc.scalar.activation(turned_parts[:, 0, at, r, :], delta_v[:, at, 1 - r, :], ACT.Copy,
                                         scale=(-2.0 if r else 2.0) / HW).then_inc(split_high, 1)

        @block.vector
        def _(dve):
            chain = [0]

            def link(ins):
                chain[0] += 1
                ins.then_inc(dve_step, 1)
                dve.wait_ge(dve_step, chain[0])

            def put(out, a, b, op):
                link(nc.vector.tensor_tensor(out, a, b, op))

            def scale(out, a, k, op=ALU.mult):
                link(nc.vector.tensor_scalar(out, a, k, None, op))

            def axpy(out, a, k, b):
                link(nc.vector.scalar_tensor_tensor(out, a, k, b, ALU.mult, ALU.add))

            def over_images(t, n):
                return t[:, :, None].to_broadcast([P, B, n])

            spec_dc = spec[DC, :, 0, 0, 0]
            link(nc.vector.memset(delta[:], 0.0))
            link(nc.vector.memset(eps[:], EPS))
            link(nc.vector.memset(ends[:], 0.0))
            rec_mean, rec_var = (records[:, :, :, :, n].rearrange("p b k e -> p (b k e)") for n in (1, 2))
            flat = moment2[:].rearrange("p b k e -> p (b k e)")
            put(flat, rec_mean, rec_mean, ALU.mult)
            axpy(flat, flat, float(W), rec_var)
            CHG = CH // GROUP
            link(nc.vector.tensor_reduce(squares[:].rearrange("p b (k g) -> p b k g", k=NCH)[:, :, :, CHG - 1],
                                         moment2[:, :, 0:NCH], AX.X, ALU.add))
            link(nc.vector.tensor_reduce(squares[:].rearrange("p b (k g) -> p b k g", k=NCH // 2)[:, :, :, 2 * CHG - 2],
                                         moment2[:, :, NCH:], AX.X, ALU.add))
            link(nc.vector.tensor_copy(ends[DC, 1], spec_dc))
            dve.sem_inc(squares_ready, 1)
            dve.wait_ge(moments_summed, 1)
            dve.wait_ge(tables_loaded, 16 * N_TABLES)
            put(masked[:], bank[0][:, 0:B * NG].rearrange("p (b g) -> p b g", g=NG),
                own_group_sb[:, None, :].to_broadcast([P, B, NG]), ALU.mult)
            link(nc.vector.tensor_reduce(mean_square[:], masked[:], AX.X, ALU.add))
            scale(mean[:], bank[1][:, 0:B], 1.0 / N_GROUP)
            m0, q0 = mean[:], mean_square[:]
            put(tmp[:], m0, m0, ALU.mult)
            put(var[:], q0, tmp[:], ALU.subtract)
            dve.sem_inc(variance_ready, 1)
            axpy(spec_dc, m0[DC], -float(HW), spec_dc)
            dve.sem_inc(centred, 1)
            link(nc.vector.tensor_copy(dc0[DC], spec_dc))
            link(nc.vector.tensor_copy(total[:], m0))
            dve.wait_ge(root_ready, 1)
            link(nc.vector.reciprocal(rstd[:], std[:]))
            g_low = [spec[:, :, g, :, 0:M0] for g in range(M0 // R)]
            low0, low1 = low
            put(low0, g_low[0], g_low[1], ALU.add)
            for g in g_low[2:]:
                put(low0, low0, g, ALU.add)
            for r in range(2):
                put(low0[:, :, r, :], low0[:, :, r, :], over_images(rstd, M0), ALU.mult)
            scale(low1[:, :, 0, :], low0[:, :, 1, :], -1.0)
            link(nc.vector.tensor_copy(low1[:, :, 1, :], low0[:, :, 0, :]))
            dve.sem_inc(low_ready, 1)
            dve.wait_ge(layer0_done, 1)
            dve.wait_ge(energy_ready, B)
            for g in range(M0 // R):
                link(nc.vector.tensor_copy(delta[:, :, g, :, 0:M0].rearrange("p b r f -> p f r b"),
                                           bank[4 + g][:, 0:M0 * 2 * B].rearrange("p (f r b) -> p f r b", f=M0, r=2)))
            n_low = 2 * M0 // R
            column = delta[:].rearrange("p b g r f -> p b (g r) f")[:, :, 0:n_low, 0]
            put(column, column, column0_sb[:, None, 0:n_low].to_broadcast([P, B, n_low]), ALU.mult)
            for g in range(M0 // R):
                put(g_low[g], g_low[g], delta[:, :, g, :, 0:M0], ALU.add)
            dve.sem_inc(layer0_read, 1)
            dve.sem_inc(centred, 1)
            link(nc.vector.tensor_copy(dc1[DC], spec_dc))

            def change(k, dc_old2, dc_old, dc_new):
                dve.wait_ge(energy_ready, B * (k + 1))
                put(tmp[:], energy[:, k], energy[:, k - 1], ALU.subtract)
                scale(ends[:, 0], tmp[:], 2.0)
                for dc, factor in ((dc_old2, 2.0), (dc_old, -1.0), (dc_new, -1.0)):
                    put(tmp[DC], dc, dc, ALU.mult)
                    axpy(ends[DC, 0], tmp[DC], factor, ends[DC, 0])
                link(nc.vector.tensor_copy(ends[DC, 1], dc_new))
                dve.sem_inc(ends_ready, 1)
                dve.wait_ge(ends_summed, k)
                scale(mean[:], bank[0][:, B:2 * B], 1.0 / N_GROUP)
                axpy(var[:], bank[0][:, 0:B], 1.0 / HW / N_GROUP, var[:])
                put(tmp[:], mean[:], mean[:], ALU.mult)
                put(var[:], var[:], tmp[:], ALU.subtract)
                dve.sem_inc(variance_ready, 1)
                put(total[:], total[:], mean[:], ALU.add)

            def coefficients_low(g):
                dve.wait_ge(coeff_loaded[g % 2], 128 * (g // 2 + 1))
                dve.wait_ge(coeff_high, g + 1)
                for part in range(2):
                    for q in range(R):
                        rows = slice(C * q, C * (q + 1))
                        last = nc.vector.tensor_tensor(diagonal[g % 2][rows, part, 1, :, rows],
                                                       coeff[g % 2][rows, part].rearrange("p r f -> p f r"),
                                                       diagonal[g % 2][rows, part, 0, :, rows], ALU.subtract)
                last.then_inc(coeff_low, 1)

            coefficients_low(0)
            change(1, dc0[DC], dc0[DC], dc1[DC])
            axpy(spec_dc, mean[DC], -float(HW), spec_dc)
            link(nc.vector.tensor_copy(dc1c[DC], spec_dc))
            dve.wait_ge(root_ready, 2)
            link(nc.vector.reciprocal(rstd[:], std[:]))

            scale(rstd[:], rstd[:], SHRINK)

            def normalise(g):
                if g >= 1:
                    dve.wait_ge(normal_high, g)
                put(normal[:].rearrange("p r b f -> p b r f"), spec[:, :, g], rstd[:, :, None, None].to_broadcast(
                    [P, B, 2, M1]), ALU.mult)
                dve.sem_inc(normal_ready, 1)

            def normal_low_part(g):
                dve.wait_ge(normal_high, g + 1)
                high, low_ = normal_parts[g % 2][:, 0], normal_parts[g % 2][:, 1]
                put(low_[:, 1:3].rearrange("p r b f -> p (r b f)"), normal[:].rearrange("p r b f -> p (r b f)"),
                    high[:, 1:3].rearrange("p r b f -> p (r b f)"), ALU.subtract)
                nc.vector.tensor_scalar(low_[:, 0], low_[:, 2], -1.0, None, ALU.mult).then_inc(normal_low, 1)

            for g in range(NKH):
                normalise(g)
                if g >= 1:
                    coefficients_low(g)
                normal_low_part(g)
            dve.wait_ge(toeplitz_loaded, 16 * N_TAPS)
            link(nc.vector.tensor_reduce(w5_sum[:], t5[:].rearrange("p k t m -> p m (k t)"), AX.X, ALU.add))
            dve.wait_ge(mixed_added, 2 * NKH)
            dve.sem_inc(centred, 1)
            change(2, dc1[DC], dc1c[DC], spec_dc)
            dve.wait_ge(root_ready, 3)
            link(nc.vector.reciprocal(rstd2[:], std2[:]))
            scale(bias2[:], total[:], bias_sb[:], ALU.add)
            axpy(delta[DC, :, 0, 0, 0], total[DC], -float(HW), delta[DC, :, 0, 0, 0])
            scale(delta[DC, :, 0, 0, 0], delta[DC, :, 0, 0, 0], 0.5)
            dve.sem_inc(delta_ready, 1)
            for k, images in enumerate(splits(B)):
                at = slice(NKH * images[0], NKH * (images[-1] + 1))
                flat = lambda v: v.rearrange("p b r f -> p (b r f)")
                dve.wait_ge(split_high, 3 * k + 1)
                nc.vector.scalar_tensor_tensor(flat(delta_parts[:, 1, at]), flat(delta_v[:, at]), 2.0 / HW,
                                               flat(delta_parts[:, 0, at]), ALU.mult,
                                               ALU.subtract).then_inc(split_low, 1)
                dve.wait_ge(split_low, k + 1)
                nc.vector.tensor_copy(turned_parts[:, 1, at, 0, :], delta_parts[:, 1, at, 1, :])
                nc.vector.tensor_scalar(turned_parts[:, 1, at, 1, :], delta_parts[:, 1, at, 0, :], -1.0, None,
                                        ALU.mult).then_inc(turned_low, 1)

    return delta_parts, turned_parts


def spatial(nc, B, x, waves, spectrum, y, bank, std2, rstd2, bias2, group_sum, centre_sb, w3, w5, w3_centre,
            w5_centre, w5_sum, eps, waves_sb, waves_loaded, spec_parts, spec_loaded, written,
            delta_parts, turned_parts):
    own = ExitStack()
    with own:
        def sb(name, shape, dt=F32):
            return own.enter_context(nc.sbuf_tensor(name, shape, dt))

        def sem(name):
            return own.enter_context(nc.semaphore(name))

        RING = 2 * PER
        CHUNK = RING // 2
        CHUNKS = BLOCKS // CHUNK
        PER_CHUNK = CHUNK // 2
        PAIRS = STEPS // 2
        HALF = P // 2
        K = H // 2
        EARLY = STEPS3 - 1 - PER3
        LATE = PER3 + 3

        x3 = sb("x3", [P, N3 + SHIFT, N3])
        x0 = sb("x0", [P, RING, W])
        x2 = [sb(f"x2_{n}", [P, ROWS, K]) for n in range(2)]
        n2 = sb("n2", [P, N2, 2, N2], F16)
        n3 = x3[:].bitcast(F16).rearrange("p i (h k) -> p i h k", h=2)
        x4 = [sb(f"x4_{n}", [P, 4, W]) for n in range(2)]
        wave = sb("wave", [P, H, C], F16)
        wave_v = wave[:].rearrange("p y (t n e) -> p t e n y", n=2, e=2)
        records_early = sb("records_early", [P, EARLY, 6])
        records_late = sb("records_late", [P, 3 + LATE * 6])
        aggregate = sb("aggregate", [P, 2])
        moments3 = sb("moments3", [P, 3])
        centre3, centre5 = sb("centre3", [P, IN3, IN3, P]), sb("centre5", [P, IN3, IN3, P])
        stats3 = sb("stats3", [P, 2])
        var3, std3, rstd3, shift3, const4, warm = (sb(n, [P, 1]) for n in (
            "var3", "std3", "rstd3", "shift3", "const4", "warm"))
        std2_b, rstd2_b, bias2_b = (sb(n, [P, 1]) for n in ("std2_b", "rstd2_b", "bias2_b"))

        edges_cleared = sem("edges_cleared")
        x0_loaded = [sem(f"x0_loaded{n}") for n in range(2)]
        wave_summed = sem("wave_summed")
        wave_high = sem("wave_high")
        wave_low = sem("wave_low")
        synth_done = sem("synth_done")
        x2_ready = sem("x2_ready")
        n2_high = sem("n2_high")
        n2_low = sem("n2_low")
        image_ready = sem("image_ready")
        weight_step = sem("weight_step")
        centre5_ready = sem("centre5_ready")
        w5_high = sem("w5_high")
        conv3_done = sem("conv3_done")
        x3_ready = sem("x3_ready")
        pixels_step = sem("pixels_step")
        reflected = sem("reflected")
        stat_step = sem("stat_step")
        moments_ready = sem("moments_ready")
        moments_summed = sem("moments_summed")
        var3_ready = sem("var3_ready")
        std3_ready = sem("std3_ready")
        rstd3_ready = sem("rstd3_ready")
        const_summed = sem("const_summed")
        const4_ready = sem("const4_ready")
        w5_ready = sem("w5_ready")
        n3_high = sem("n3_high")
        n3_low = sem("n3_low")
        conv5_done = sem("conv5_done")
        x4_ready = sem("x4_ready")
        pe_waited, dve_waited, pool_waited = sem("pe_waited"), sem("dve_waited"), sem("pool_waited")
        x4_stored = [sem(f"x4_stored{n}") for n in range(2)]

        S1 = STEPS + 1
        BANKS3 = [u % 2 for u in range(PER3)] + [7]
        X0_LOADS = CHUNKS // 2 * 16 * R
        REFLECTS = STEPS3 // PER3 + 1
        x_rows = x.rearrange("b c (j r) w -> b r c j w", r=R)
        y_rows = y.rearrange("b c (j r) w -> b r c j w", r=R)

        def wave_bank(t, banks):
            return bank[6 if banks == 1 else 6 + t % 2]

        block = own.enter_context(nc.Block())

        @block.sync
        def _(sp):
            for n in range(2):
                sp.dma_start(x4[n][:, 0, 0:2 * M1], waves.bitcast(F32)[:, 0, 0:2 * M1]).then_inc(x4_stored[n], 16)

            def load_parts(b):
                sp.wait_ge(wave_summed, b * WAVES + 1)
                load_spectrum(sp, spectrum[b], spec_parts, spec_loaded)

            def load_x0(b, k, half):
                for r in range(R):
                    sp.dma_start(x0[C * r:C * (r + 1), CHUNK * half:CHUNK * (half + 1), :],
                                 x_rows[b, r, :, bass.ds(k * CHUNK, CHUNK), :]).then_inc(x0_loaded[half], 16)

            def load_next_x0(b, k, half):
                sp.wait_ge(x2_ready, b * STEPS + (k * PER_CHUNK + (2 - PER_CHUNK)))
                load_x0(b, k, half)

            def store_x4(b, s, n):
                sp.wait_ge(x4_ready, b * STEPS + s + 4)
                for r in range(R):
                    sp.dma_start(y_rows[b, r, :, bass.ds(s * 2, 4), :],
                                 x4[n][C * r:C * (r + 1), :, :]).then_inc(x4_stored[n], 16)

            def image(b, with_next, with_second):
                if with_next:
                    for n in range(2):
                        load_next_x0(b + 1, n, n)
                if with_second:
                    load_parts(b + 2)

                def body(i, last_one):
                    for n in range(2):
                        for m in range(2):
                            store_x4(b, i * PER + (n * PER_CHUNK + 2 * m), m)
                        if with_next and not last_one:
                            load_next_x0(b + 1, i * 2 + (n + 2), n)

                with sp.Fori(0, STEPS // PER - 1) as i:
                    body(i, False)
                body(STEPS // PER - 1, True)

            for k in range(CHUNKS):
                if k < 2:
                    load_x0(0, k, k)
                else:
                    load_next_x0(0, k, k % 2)
                if 1 <= k < len(written):
                    store_spectra(sp, splits(B)[k], spectrum, delta_parts, turned_parts, written[k])
            for k, images in enumerate(splits(B)):
                sp.wait_ge(written[k], 32 * len(images))
            load_parts(1)
            with sp.Fori(0, B - 2) as b:
                image(b, True, True)
            image(B - 2, True, False)
            image(B - 1, False, False)
            for n in range(2):
                sp.wait_ge(x4_stored[n], 16 + B * (PAIRS // 2) * 64)

        @block.tensor
        def _(pe):
            def row_dft(b, t, banks=1):
                pe.wait_ge(wave_low, b * WAVES + t + 1 if banks == 1 else max(1, t))
                for n in range(2):
                    lhs = spec_parts[:, bass.ds(t * 4 + 2 * n, 2), :].rearrange("p c f -> p (c f)")
                    for part in range(2):
                        last = nc.tensor.matmul(wave_bank(t, banks)[:, H * n:H * (n + 1)], lhs, waves_sb[:, part, :],
                                                start=(part == 0), stop=(part == 1))
                last.then_inc(wave_summed, 1)

            def synth(b, s, parity):
                pe.wait_ge(x2_ready, b * STEPS + s + 1)
                for n in range(2):
                    lhs = wave[:, bass.ds(s * (2 * R) + R * n, R), :].rearrange("p y c -> p (y c)")
                    for part in range(2):
                        last = nc.tensor.matmul(bank[4 + parity][:, W * n:W * (n + 1)], lhs, waves_sb[:, part, :],
                                                start=(part == 0), stop=(part == 1))
                last.then_inc(synth_done, 1)

            def conv(patches, src, w, out, row, rows, width, before_part=None):
                todo = [(wh, xh, a, b) for wh, xh in ((0, 0), (1, 0), (0, 1)) for a in range(patches)
                        for b in range(patches)]
                for n, (wh, xh, a, b) in enumerate(todo):
                    if before_part and n % (patches * patches) == 0:
                        before_part(n // (patches * patches))
                    last = nc.tensor.matmul(out[:, 0:rows * width], w[:, wh, a, b, :],
                                            src[:, bass.ds(row + a, rows), xh, b:b + width],
                                            start=(n == 0), stop=(n == len(todo) - 1))
                return last

            def conv3_step(b, s, u):
                pe.wait_ge(x3_ready, b * STEPS3 + s + 1)
                conv(IN3, n2, w3, bank[BANKS3[u]], s * ROWS3, ROWS3, OUT3).then_inc(conv3_done, 1)

            def conv3(b, with_next):
                pe.wait_ge(image_ready, b * 3 + 3)
                pe.wait_ge(n2_low, b * STEPS + (STEPS + 2))
                pe.sem_inc(pe_waited, 1)
                if with_next:
                    pe.wait_ge(spec_loaded, b * (16 * SPEC_LOADS) + 32 * SPEC_LOADS)
                    row_dft(b + 1, 0)
                with pe.Fori(0, STEPS3 // PER3) as i:
                    for u in range(PER3):
                        conv3_step(b, i * PER3 + u, u)
                        if with_next and u == 1:
                            row_dft(b + 1, i + 1)
                conv3_step(b, STEPS3 - 1, PER3)

            def moments(b):
                pe.wait_ge(moments_ready, b + 1)
                nc.tensor.matmul(bank[7][:, 0:2], group_sum[:], moments3[:, 0:2], start=True,
                                 stop=True).then_inc(moments_summed, 1)

            def constant(b):
                pe.wait_ge(rstd3_ready, b + 1)
                nc.tensor.matmul(bank[7][:, 0:1], w5_sum[:], shift3[:], start=True, stop=True).then_inc(const_summed, 1)

            def conv5(b, with_next):
                if with_next:
                    pe.wait_ge(wave_low, (b + 1) * WAVES + (WAVES + 1))
                    synth(b + 1, 0, 0)
                moments(b)
                constant(b)
                pe.wait_ge(w5_high, b + 1)
                pe.sem_inc(pe_waited, 1)

                def body(i, last_one):
                    for u in range(PER):
                        s = i * PER + u
                        if with_next and not (last_one and u == PER - 1):
                            synth(b + 1, s + 1, (u + 1) % 2)

                        def before_part(n):
                            if n == 0:
                                pe.wait_ge(x4_ready, b * STEPS + s + 1)
                                pe.wait_ge(n3_high, b * S1 + s + 2)
                            elif n == 1 and u == 0:
                                pe.wait_ge(w5_ready, b + 1)
                            elif n == 2:
                                pe.wait_ge(n3_low, b * S1 + s + 4)

                        conv(IN5, n3, w5, bank[2 + u % 2], s * ROWS, ROWS, K, before_part).then_inc(conv5_done, 1)

                with pe.Fori(0, STEPS // PER - 1) as i:
                    body(i, False)
                body(STEPS // PER - 1, True)

            pe.sem_inc(wave_summed, 1)
            pe.wait_ge(waves_loaded, 16)
            pe.wait_ge(edges_cleared, 4)
            pe.wait_ge(spec_loaded, 16 * SPEC_LOADS)
            for t in range(WAVES):
                row_dft(0, t, 2)
            pe.wait_ge(wave_low, WAVES + 1)
            with pe.Fori(0, STEPS // PER) as i:
                for u in range(PER):
                    synth(0, i * PER + u, u % 2)
            with pe.Fori(0, B - 1) as b:
                conv3(b, True)
                conv5(b, True)
            conv3(B - 1, False)
            conv5(B - 1, False)

        @block.gpsimd
        def _(pool):
            def columns(b, slot, rows, done):
                pool.wait_ge(x3_ready, b * STEPS3 + done)
                pool.sem_inc(pool_waited, 1)
                for xi, to, at in ((0, 0, 1), (0, N3 - 1, N3 - 3), (1, N3 - 2, N3 - 3), (1, N3 - 1, 1)):
                    half = slice(HALF * xi, HALF * (xi + 1))
                    last = nc.gpsimd.tensor_copy(x3[half, bass.ds(slot, rows), to:to + 1],
                                                 x3[half, bass.ds(slot, rows), at:at + 1])
                return last

            def pixel_rows(todo, count):
                copies = [(yi, xi, to, at) for yi, to, at in todo for xi in range(2)]
                for n, (yi, xi, to, at) in enumerate(copies):
                    pool.wait_ge(pixels_step, count + n)
                    pool.sem_inc(pool_waited, 1)
                    q = slice(C * (2 * xi + yi), C * (2 * xi + yi + 1))
                    nc.gpsimd.tensor_copy(x3[q, to + SHIFT, :], x3[q, at + SHIFT, :]).then_inc(pixels_step, 1)
                pool.wait_ge(pixels_step, count + len(copies))
                pool.sem_inc(reflected, 1)

            nc.gpsimd.memset(n2[:, 1:N2 - 1, :, 0:1], 0.0).then_inc(edges_cleared, 1)
            nc.gpsimd.memset(n2[:, 1:N2 - 1, :, N2 - 1:N2], 0.0).then_inc(edges_cleared, 1)
            nc.gpsimd.memset(n2[:, 0, :, :], 0.0).then_inc(edges_cleared, 1)
            nc.gpsimd.memset(n2[:, N2 - 1, :, :], 0.0).then_inc(edges_cleared, 1)
            LINKS = 2 * 5
            with pool.Fori(0, B) as b:
                PR = PER3 * ROWS3
                columns(b, SHIFT, PR, PER3 + 2).then_inc(pixels_step, 1)
                pixel_rows(((0, 0, 1), (1, N3 - 1, 1)), b * LINKS + 1)
                with pool.Fori(1, STEPS3 // PER3) as i:
                    columns(b, i * PR + SHIFT, PR, i * PER3 + (PER3 + 2)).then_inc(reflected, 1)
                columns(b, PR * (STEPS3 // PER3) + SHIFT, ROWS3, STEPS3 + 2).then_inc(pixels_step, 1)
                pixel_rows(((1, N3 - 2, N3 - 3), (0, N3 - 1, N3 - 3)), b * LINKS + LINKS // 2 + 1)

        @block.scalar
        def _(act):
            def wave_part(b, t, banks=1):
                act.wait_ge(wave_summed, b * WAVES + t + 2)
                for e in range(2):
                    src = wave_bank(t, banks)[HALF * e:HALF * (e + 1), :].rearrange("p (n y) -> p n y", n=2)
                    last = nc.scalar.activation(wave_v[0:HALF, t, e], src, ACT.Copy)
                last.then_inc(wave_high, 1)

            def normalise2(b, s, parity):
                act.wait_ge(x2_ready, b * STEPS + s + 3)
                nc.scalar.activation(n2[:, bass.ds(s * ROWS + 1, ROWS), 0, 1:K + 1], x2[parity][:], ACT.Copy,
                                     scale=rstd2_b[:]).then_inc(n2_high, 1)

            def take_x3(b, with_next):
                act.wait_ge(image_ready, b * 3 + 2)

                def step(s, u):
                    act.wait_ge(conv3_done, b * STEPS3 + s + 1)
                    nc.scalar.activation(x3[:, bass.ds(s * ROWS3 + SHIFT, ROWS3), 0:OUT3],
                                         bank[BANKS3[u]][:, 0:ROWS3 * OUT3].rearrange("p (i k) -> p i k", i=ROWS3),
                                         ACT.Identity, bias=bias2_b[:]).then_inc(x3_ready, 1)

                if with_next:
                    wave_part(b + 1, 0)
                with act.Fori(0, STEPS3 // PER3) as i:
                    for u in range(PER3):
                        step(i * PER3 + u, u)
                        if with_next and u == 2:
                            wave_part(b + 1, i + 1)
                nc.scalar.activation(warm[:], eps[:], ACT.Sqrt)
                step(STEPS3 - 1, PER3)

            def normalise3(b, s, rows=ROWS):
                act.wait_ge(n3_low, b * S1 + s + 1)
                nc.scalar.activation(n3[:, bass.ds(s * ROWS, rows), 0, :], x3[:, bass.ds(s * ROWS + SHIFT, rows), :],
                                     ACT.Copy, scale=rstd3[:]).then_inc(n3_high, 1)

            def take_x4(b, i, u):
                s = i * PER + u
                place = x4[u // 2 % 2]
                act.wait_ge(conv5_done, b * STEPS + s + 1)
                if u % 2 == 0:
                    act.wait_ge(x4_stored[u // 2 % 2],
                                b * (PAIRS // 2 * 64) + (i * (PER // 4 * 64) + (u // 4 * 64 + 16)))
                src = bank[2 + u % 2][:].rearrange("p (j h k) -> p h j k", j=2, h=2)
                for xi in range(2):
                    for h in range(2):
                        last = nc.scalar.activation(
                            place[HALF * h:HALF * (h + 1), 2 * (u % 2):2 * (u % 2) + 2, xi:W:2],
                            src[HALF * xi:HALF * (xi + 1), h], ACT.Identity, bias=const4[HALF * xi:HALF * (xi + 1)])
                last.then_inc(x4_ready, 1)

            def conv5(b, with_next):
                act.wait_ge(var3_ready, b + 1)
                nc.scalar.activation(std3[:], var3[:], ACT.Sqrt, bias=eps[:]).then_inc(std3_ready, 1)
                act.wait_ge(rstd3_ready, b + 1)
                act.wait_ge(reflected, b * REFLECTS + REFLECTS)
                normalise3(b, 0)
                act.wait_ge(centre5_ready, b + 1)
                nc.scalar.activation(w5[:, 0, 0:IN3, 0:IN3, :], centre5[:], ACT.Copy).then_inc(w5_high, 1)
                normalise3(b, 1)
                if with_next:
                    normalise2(b + 1, 0, 0)
                act.wait_ge(const4_ready, b + 1)

                def body(i, last_one):
                    for u in range(PER):
                        s = i * PER + u
                        if not last_one or u < PER - 2:
                            normalise3(b, s + 2)
                        elif u == PER - 2:
                            normalise3(b, STEPS, N3 - ROWS * STEPS)
                        if with_next and not (last_one and u == PER - 1):
                            normalise2(b + 1, s + 1, (u + 1) % 2)
                        take_x4(b, i, u)

                with act.Fori(0, STEPS // PER - 1) as i:
                    body(i, False)
                body(STEPS // PER - 1, True)

            act.sem_inc(x3_ready, 2)
            act.sem_inc(x4_ready, 2)
            for t in range(WAVES):
                wave_part(0, t, 2)
            with act.Fori(0, STEPS // 2) as i:
                for u in range(2):
                    normalise2(0, i * 2 + u, u)
            for k, images in enumerate(splits(B)):
                act.wait_ge(written[k], 32 * len(images))
            with act.Fori(0, B - 1) as b:
                take_x3(b, True)
                conv5(b, True)
            take_x3(B - 1, False)
            conv5(B - 1, False)

        @block.vector
        def _(dve):
            STAT_LINKS = 7

            def image_rstd(b):
                nc.vector.tensor_copy(rstd2_b[:], rstd2[:, bass.ds(b, 1)]).then_inc(image_ready, 1)
                dve.wait_ge(image_ready, b * 3 + 1)

            def image_weights(b):
                nc.vector.tensor_copy(bias2_b[:], bias2[:, bass.ds(b, 1)]).then_inc(image_ready, 1)
                nc.vector.tensor_copy(std2_b[:], std2[:, bass.ds(b, 1)]).then_inc(weight_step, 1)
                dve.wait_ge(weight_step, b * 3 + 1)
                nc.vector.scalar_tensor_tensor(centre3[:].rearrange("p a b m -> p (a b) m"), centre_sb[:], std2_b[:],
                                               w3_centre[:].rearrange("p a b m -> p (a b) m"), ALU.mult,
                                               ALU.add).then_inc(weight_step, 1)
                dve.wait_ge(weight_step, b * 3 + 2)
                nc.vector.tensor_copy(w3[:, 0], centre3[:]).then_inc(weight_step, 1)
                dve.wait_ge(weight_step, b * 3 + 3)
                nc.vector.tensor_tensor(w3[:, 1], centre3[:], w3[:, 0], ALU.subtract).then_inc(image_ready, 1)

            def wave_part(b, t, banks=1):
                dve.wait_ge(wave_high, b * WAVES + t + 1)
                for e in range(2):
                    src = wave_bank(t, banks)[HALF * e:HALF * (e + 1), :].rearrange("p (n y) -> p n y", n=2)
                    last = nc.vector.tensor_tensor(wave_v[HALF:P, t, e], src, wave_v[0:HALF, t, e], ALU.subtract)
                last.then_inc(wave_low, 1)

            def take_synth(b, s, u):
                dve.wait_ge(synth_done, b * STEPS + s + 1)
                dve.wait_ge(n2_low, b * STEPS + s + 1)
                for xi in range(2):
                    for h in range(2):
                        half = slice(HALF * h, HALF * (h + 1))
                        last = nc.vector.tensor_tensor(
                            x2[u % 2][HALF * xi:HALF * (xi + 1), h:ROWS:2, :],
                            bank[4 + u % 2][half, :].rearrange("p (j w) -> p j w", j=2)[:, :, xi:W:2],
                            x0[half, 2 * u:2 * u + 2, xi:W:2], ALU.add)
                last.then_inc(x2_ready, 1)

            def normalise2(b, s, u):
                dve.wait_ge(n2_high, b * STEPS + s + 1)
                high_low = n2[:, bass.ds(s * ROWS + 1, ROWS)]
                nc.vector.scalar_tensor_tensor(high_low[:, :, 1, 1:K + 1], x2[u % 2][:], rstd2_b[:],
                                               high_low[:, :, 0, 1:K + 1], ALU.mult, ALU.subtract).then_inc(n2_low, 1)

            def late(n):
                return slice(3 + 6 * n, 3 + 6 * (n + 1))

            def statistics(b, with_next):
                inner = slice(1, K)

                def take(g, out):
                    dve.wait_ge(x3_ready, b * STEPS3 + g + 4)
                    return nc.vector.bn_stats(out, x3[:, bass.ds(g * ROWS3 + (1 + SHIFT), ROWS3), inner])

                def edge_row(yi, place, n):
                    for xi in range(2):
                        q = slice(C * (2 * xi + yi), C * (2 * xi + yi + 1))
                        last = nc.vector.bn_stats(records_late[q, late(n)], x3[q, place + SHIFT, 1 - xi:K + 1 - xi])
                    return last

                if with_next:
                    wave_part(b + 1, 0)
                with dve.Fori(0, EARLY // PER3) as i:
                    for u in range(PER3):
                        g = i * PER3 + u
                        take(g, records_early[:, bass.ds(g, 1), :].rearrange("p n t -> p (n t)"))
                        if with_next and u == 2:
                            wave_part(b + 1, i + 1)
                edge_row(1, 0, PER3).then_inc(stat_step, 1)
                dve.wait_ge(stat_step, b * STAT_LINKS + 1)
                dve.sem_inc(dve_waited, 1)
                nc.vector.bn_aggr(aggregate[:], records_early[:].rearrange("p n t -> p (n t)")).then_inc(stat_step, 1)
                dve.wait_ge(stat_step, b * STAT_LINKS + 2)
                nc.vector.tensor_copy(records_late[:, 1:2], aggregate[:, 0:1])
                nc.vector.tensor_scalar(records_late[:, 2:3], aggregate[:, 1:2], float(EARLY * ROWS3 * (K - 1)), None,
                                        ALU.mult)
                for u in range(PER3):
                    take(EARLY + u, records_late[:, late(u)])
                    if with_next and u == 2:
                        wave_part(b + 1, WAVES - 1)
                nc.vector.bn_stats(records_late[:, late(PER3 + 1)], x3[:, K - 1 + SHIFT, inner])
                edge_row(0, K, PER3)
                for xi in range(2):
                    half = slice(HALF * xi, HALF * (xi + 1))
                    last = nc.vector.bn_stats(records_late[half, late(PER3 + 2)],
                                              x3[half, 1 + SHIFT:K + SHIFT, (0 if xi else K):(1 if xi else K + 1)]
                                              .rearrange("p i k -> p (i k)"))
                last.then_inc(stat_step, 1)
                dve.wait_ge(stat_step, b * STAT_LINKS + 3)
                dve.sem_inc(dve_waited, 1)
                nc.vector.bn_aggr(moments3[:, 0:2], records_late[:]).then_inc(stat_step, 1)
                dve.wait_ge(stat_step, b * STAT_LINKS + 4)
                nc.vector.scalar_tensor_tensor(moments3[:, 1:2], moments3[:, 0:1], moments3[:, 0:1], moments3[:, 1:2],
                                               ALU.mult, ALU.add).then_inc(moments_ready, 1)
                dve.wait_ge(moments_summed, b + 1)
                nc.vector.tensor_scalar(stats3[:], bank[7][:, 0:2], 1.0 / (GROUP * R), None,
                                        ALU.mult).then_inc(stat_step, 1)
                dve.wait_ge(stat_step, b * STAT_LINKS + 5)
                nc.vector.tensor_tensor(moments3[:, 2:3], stats3[:, 0:1], stats3[:, 0:1],
                                        ALU.mult).then_inc(stat_step, 1)
                dve.wait_ge(stat_step, b * STAT_LINKS + 6)
                nc.vector.tensor_tensor(var3[:], stats3[:, 1:2], moments3[:, 2:3], ALU.subtract).then_inc(var3_ready, 1)
                dve.wait_ge(std3_ready, b + 1)
                nc.vector.reciprocal(rstd3[:], std3[:]).then_inc(stat_step, 1)
                dve.wait_ge(stat_step, b * STAT_LINKS + 7)
                nc.vector.tensor_tensor(shift3[:], stats3[:, 0:1], rstd3[:], ALU.mult).then_inc(rstd3_ready, 1)

            def weights5(b):
                nc.vector.scalar_tensor_tensor(centre5[:].rearrange("p a b m -> p (a b) m"), centre_sb[:], std3[:],
                                               w5_centre[:].rearrange("p a b m -> p (a b) m"), ALU.mult,
                                               ALU.add).then_inc(centre5_ready, 1)
                normalise3(b, 0)
                dve.wait_ge(w5_high, b + 1)
                nc.vector.tensor_tensor(w5[:, 1, 0:IN3, 0:IN3, :], centre5[:], w5[:, 0, 0:IN3, 0:IN3, :],
                                        ALU.subtract).then_inc(w5_ready, 1)

            def normalise3(b, s, rows=ROWS):
                dve.wait_ge(n3_high, b * S1 + s + 1)
                nc.vector.scalar_tensor_tensor(n3[:, bass.ds(s * ROWS, rows), 1, :],
                                               x3[:, bass.ds(s * ROWS + SHIFT, rows), :], rstd3[:],
                                               n3[:, bass.ds(s * ROWS, rows), 0, :], ALU.mult,
                                               ALU.subtract).then_inc(n3_low, 1)

            def conv5(b, with_next):
                weights5(b)
                normalise3(b, 1)
                dve.wait_ge(const_summed, b + 1)
                nc.vector.tensor_scalar(const4[:], bank[7][:, 0:1], -1.0, None, ALU.mult).then_inc(const4_ready, 1)
                if with_next:
                    image_rstd(b + 1)
                    dve.wait_ge(x0_loaded[0], (b + 1) * X0_LOADS + 16 * R)
                    take_synth(b + 1, 0, 0)
                    normalise2(b + 1, 0, 0)

                def body(i, last_one):
                    for u in range(PER):
                        s = i * PER + u
                        synth = with_next and not (last_one and u == PER - 1)
                        if synth:
                            if (u + 1) % PER_CHUNK == 0:
                                n = (u + 1) // PER_CHUNK
                                dve.wait_ge(x0_loaded[n % 2],
                                            (b + 1) * X0_LOADS + (i * (16 * R) + (n // 2 + 1) * 16 * R))
                            take_synth(b + 1, s + 1, (u + 1) % PER)
                        if not last_one or u < PER - 2:
                            normalise3(b, s + 2)
                        elif u == PER - 2:
                            normalise3(b, STEPS, N3 - ROWS * STEPS)
                        if synth:
                            normalise2(b + 1, s + 1, u + 1)

                with dve.Fori(0, STEPS // PER - 1) as i:
                    body(i, False)
                body(STEPS // PER - 1, True)

            dve.sem_inc(n3_low, 2)
            dve.sem_inc(x2_ready, 2)
            dve.sem_inc(n2_low, 2)
            dve.sem_inc(wave_low, 1)
            nc.vector.memset(records_late[:, 0:1], float(EARLY * ROWS3 * (K - 1)))
            dve.wait_ge(edges_cleared, 4)
            image_rstd(0)
            image_weights(0)
            for t in range(WAVES):
                wave_part(0, t, 2)
            dve.wait_ge(x0_loaded[0], 16 * R)
            take_synth(0, 0, 0)

            def first_image(i, last_one):
                for u in range(PER):
                    s = i * PER + u
                    if not (last_one and u == PER - 1):
                        if (u + 1) % PER_CHUNK == 0:
                            n = (u + 1) // PER_CHUNK
                            dve.wait_ge(x0_loaded[n % 2], i * (16 * R) + (n // 2 + 1) * 16 * R)
                        take_synth(0, s + 1, (u + 1) % PER)
                    normalise2(0, s, u)

            with dve.Fori(0, STEPS // PER - 1) as i:
                first_image(i, False)
            first_image(STEPS // PER - 1, True)
            with dve.Fori(0, B - 1) as b:
                statistics(b, True)
                conv5(b, True)
                image_weights(b + 1)
            statistics(B - 1, False)
            conv5(B - 1, False)


_TABLES = ["dft_parts", "waves", "same_group", "own_group", "pick", "column0", "centre"]


def kernel(x, L0_conv_weights_real, L0_conv_weights_imag, L1_conv_coeff_real, L1_conv_coeff_imag, L1_conv_proj,
           L2_conv_W, L2_conv_b, L3_conv_weight):
    import concourse.bacc as bacc
    from concourse.bass_utils import run_bass_kernel_spmd

    x = np.ascontiguousarray(x)
    batch = x.shape[0]
    arrays = {
        "x": x,
        "w0r": L0_conv_weights_real, "w0i": L0_conv_weights_imag,
        "coeff_r": L1_conv_coeff_real, "coeff_i": L1_conv_coeff_imag,
        "proj_t": np.asarray(L1_conv_proj).T,
        "w3_t": np.asarray(L2_conv_W).transpose(1, 2, 3, 0),
        "bias3": np.asarray(L2_conv_b).reshape(C, 1),
        "w5_t": np.asarray(L3_conv_weight).transpose(1, 2, 3, 0),
    }
    tables = constants(batch)
    arrays.update({name: tables[name] for name in _TABLES})
    nc = bacc.Bacc("TRN2", target_bir_lowering=False, num_devices=1)
    ins, args = {}, []
    for name, a in arrays.items():
        a = np.ascontiguousarray(a)
        ins[f"{name}_in"] = a
        args.append(nc.dram_tensor(f"{name}_in", a.shape, mybir.dt.from_np(a.dtype), kind="ExternalInput").ap())
    y = nc.dram_tensor("y_out", x.shape, F32, kind="ExternalOutput").ap()
    four_convolutions(nc, batch, *args, y)
    r = run_bass_kernel_spmd(nc, [ins], core_ids=[0])
    return r.results[0]["y_out"]
```
